# Optimizing a Trainium2 kernel written in Bass

```python
import numpy as np
import jax
import jax.numpy as jnp

def _softmax(x, axis=-1):
    return jax.nn.softmax(x, axis=axis)

def _gelu(x):
    return jax.nn.gelu(x, approximate=True)

def _silu(x):
    return jax.nn.silu(x)

def _sigmoid(x):
    return jax.nn.sigmoid(x)

def _layernorm(x, axis=-1, eps=1e-05):
    m = jnp.mean(x, axis=axis, keepdims=True)
    v = jnp.var(x, axis=axis, keepdims=True)
    return (x - m) / jnp.sqrt(v + eps)

def _scatter_add(tgt, idx, src, axis=0):
    return tgt.at[idx].add(src)

def _segment_sum(src, seg, n):
    return jax.ops.segment_sum(src, seg, n)
kernel_name = 'mk_hybrid_d1_jaxref_r4_739cc8'

def setup_inputs(seed: int=0):
    np.random.seed(seed)
    _w = jnp.asarray

    def _L0_attn_a_setup():
        import jax, jax.numpy as jnp
        import numpy as np
        B, T, C, NF = (8, 512, 256, 64)
        EPS = 1e-06

        def mmnorm(x):
            return x / (jnp.max(jnp.abs(x), axis=-1, keepdims=True) + EPS)

        def _scanner(y, x, freq_W, freq_b, out_W, out_b):
            z = jnp.concatenate([y, x], axis=-1)
            f = z @ freq_W + freq_b
            z = jnp.concatenate([jnp.sin(f), jnp.cos(f)], -1) @ out_W + out_b
            return mmnorm(z)
        key = jax.random.key(seed)
        ks = jax.random.split(key, 8)

        def w(k, shape, fan_in):
            return jax.random.normal(k, shape, jnp.float32) * (1.0 / np.sqrt(fan_in))
        return {'x': jax.random.normal(ks[0], (B, T, C), jnp.float32), 'attn_W': w(ks[1], (C, 2 * C), C), 'attn_b': jnp.zeros((2 * C,), jnp.float32), 'freq_W': w(ks[2], (2 * C, NF), 2 * C), 'freq_b': jnp.zeros((NF,), jnp.float32), 'out_W': w(ks[3], (2 * NF, C), 2 * NF), 'out_b': jnp.zeros((C,), jnp.float32), 'proj_W': w(ks[4], (C, C), C), 'proj_b': jnp.zeros((C,), jnp.float32), 'identity': jax.random.uniform(ks[5], (C,), jnp.float32)}
    _L0_attn_a_in = _L0_attn_a_setup()

    def _L0_attn_b_setup():
        import jax, jax.numpy as jnp
        import numpy as np
        HID = 256
        HEADS = 16
        FEAT = 16
        HD = HID // HEADS
        EPS = 1e-05
        LN_EPS = 1e-05
        B, T = (1, 256)
        IU, JU = np.triu_indices(FEAT, 1)

        def _feature_map(x, gamma, beta):
            mu = x.mean(axis=-1, keepdims=True)
            var = ((x - mu) ** 2).mean(axis=-1, keepdims=True)
            xn = (x - mu) / jnp.sqrt(var + LN_EPS) * gamma + beta
            diag = xn * xn
            off = xn[..., IU] * xn[..., JU]
            return jnp.concatenate([diag * FEAT ** (-0.5), off * (2.0 / FEAT) ** 0.5], axis=-1)
        key = jax.random.key(seed)
        ks = jax.random.split(key, 5)
        s = 0.02
        return {'hidden_states': jax.random.normal(ks[0], (B, T, HID), dtype=jnp.float32), 'Wq': jax.random.normal(ks[1], (FEAT * HEADS, HID), dtype=jnp.float32) * s, 'Wk': jax.random.normal(ks[2], (FEAT * HEADS, HID), dtype=jnp.float32) * s, 'Wv': jax.random.normal(ks[3], (HEADS * HD, HID), dtype=jnp.float32) * s, 'Wo': jax.random.normal(ks[4], (HID, HEADS * HD), dtype=jnp.float32) * s, 'gamma': jnp.ones((FEAT,), dtype=jnp.float32), 'beta': jnp.zeros((FEAT,), dtype=jnp.float32)}
    _L0_attn_b_in = _L0_attn_b_setup()

    def _L0_ffn_setup():
        import jax, jax.numpy as jnp
        import numpy as np
        B, T, D = (2, 512, 256)
        DCD = 1024
        RET = 128
        NEXP = 1024
        NKEYS = 64
        H = 4
        KPH = 8
        key = jax.random.key(seed)
        ks = jax.random.split(key, 10)
        s = lambda k, shape, scale: jax.random.normal(k, shape, jnp.float32) * scale
        return {'hidden_states': jax.random.normal(ks[0], (B, T, D), jnp.float32), 'Wg': s(ks[1], (D, DCD), 0.02), 'bg': jnp.zeros((DCD,), jnp.float32), 'Wu': s(ks[2], (D, DCD), 0.02), 'bu': jnp.zeros((DCD,), jnp.float32), 'Wd': s(ks[3], (DCD, D), 0.02), 'bd': jnp.zeros((D,), jnp.float32), 'Wq': s(ks[4], (D, RET * H), 0.02), 'keys': s(ks[5], (H, NKEYS, 2, RET // 2), 0.02), 'down_embed': s(ks[6], (NEXP, D), 0.02), 'up_embed': s(ks[7], (NEXP, D), 0.02)}
    _L0_ffn_in = _L0_ffn_setup()
    _d = {'L0_attn_a_x': _L0_attn_a_in['x'], 'L0_attn_a_attn_W': _L0_attn_a_in['attn_W'], 'L0_attn_a_attn_b': _L0_attn_a_in['attn_b'], 'L0_attn_a_freq_W': _L0_attn_a_in['freq_W'], 'L0_attn_a_freq_b': _L0_attn_a_in['freq_b'], 'L0_attn_a_out_W': _L0_attn_a_in['out_W'], 'L0_attn_a_out_b': _L0_attn_a_in['out_b'], 'L0_attn_a_proj_W': _L0_attn_a_in['proj_W'], 'L0_attn_a_proj_b': _L0_attn_a_in['proj_b'], 'L0_attn_a_identity': _L0_attn_a_in['identity'], 'L0_attn_b_Wq': _L0_attn_b_in['Wq'], 'L0_attn_b_Wk': _L0_attn_b_in['Wk'], 'L0_attn_b_Wv': _L0_attn_b_in['Wv'], 'L0_attn_b_Wo': _L0_attn_b_in['Wo'], 'L0_attn_b_gamma': _L0_attn_b_in['gamma'], 'L0_attn_b_beta': _L0_attn_b_in['beta'], 'L0_ffn_Wg': _L0_ffn_in['Wg'], 'L0_ffn_bg': _L0_ffn_in['bg'], 'L0_ffn_Wu': _L0_ffn_in['Wu'], 'L0_ffn_bu': _L0_ffn_in['bu'], 'L0_ffn_Wd': _L0_ffn_in['Wd'], 'L0_ffn_bd': _L0_ffn_in['bd'], 'L0_ffn_Wq': _L0_ffn_in['Wq'], 'L0_ffn_keys': _L0_ffn_in['keys'], 'L0_ffn_down_embed': _L0_ffn_in['down_embed'], 'L0_ffn_up_embed': _L0_ffn_in['up_embed']}
    _x0 = _d['L0_attn_a_x']
    _d['L0_attn_a_x'] = jax.random.normal(jax.random.fold_in(jax.random.key(seed), 1), (8, 512, 256), dtype=_x0.dtype)
    del _x0
    return _d

def reference(L0_attn_a_x, L0_attn_a_attn_W, L0_attn_a_attn_b, L0_attn_a_freq_W, L0_attn_a_freq_b, L0_attn_a_out_W, L0_attn_a_out_b, L0_attn_a_proj_W, L0_attn_a_proj_b, L0_attn_a_identity, L0_attn_b_Wq, L0_attn_b_Wk, L0_attn_b_Wv, L0_attn_b_Wo, L0_attn_b_gamma, L0_attn_b_beta, L0_ffn_Wg, L0_ffn_bg, L0_ffn_Wu, L0_ffn_bu, L0_ffn_Wd, L0_ffn_bd, L0_ffn_Wq, L0_ffn_keys, L0_ffn_down_embed, L0_ffn_up_embed):

    def _L0_attn_a_ref(x, attn_W, attn_b, freq_W, freq_b, out_W, out_b, proj_W, proj_b, identity):
        import jax, jax.numpy as jnp
        import numpy as np
        B, T, C, NF = (8, 512, 256, 64)
        EPS = 1e-06

        def mmnorm(x):
            return x / (jnp.max(jnp.abs(x), axis=-1, keepdims=True) + EPS)

        def _scanner(y, x, freq_W, freq_b, out_W, out_b):
            z = jnp.concatenate([y, x], axis=-1)
            f = z @ freq_W + freq_b
            z = jnp.concatenate([jnp.sin(f), jnp.cos(f)], -1) @ out_W + out_b
            return mmnorm(z)
        b, t, c = x.shape
        qv = x @ attn_W + attn_b
        q, v = (qv[..., :c], qv[..., c:])
        n = 1
        while n < t:
            prev = jnp.concatenate([jnp.broadcast_to(identity, (b, n, c)), q[:, :t - n]], axis=1)
            q = _scanner(prev, q, freq_W, freq_b, out_W, out_b)
            n *= 2
        Y = q * v
        return Y @ proj_W + proj_b

    def _L0_attn_b_ref(hidden_states, Wq, Wk, Wv, Wo, gamma, beta):
        import jax, jax.numpy as jnp
        import numpy as np
        HID = 256
        HEADS = 16
        FEAT = 16
        HD = HID // HEADS
        EPS = 1e-05
        LN_EPS = 1e-05
        B, T = (1, 256)
        IU, JU = np.triu_indices(FEAT, 1)

        def _feature_map(x, gamma, beta):
            mu = x.mean(axis=-1, keepdims=True)
            var = ((x - mu) ** 2).mean(axis=-1, keepdims=True)
            xn = (x - mu) / jnp.sqrt(var + LN_EPS) * gamma + beta
            diag = xn * xn
            off = xn[..., IU] * xn[..., JU]
            return jnp.concatenate([diag * FEAT ** (-0.5), off * (2.0 / FEAT) ** 0.5], axis=-1)
        b, t, _ = hidden_states.shape
        q = (hidden_states @ Wq.T).reshape(b, t, HEADS, FEAT).transpose(0, 2, 1, 3)
        k = (hidden_states @ Wk.T).reshape(b, t, HEADS, FEAT).transpose(0, 2, 1, 3)
        v = (hidden_states @ Wv.T).reshape(b, t, HEADS, HD).transpose(0, 2, 1, 3)
        phi_q = _feature_map(q, gamma, beta)
        phi_k = _feature_map(k, gamma, beta)
        kv_cum = jnp.cumsum(phi_k[..., :, None] * v[..., None, :], axis=2)
        num = jnp.einsum('bhtf,bhtfd->bhtd', phi_q, kv_cum)
        den = jnp.einsum('bhtf,bhtf->bht', phi_q, jnp.cumsum(phi_k, axis=2))[..., None] + EPS
        y = (num / den).transpose(0, 2, 1, 3).reshape(b, t, HEADS * HD)
        return y @ Wo.T

    def _L0_ffn_ref(hidden_states, Wg, bg, Wu, bu, Wd, bd, Wq, keys, down_embed, up_embed):
        import jax, jax.numpy as jnp
        import numpy as np
        B, T, D = (2, 512, 256)
        DCD = 1024
        RET = 128
        NEXP = 1024
        NKEYS = 64
        H = 4
        KPH = 8
        b, t, d = hidden_states.shape
        q = (hidden_states @ Wq).reshape(b, t, 2, H, RET // 2)
        sim = jnp.einsum('btphn,hkpn->pbthk', q, keys)
        sc, ix = jax.lax.top_k(sim, KPH)
        sx, sy = (sc[0], sc[1])
        ixx, ixy = (ix[0], ix[1])
        all_sc = (sx[..., :, None] + sy[..., None, :]).reshape(b, t, H, KPH * KPH)
        all_ix = (ixx[..., :, None] * NKEYS + ixy[..., None, :]).reshape(b, t, H, KPH * KPH)
        scores, pk = jax.lax.top_k(all_sc, KPH)
        idx = jnp.take_along_axis(all_ix, pk, axis=-1)
        de = down_embed[idx]
        ue = up_embed[idx]
        w = jnp.einsum('btd,bthkd->bthk', hidden_states, de)
        w = jax.nn.silu(w) * jax.nn.softmax(scores, axis=-1)
        experts_states = jnp.einsum('bthk,bthkd->btd', w, ue)
        mlp = jax.nn.silu(hidden_states @ Wg + bg) * (hidden_states @ Wu + bu) @ Wd + bd
        return mlp + experts_states
    x = L0_attn_a_x
    x = x + _L0_attn_a_ref(_layernorm(x, axis=-1), L0_attn_a_attn_W, L0_attn_a_attn_b, L0_attn_a_freq_W, L0_attn_a_freq_b, L0_attn_a_out_W, L0_attn_a_out_b, L0_attn_a_proj_W, L0_attn_a_proj_b, L0_attn_a_identity)
    x = x + _L0_ffn_ref(_layernorm(x, axis=-1), L0_ffn_Wg, L0_ffn_bg, L0_ffn_Wu, L0_ffn_bu, L0_ffn_Wd, L0_ffn_bd, L0_ffn_Wq, L0_ffn_keys, L0_ffn_down_embed, L0_ffn_up_embed)
    x = x + _L0_attn_b_ref(_layernorm(x, axis=-1), L0_attn_b_Wq, L0_attn_b_Wk, L0_attn_b_Wv, L0_attn_b_Wo, L0_attn_b_gamma, L0_attn_b_beta)
    x = x + _L0_ffn_ref(_layernorm(x, axis=-1), L0_ffn_Wg, L0_ffn_bg, L0_ffn_Wu, L0_ffn_bu, L0_ffn_Wd, L0_ffn_bd, L0_ffn_Wq, L0_ffn_keys, L0_ffn_down_embed, L0_ffn_up_embed)
    return x

_drawn_inputs = setup_inputs


def setup_inputs(seed=0):
    import zlib

    import numpy as np

    out = dict(_drawn_inputs(seed))
    spreads = {'L0_attn_a_attn_b': (0.0, 0.1),
     'L0_attn_a_freq_b': (0.0, 0.1),
     'L0_attn_a_out_b': (0.0, 0.1),
     'L0_attn_a_proj_b': (0.0, 0.1),
     'L0_attn_b_gamma': (1.0, 0.6),
     'L0_attn_b_beta': (0.0, 0.8),
     'L0_ffn_bg': (0.0, 0.377),
     'L0_ffn_bu': (0.0, 0.374),
     'L0_ffn_bd': (0.0, 0.1)}
    factors = {'L0_attn_b_Wq': 4.85,
     'L0_attn_b_Wk': 4.751,
     'L0_attn_b_Wo': 2.706,
     'L0_ffn_Wq': 8.0,
     'L0_ffn_keys': 8.0,
     'L0_ffn_down_embed': 3.108,
     'L0_ffn_up_embed': 2.984}
    for name, (base, spread) in spreads.items():
        noise = np.random.default_rng([zlib.crc32(name.encode()), seed]).standard_normal(out[name].shape)
        drawn = base * np.exp(spread * noise) if base else spread * noise
        out[name] = jnp.asarray(drawn.astype(out[name].dtype))
    for name, factor in factors.items():
        out[name] = (out[name] * factor).astype(out[name].dtype)
    return out
```

```python
from contextlib import ExitStack
import math

import concourse.bass as bass
from concourse import mybir

F32 = mybir.dt.float32
F32R = mybir.dt.float32r
BF16 = mybir.dt.bfloat16
U32 = mybir.dt.uint32
ACT = mybir.ActivationFunctionType
ALU = mybir.AluOpType
AX = mybir.AxisListType

P = 128
B, T, C = 8, 512, 256
KC = C // P
TJ = T // P
NF = 64
SHIFTS = [1 << s for s in range(9)]
TURN = 2.0 * math.pi
SIN_SCALE = 6.2831850
MAGIC = 1.5 * 2.0 ** 23
DCD, NEXP, H, NKEYS, KPH = 1024, 1024, 4, 64, 8
FC = DCD // P
NHI = NEXP // NKEYS
ROWS = 96
HEADS, FEAT = 16, 16
LN_EPS = 1e-5

BIAS = {}
_at = 0
for _name, _n in (("v", C), ("gq", P), ("z", C), ("gz", P), ("proj", C), ("bd", C), ("f", P), ("id", P)):
    BIAS[_name] = (_at, _at + _n)
    _at += _n
NBIAS = _at

START = 1


class Named:
    pass


class ScanSignals:
    def __init__(self, sem, tag):
        self.all = [sem(f"{tag}_{n}") for n in (
            "stats_ready mv_ready var_eps rstd_ready xn_ready xT_psum xT_ready z_psum v_ready gs_ready "
            "f_psum whole_ready turns_ready wave_ready peak_ready peak_eps scale_ready y_ready y_psum "
            "proj_psum x_added "
        ).split()]
        (self.stats_ready, self.mv_ready, self.var_eps, self.rstd_ready, self.xn_ready, self.xT_psum,
         self.xT_ready, self.z_psum, self.v_ready, self.gs_ready, self.f_psum, self.whole_ready,
         self.turns_ready, self.wave_ready, self.peak_ready, self.peak_eps, self.scale_ready, self.y_ready,
         self.y_psum, self.proj_psum, self.x_added) = self.all


class FfnSignals:
    def __init__(self, sem, tag):
        self.all = [sem(f"{tag}_{n}") for n in (
            "stats_ready mv_ready var_eps rstd_ready xn_ready hT_psum hT_ready sim_psum sim_ready "
            "gu_psum gate_ready mid_ready w_psum reach_ready rank_step below_ready expo_ready "
            "total_ready ln_ready digits_ready turned_psum turned_ready ds_psum E_ready masked pool_sum "
            "mix_ready mix_used over_psum x_added mix_step top_ready hot_ready hot_weighted second_ready rest_ready mid_used over_ready "
        ).split()]
        (self.stats_ready, self.mv_ready, self.var_eps, self.rstd_ready, self.xn_ready, self.hT_psum,
         self.hT_ready, self.sim_psum, self.sim_ready, self.gu_psum, self.gate_ready, self.mid_ready,
         self.w_psum, self.reach_ready, self.rank_step, self.below_ready, self.expo_ready, self.total_ready,
         self.ln_ready, self.digits_ready, self.turned_psum, self.turned_ready, self.ds_psum, self.E_ready,
         self.masked, self.pool_sum, self.mix_ready, self.mix_used, self.over_psum, self.x_added,
         self.mix_step, self.top_ready, self.hot_ready, self.hot_weighted,
         self.second_ready, self.rest_ready, self.mid_used, self.over_ready) = self.all


class AttnSignals:
    def __init__(self, sem, tag):
        self.all = [sem(f"{tag}_{n}") for n in (
            "stats_ready mv_ready var_eps rstd_ready xn_ready hT_psum hT_ready qkv_psum qk_ready "
            "v_ready feat_step squared var_ready rms_step rms_ready qk_normal hi_ready lo_ready "
            "turned_psum turned_ready score_psum U_ready U_masked y_psum den_step y_ready yT_psum "
            "proj_psum x_added "
        ).split()]
        (self.stats_ready, self.mv_ready, self.var_eps, self.rstd_ready, self.xn_ready, self.hT_psum,
         self.hT_ready, self.qkv_psum, self.qk_ready, self.v_ready, self.feat_step, self.squared,
         self.var_ready, self.rms_step, self.rms_ready, self.qk_normal, self.hi_ready, self.lo_ready,
         self.turned_psum, self.turned_ready, self.score_psum, self.U_ready, self.U_masked, self.y_psum,
         self.den_step, self.y_ready, self.yT_psum, self.proj_psum, self.x_added) = self.all



def spread(ap, axis, n):
    out = ap.unsqueeze(axis)
    shape = list(out.shape)
    shape[axis] = n
    return out.to_broadcast(shape)


def setup(nc, w, io, sem):
    with ExitStack() as ctx:
        def tmp(name, shape, dt=F32):
            return ctx.enter_context(nc.sbuf_tensor(name, shape, dt))

        bank = [ctx.enter_context(nc.psum_tensor(f"setup_bank{i}", [P, 512], F32)) for i in range(4)]
        loaded = sem("loaded")
        ident_ready = sem("ident_ready")
        steps = sem("pool_steps")
        job_done, job_out = sem("job_done"), sem("job_out")
        bias_made, bias_moved = sem("bias_made"), sem("bias_moved")

        sel0, selovf0 = tmp("sel0", [ROWS, FC, 2, NKEYS]), tmp("selovf0", [ROWS, P])
        outw = tmp("outw", [P, C])
        freqw = tmp("freqw", [P, 4, NF])
        attnw = tmp("attnw", [P, KC, 2 * C])
        outwT = tmp("outwT", [P, KC, P])
        attnqT = tmp("attnqT", [P, KC, C])
        bq_col, bo_col, id_col = tmp("bq_col", [P, KC]), tmp("bo_col", [P, KC]), tmp("id_col", [P, KC])
        ffq = tmp("ffq", [P, KC, H, 2, NKEYS])
        ffqT = tmp("ffqT", [P, H, C])
        keys = tmp("keys_rows", [P, 2, P])
        keysT = tmp("keysT", [P, 2, P])
        de = tmp("de_rows", [P, FC, C])
        wrow = tmp("wrow", [P, 4, 2, C])
        brow = tmp("brow", [1, NBIAS])
        rest = tmp("rest", [1, NBIAS])
        parts = tmp("parts", [1, 3, NBIAS], BF16)
        fq_row = tmp("fq_row", [1, NF])

        loads = [
            (outw[:], io.out_W), (freqw[:], io.freq_W.rearrange("(k p) n -> p k n", p=P)),
            (attnw[:], io.attn_W.rearrange("(k p) n -> p k n", p=P)),
            (bq_col[:], io.attn_b[0:C].rearrange("(k p) -> p k", p=P)),
            (bo_col[:], io.out_b.rearrange("(k p) -> p k", p=P)),
            (id_col[:], io.identity.rearrange("(k p) -> p k", p=P)),
            (brow[0:1, BIAS["v"][0]:BIAS["v"][1]], io.attn_b[C:2 * C].unsqueeze(0)),
            (brow[0:1, BIAS["z"][0]:BIAS["z"][1]], io.out_b.unsqueeze(0)),
            (brow[0:1, BIAS["proj"][0]:BIAS["proj"][1]], io.proj_b.unsqueeze(0)),
            (brow[0:1, BIAS["bd"][0]:BIAS["bd"][1]], io.bd.unsqueeze(0)),
            (fq_row[:], io.freq_b.unsqueeze(0)),
            (w.wz[:], io.out_W), (w.wproj[:], io.proj_W.rearrange("(k p) n -> p k n", p=P)),
            (w.wv[:], io.attn_W[:, C:2 * C].rearrange("(k p) n -> p k n", p=P)),
            (keys[:], io.keys.rearrange("(a b) k q n -> (b k) a (q n)", a=2)),
            (de[:], io.down_embed.rearrange("(e p) c -> p e c", p=P)),
            (w.ue[:], io.up_embed.rearrange("(e p) c -> p e c", p=P)),
            (w.wg[:], io.Wg.rearrange("(k p) n -> p k n", p=P)),
            (w.wu[:], io.Wu.rearrange("(k p) n -> p k n", p=P)),
            (w.wd[:], io.Wd.rearrange("(f p) n -> p f n", p=P)),
            (w.bg[:], io.bg.rearrange("(f p) -> p f", p=P)),
            (w.bu[:], io.bu.rearrange("(f p) -> p f", p=P)),
            (w.gamma[:], io.gamma.partition_broadcast(P)),
            (w.beta[:], io.beta.partition_broadcast(P)),
        ]
        for k in range(KC):
            for q in range(2):
                loads.append((ffq[:, k, :, q, :], io.ffn_Wq[k * P:(k + 1) * P, q * C:(q + 1) * C]
                              .rearrange("p (h n) -> p h n", h=H)))
        for m, src in enumerate((io.b_Wq, io.b_Wk, io.b_Wv, io.b_Wo)):
            loads.append((wrow[:, m], src.rearrange("(r p) c -> p r c", p=P)))

        jobs = []

        def turned(src, dst):
            jobs.append(([(src, None)], P, dst, 1.0))

        for k in range(KC):
            turned(outw[:, k * P:(k + 1) * P], outwT[:, k, :])
            for r in range(KC):
                turned(attnw[:, r, k * P:(k + 1) * P], attnqT[:, k, r * P:(r + 1) * P])
            for h in range(H):
                turned(ffq[:, k, h].rearrange("p q n -> p (q n)"), ffqT[:, h, k * P:(k + 1) * P])
            turned(keys[:, k, :], keysT[:, k, :])
            for e in range(FC):
                turned(de[:, e, k * P:(k + 1) * P], w.deT[:, k, e * P:(e + 1) * P])
            for r in range(2):
                turned(wrow[:, 0, r, k * P:(k + 1) * P], w.wqk[:, k, r * P:(r + 1) * P])
                turned(wrow[:, 1, r, k * P:(k + 1) * P], w.wqk[:, k, C + r * P:C + (r + 1) * P])
                turned(wrow[:, 2, r, k * P:(k + 1) * P], w.wvb[:, k, r * P:(r + 1) * P])
                turned(wrow[:, 3, r, k * P:(k + 1) * P], w.wo[:, k, r * P:(r + 1) * P])
        for half in range(2):
            fw = [freqw[:, 2 * half + k, :] for k in range(KC)]
            cols = slice(half * NF, (half + 1) * NF)
            jobs.append(([(outwT[:, k, :], fw[k]) for k in range(KC)], P, w.gz[:, cols], 1.0 / TURN))
            for r in range(KC):
                jobs.append(([(attnqT[:, k, r * P:(r + 1) * P], fw[k]) for k in range(KC)],
                             P, w.gq[:, r, cols], 1.0 / TURN))
            for name, col in (("gz", bo_col), ("gq", bq_col)):
                at = BIAS[name][0] + half * NF
                jobs.append(([(col[:, k:k + 1], fw[k]) for k in range(KC)], 1, brow[0:1, at:at + NF], 1.0 / TURN))
            if half == 0:
                for d in range(2):
                    at = BIAS["id"][0] + d * NF
                    jobs.append(([(id_col[:, k:k + 1], fw[k]) for k in range(KC)], 1,
                                 brow[0:1, at:at + NF], 1.0 / TURN))
        for q in range(2):
            for h in range(H):
                rows = slice(q * NKEYS, (q + 1) * NKEYS)
                for k in range(KC):
                    jobs.append(([(ffqT[rows, h, k * P:(k + 1) * P],
                                   keysT[rows, h // 2, (h % 2) * NKEYS:(h % 2 + 1) * NKEYS])],
                                 P, w.wsim[:, k, (q * H + h) * NKEYS:(q * H + h + 1) * NKEYS], 1.0))

        with nc.Block() as block:
            @block.sync
            def _(sp):
                for dst, src in loads:
                    sp.dma_start(dst, src, allow_slow_non_contiguous=True).then_inc(loaded, 16)
                for b in range(B):
                    sp.dma_start(w.x[:, b * TJ:(b + 1) * TJ, :],
                                 io.x[b].rearrange("(j p) c -> p j c", p=P)).then_inc(w.x_loaded[b], 16)
                for signal in w.all_signals:
                    sp.sem_inc(signal, START)
                sp.wait_ge(bias_made, 1)
                sp.dma_start(w.bias3[:], parts[:]).then_inc(bias_moved, 16)
                sp.wait_ge(bias_moved, 16)

            @block.gpsimd
            def _(pool):
                pool.memset(w.ident[:], 0.0).then_inc(steps, 1)
                pool.memset(w.tri[:], 1.0).then_inc(steps, 1)
                pool.memset(w.ones3[:], 1.0)
                pool.memset(w.ones3b[:], 1.0)
                pool.memset(w.minus_half[:], -0.5)
                pool.memset(w.eps[:], LN_EPS)
                pool.memset(sel0[:], 0.0).then_inc(steps, 1)
                pool.memset(selovf0[:], 0.0).then_inc(steps, 1)
                pool.iota(w.iota_lo[:], pattern=[[1, NKEYS], [0, KPH]], base=0, channel_multiplier=0,
                          allow_small_or_imprecise_dtypes=True)
                pool.iota(w.rank_weight[:], pattern=[[0, NKEYS], [-1, KPH]], base=KPH, channel_multiplier=0,
                          allow_small_or_imprecise_dtypes=True)
                pool.wait_ge(steps, 1)
                pool.affine_select(out=w.ident[:], in_=w.ident[:], compare_op=ALU.not_equal, fill=1.0, base=0,
                                   pattern=[[-1, P]], channel_multiplier=1).then_inc(ident_ready, 1)
                pool.wait_ge(ident_ready, 1)
                pool.tensor_copy(w.identb[:], w.ident[:])
                pool.wait_ge(steps, 2)
                pool.affine_select(out=w.tri[:], in_=w.tri[:], compare_op=ALU.is_ge, fill=0.0, base=0,
                                   pattern=[[1, P]], channel_multiplier=-1)
                pool.wait_ge(steps, 4)
                pool.affine_select(out=sel0[:], in_=sel0[:], compare_op=ALU.not_equal, fill=1.0,
                                   base=0, pattern=[[-2, FC], [-1, 2], [0, NKEYS]],
                                   channel_multiplier=1).then_inc(steps, 1)
                pool.wait_ge(steps, 5)
                pool.affine_select(out=sel0[:], in_=sel0[:], compare_op=ALU.not_equal, fill=1.0,
                                   base=-NHI, pattern=[[0, FC], [0, 2], [-1, NKEYS]],
                                   channel_multiplier=1).then_inc(steps, 1)
                pool.affine_select(out=selovf0[:, P - 1:P], in_=selovf0[:, P - 1:P], compare_op=ALU.not_equal,
                                   fill=1.0, base=-(NHI + NKEYS), pattern=[[0, 1]], channel_multiplier=1
                                   ).then_inc(steps, 1)

            @block.tensor
            def _(pe):
                pe.wait_ge(loaded, 16 * len(loads))
                pe.wait_ge(ident_ready, 1)
                for n, (products, m, dst, scale) in enumerate(jobs):
                    if n >= 4:
                        pe.wait_ge(job_out, n - 3)
                    width = products[0][1].shape[-1] if products[0][1] is not None else P
                    out = bank[n % 4][0:m, 0:width]
                    if products[0][1] is None:
                        pe.transpose(out, products[0][0], w.ident[:]).then_inc(job_done, 1)
                        turned_last = n
                        continue
                    if n == turned_last + 1:
                        pe.wait_ge(job_out, n)
                    for k, (lhsT, rhs) in enumerate(products):
                        mm = pe.matmul(out, lhsT, rhs, start=(k == 0), stop=(k == len(products) - 1))
                    mm.then_inc(job_done, 1)

            @block.vector
            def _(dve):
                for n, (products, m, dst, scale) in enumerate(jobs):
                    width = products[0][1].shape[-1] if products[0][1] is not None else P
                    dve.wait_ge(job_done, n + 1)
                    src = bank[n % 4][0:m, 0:width]
                    if scale == 1.0:
                        dve.tensor_copy(dst, src).then_inc(job_out, 1)
                    else:
                        dve.tensor_scalar(dst, src, scale, None, ALU.mult).then_inc(job_out, 1)
                dve.wait_ge(steps, 7)
                dve.tensor_copy(w.sel[:], sel0[:])
                dve.tensor_copy(w.selb[:], sel0[:])
                dve.tensor_copy(w.selovf[:], selovf0[:])
                chain = sem("bias_chain")
                f0 = BIAS["f"][0]
                dve.wait_ge(loaded, 16 * len(loads))
                dve.wait_ge(job_out, len(jobs))
                dve.tensor_scalar(brow[0:1, f0:f0 + NF], fq_row[:], 1.0 / TURN, None, ALU.mult).then_inc(chain, 1)
                dve.tensor_scalar(brow[0:1, f0 + NF:f0 + 2 * NF], fq_row[:], 1.0 / TURN, 0.25,
                                  ALU.mult, ALU.add).then_inc(chain, 1)
                dve.wait_ge(chain, 2)
                dve.tensor_copy(parts[0:1, 0, :], brow[:]).then_inc(chain, 1)
                dve.wait_ge(chain, 3)
                dve.tensor_tensor(rest[:], brow[:], parts[0:1, 0, :], ALU.subtract).then_inc(chain, 1)
                dve.wait_ge(chain, 4)
                dve.tensor_copy(parts[0:1, 1, :], rest[:]).then_inc(chain, 1)
                dve.wait_ge(chain, 5)
                dve.tensor_tensor(brow[:], rest[:], parts[0:1, 1, :], ALU.subtract).then_inc(chain, 1)
                dve.wait_ge(chain, 6)
                dve.tensor_copy(parts[0:1, 2, :], brow[:]).then_inc(bias_made, 1)


def bias(w, name, times=1):
    a, b = BIAS[name]
    return spread(w.bias3[:, a:b], 1, times) if times > 1 else w.bias3[:, a:b]


def scan_attention(nc, w, sem):
    with ExitStack() as ctx:
        def tmp(name, shape, dt=F32):
            return [ctx.enter_context(nc.sbuf_tensor(f"{name}{lane}", shape, dt)) for lane in range(2)]

        def psum(name, n):
            return [ctx.enter_context(nc.psum_tensor(f"{name}{lane}", [P, n], F32)) for lane in range(2)]

        zb, gb, fb = psum("zb", 4 * C), psum("gb", 4 * P), psum("fb", T)
        stats, mv, rstd = tmp("a_stats", [P, TJ, 6]), tmp("a_mv", [P, TJ, 2]), tmp("a_rstd", [P, TJ])
        xn = tmp("a_xn", [P, TJ, C])
        xT = tmp("a_xT", [P, KC, T])
        v = tmp("a_v", [P, TJ, C])
        gs = tmp("a_gs", [P, 2 * TJ, 2, NF])
        whole, turns, wave = tmp("a_whole", [P, T]), tmp("a_turns", [P, T]), tmp("a_wave", [P, T])
        pause = tmp("a_pause", [P, 1])
        peak, scale = tmp("a_peak", [P, TJ]), tmp("a_scale", [P, TJ])

        S = w.scan_signals
        NS = len(SHIFTS)
        ROUNDS = B // 2

        def twice(g):
            return spread(g[:].rearrange("p (q n) -> p q n", n=NF), 2, 2)

        def nth(i, per_lane, k, lane):
            return i * (2 * per_lane) + 2 * k + lane + 1

        with nc.Block() as block:
            @block.vector
            def _(dve):
                for b in range(B):
                    dve.wait_ge(w.x_loaded[b], 16)
                with dve.Fori(0, ROUNDS) as i:
                    for l in range(2):
                        for j in range(TJ):
                            dve.bn_stats(stats[l][:, j, :], w.x[:, bass.ds(i * 2 * TJ + l * TJ + j, 1), :]
                                         ).then_inc(S.stats_ready, 1)
                        dve.wait_ge(S.stats_ready, i * (2 * TJ) + (l + 1) * TJ + START)
                        dve.memset(pause[l][:], 0.0)
                        for j in range(TJ):
                            dve.bn_aggr(mv[l][:, j, :], stats[l][:, j, :]).then_inc(S.mv_ready, 1)
                    for l in range(2):
                        dve.wait_ge(S.rstd_ready, nth(i, 1, 0, l) + START)
                        for j in range(TJ):
                            dve.tensor_scalar(xn[l][:, j, :], w.x[:, bass.ds(i * 2 * TJ + l * TJ + j, 1), :],
                                              mv[l][:, j, 0:1], rstd[l][:, j:j + 1],
                                              ALU.subtract, ALU.mult).then_inc(S.xn_ready, 1)
                    for l in range(2):
                        dve.wait_ge(S.z_psum, nth(i, NS + 1, 0, l) + START)
                        dve.tensor_copy(gs[l][:], twice(gb[l])).then_inc(S.gs_ready, 1)
                    for s in range(NS):
                        for l in range(2):
                            dve.wait_ge(S.whole_ready, nth(i, NS, s, l) + START)
                            dve.scalar_tensor_tensor(out=turns[l][:], in0=whole[l][:], scalar=MAGIC, in1=fb[l][:],
                                                     op0=ALU.subtract, op1=ALU.subtract).then_inc(S.turns_ready, 1)
                        for l in range(2):
                            dve.wait_ge(S.z_psum, nth(i, NS + 1, s + 1, l) + START)
                            dve.tensor_reduce(peak[l][:], zb[l][:].rearrange("p (j c) -> p j c", c=C), AX.X, ALU.max,
                                              apply_absolute_value=True).then_inc(S.peak_ready, 1)
                            dve.wait_ge(S.peak_ready, nth(i, NS, s, l) + START)
                            dve.tensor_scalar(peak[l][:], peak[l][:], 1e-6, None, ALU.add).then_inc(S.peak_eps, 1)
                            dve.wait_ge(S.peak_eps, nth(i, NS, s, l) + START)
                            dve.reciprocal(scale[l][:], peak[l][:]).then_inc(S.scale_ready, 1)
                            dve.wait_ge(S.scale_ready, nth(i, NS, s, l) + START)
                            if s < NS - 1:
                                for j in range(TJ):
                                    g = dve.tensor_scalar(gs[l][:, 2 * j:2 * j + 2], twice(gb[l])[:, 2 * j:2 * j + 2],
                                                          scale[l][:, j:j + 1], None, ALU.mult)
                                g.then_inc(S.gs_ready, 1)
                            else:
                                dve.wait_ge(S.v_ready, nth(i, 1, 0, l) + START)
                                for j in range(TJ):
                                    dve.scalar_tensor_tensor(out=xn[l][:, j, :], in0=zb[l][:, j * C:(j + 1) * C],
                                                             scalar=scale[l][:, j:j + 1], in1=v[l][:, j, :],
                                                             op0=ALU.mult, op1=ALU.mult).then_inc(S.y_ready, 1)
                    for l in range(2):
                        dve.wait_ge(S.proj_psum, nth(i, 1, 0, l) + START)
                        xs = w.x[:, bass.ds((i * 2 + l) * TJ, TJ), :].rearrange("p j c -> p (j c)")
                        dve.tensor_tensor(xs, zb[l][:], xs, ALU.add).then_inc(S.x_added, 1)

            @block.gpsimd
            def _(pool):
                with pool.Fori(0, ROUNDS) as i:
                    for l in range(2):
                        pool.wait_ge(S.mv_ready, i * (2 * TJ) + (l + 1) * TJ + START)
                        pool.wait_ge(S.xn_ready, i * (2 * TJ) + START)
                        pool.tensor_tensor(rstd[l][:], mv[l][:, :, 1], w.eps[:, 0:TJ], ALU.add).then_inc(S.var_eps, 1)
                        pool.wait_ge(S.var_eps, nth(i, 1, 0, l) + START)
                        pool.tensor_tensor(rstd[l][:], rstd[l][:], w.minus_half[:, 0:TJ], ALU.pow
                                           ).then_inc(S.rstd_ready, 1)

            @block.tensor
            def _(pe):
                def turn_to(l, src, out):
                    for k in range(KC):
                        for j in range(TJ):
                            mm = pe.transpose(out[:, k * T + j * P:k * T + (j + 1) * P],
                                              src[:, j, k * P:(k + 1) * P], w.ident[:])
                    return mm

                def tokens(l, lhsT, rz, rg, bz, bg):
                    for n in range(2):
                        pe.matmul(zb[l][:, n * T:(n + 1) * T], w.ones3[:], bias(w, bz, 2), start=True, stop=True)
                    if rg is not None:
                        pe.matmul(gb[l][:], w.ones3[:], bias(w, bg, TJ), start=True, stop=True)
                    for j in range(TJ):
                        for k, a in enumerate(lhsT):
                            last = k == len(lhsT) - 1
                            mm = pe.matmul(zb[l][:, j * C:(j + 1) * C], a[:, j * P:(j + 1) * P], rz[k],
                                           start=False, stop=last, skip_group_check=True)
                            if rg is not None:
                                mm = pe.matmul(gb[l][:, j * P:(j + 1) * P], a[:, j * P:(j + 1) * P], rg[k],
                                               start=False, stop=last, skip_group_check=True)
                    return mm

                with pe.Fori(0, ROUNDS) as i:
                    for l in range(2):
                        pe.wait_ge(S.xn_ready, i * (2 * TJ) + (l + 1) * TJ + START)
                        pe.wait_ge(S.x_added, i * 2 + START)
                        turn_to(l, xn[l], zb[l]).then_inc(S.xT_psum, 1)
                    for l in range(2):
                        pe.wait_ge(S.xT_ready, nth(i, 2, 0, l) + START)
                        tokens(l, [xT[l][:, k, :] for k in range(KC)], [w.wv[:, k, :] for k in range(KC)],
                               [w.gq[:, k, :] for k in range(KC)], "v", "gq").then_inc(S.z_psum, 1)
                    for s, n in enumerate(SHIFTS):
                        for l in range(2):
                            pe.wait_ge(S.gs_ready, nth(i, NS, s, l) + START)
                            pe.matmul(fb[l][:], bias(w, "f"), w.ones3b[:], start=True, stop=True)
                            pe.matmul(fb[l][:, 0:n], bias(w, "id"), w.ones3b[:, 0:n], start=False, stop=False,
                                      skip_group_check=True)
                            for j in range(TJ):
                                width = min(P, T - j * P - n)
                                if width > 0:
                                    prev = gs[l][:, 2 * j].rearrange("p d n -> p (d n)")
                                    pe.matmul(fb[l][:, j * P + n:j * P + n + width], prev, w.ident[:, 0:width],
                                              start=False, stop=False, skip_group_check=True)
                            for j in range(TJ):
                                own = gs[l][:, 2 * j + 1].rearrange("p d n -> p (d n)")
                                mm = pe.matmul(fb[l][:, j * P:(j + 1) * P], own, w.ident[:],
                                               start=False, stop=True, skip_group_check=True)
                            mm.then_inc(S.f_psum, 1)
                        for l in range(2):
                            pe.wait_ge(S.wave_ready, nth(i, NS, s, l) + START)
                            if s == 0:
                                pe.wait_ge(S.v_ready, nth(i, 1, 0, l) + START)
                            more = s < NS - 1
                            tokens(l, [wave[l]], [w.wz[:]], [w.gz[:]] if more else None,
                                   "z", "gz").then_inc(S.z_psum, 1)
                    for l in range(2):
                        pe.wait_ge(S.y_ready, i * (2 * TJ) + (l + 1) * TJ + START)
                        turn_to(l, xn[l], zb[l]).then_inc(S.y_psum, 1)
                    for l in range(2):
                        pe.wait_ge(S.xT_ready, nth(i, 2, 1, l) + START)
                        tokens(l, [xT[l][:, k, :] for k in range(KC)], [w.wproj[:, k, :] for k in range(KC)],
                               None, "proj", None).then_inc(S.proj_psum, 1)

            @block.scalar
            def _(act):
                with act.Fori(0, ROUNDS) as i:
                    for l in range(2):
                        act.wait_ge(S.xT_psum, nth(i, 1, 0, l) + START)
                        act.activation(xT[l][:].rearrange("p k t -> p (k t)"), zb[l][:], ACT.Copy).then_inc(S.xT_ready, 1)
                    for l in range(2):
                        act.wait_ge(S.z_psum, nth(i, NS + 1, 0, l) + START)
                        act.activation(v[l][:].rearrange("p j c -> p (j c)"), zb[l][:], ACT.Copy).then_inc(S.v_ready, 1)
                    for s in range(NS):
                        for l in range(2):
                            act.wait_ge(S.f_psum, nth(i, NS, s, l) + START)
                            act.activation(whole[l][:], fb[l][:], ACT.Copy, bias=MAGIC).then_inc(S.whole_ready, 1)
                        for l in range(2):
                            act.wait_ge(S.turns_ready, nth(i, NS, s, l) + START)
                            act.activation(wave[l][:], turns[l][:], ACT.Sin, scale=-SIN_SCALE).then_inc(S.wave_ready, 1)
                    for l in range(2):
                        act.wait_ge(S.y_psum, nth(i, 1, 0, l) + START)
                        act.activation(xT[l][:].rearrange("p k t -> p (k t)"), zb[l][:], ACT.Copy).then_inc(S.xT_ready, 1)


def experts_ffn(nc, w, sem, tag):
    with ExitStack() as ctx:
        def tmp(name, shape, dt=F32):
            return ctx.enter_context(nc.sbuf_tensor(f"{tag}_{name}", shape, dt))

        def psum(name, n):
            return ctx.enter_context(nc.psum_tensor(f"{tag}_{name}", [P, n], F32))

        G = TJ * H
        R = NHI + NKEYS

        bk01, bk2, bk3, bk4, bk5, acc = (
            psum("bk01", 1024), psum("bk2", 512), psum("bk3", 512), psum("bk4", 512), psum("bk5", 512),
            psum("acc", TJ * C))
        bk = [bk01[:, 0:512], bk01[:, 512:1024], bk2[:], bk3[:], bk4[:], bk5[:]]
        rank_bank, score_bank = [bk[2], bk[3], bk[0]], [bk[4], bk[5], bk[1]]

        stats, mv, rstd = tmp("stats", [P, TJ, 6]), tmp("mv", [P, TJ, 2]), tmp("rstd", [P, TJ])
        xn = tmp("xn", [P, TJ, C])
        hot_x = xn[:].rearrange("p j c -> p (j c)").bitcast(BF16).rearrange("p (g r i) -> p g r i", g=G, i=KPH)
        hT = tmp("hT", [P, KC, T])
        sim_row = tmp("sim", [P, TJ * 512])
        sim = sim_row[:].rearrange("p (t q h k) -> p t q h k", q=2, h=H, k=NKEYS)
        top, idx, idxb = tmp("top", [P, 2, G, KPH]), tmp("idx", [P, 2, G, KPH], U32), tmp("idxb", [P, 2, G, KPH], BF16)
        pair, best = tmp("pair", [P, G, KPH, KPH]), tmp("best", [P, G, KPH])
        picked = tmp("picked", [P, G, KPH, KPH])
        hot_y = [x[:].rearrange("p g i j -> p (g i j)").bitcast(BF16).rearrange("p (h k j) -> p h k j", h=H, j=KPH)
                 for x in (picked, pair)]
        count, countb = tmp("count", [P, G, KPH]), tmp("countb", [P, G, KPH], BF16)
        below, expo = tmp("below", [P, 2, G, KPH]), tmp("expo", [P, 2, G, KPH])
        row_sum, beyond = tmp("row_sum", [P, G, KPH]), tmp("beyond", [P, G, KPH])
        total, ln_total, inv_total, offset, over = (tmp(n, [P, G]) for n in (
            "total", "ln_total", "inv_total", "offset", "over"))
        idle = tmp("idle", [P, 1])
        pause = tmp("pause", [P, 16])
        digits = tmp("digits", [P, TJ, H, ROWS], BF16)
        scores = tmp("scores", [P, TJ, H, ROWS])
        digitsT = tmp("digitsT", [ROWS, H, T], BF16)
        scoreT = tmp("scoreT", [ROWS, 2, H, T], F32R)
        gate = tmp("gate", [P, 2, T])
        mid = tmp("mid", [P, 4, T])
        mixed, over_row = [mid[:, 0, :], mid[:, 1, :]], mid[:, 3, :]
        reach = tmp("reach", [P, FC, T])
        E = tmp("E", [P, 2, H, T])

        S = w.ffn_signals[tag]
        ROUNDS = B
        RANK_STEPS = 24
        POOL_SUMS = 2 * FC + 1

        with nc.Block() as block:
            @block.vector
            def _(dve):
                dve.memset(digits[:], 0.0)
                dve.memset(scores[:], 0.0)
                with dve.Fori(0, ROUNDS) as i:
                    steps, pauses = [0], [0]

                    def carry_wait():
                        dve.memset(pause[:, pauses[0]:pauses[0] + 1], 0.0)
                        pauses[0] += 1

                    def link(ins):
                        steps[0] += 1
                        ins.then_inc(S.rank_step, 1)

                    def settle(carry=False):
                        dve.wait_ge(S.rank_step, i * RANK_STEPS + steps[0] + START)
                        if carry:
                            carry_wait()

                    def times_up(f):
                        dve.wait_ge(S.gate_ready, i * FC + f + 1 + START)
                        dve.wait_ge(S.mid_used, i * FC + max(f - 3, 0) + START)
                        up = bk[5] if f % 2 == 0 else bk[1]
                        dve.scalar_tensor_tensor(out=mid[:, f % 4, :], in0=up, scalar=w.bu[:, f:f + 1],
                                                 in1=gate[:, f % 2, :], op0=ALU.add, op1=ALU.mult
                                                 ).then_inc(S.mid_ready, 1)

                    def rank_lo(t):
                        dve.wait_ge(S.hot_weighted, i * TJ + t + 1 + START)
                        with nc.allow_low_precision(reason="whole numbers up to 8, exact in bf16"):
                            dve.tensor_reduce(digits[:, t, :, NHI:R], hot_y[t % 2], AX.X, ALU.add
                                              ).then_inc(S.digits_ready, 1)

                    for j in range(TJ):
                        dve.bn_stats(stats[:, j, :], w.x[:, bass.ds(i * TJ + j, 1), :]).then_inc(S.stats_ready, 1)
                    dve.wait_ge(S.stats_ready, i * TJ + TJ + START)
                    carry_wait()
                    for j in range(TJ):
                        dve.bn_aggr(mv[:, j, :], stats[:, j, :]).then_inc(S.mv_ready, 1)
                    dve.wait_ge(S.rstd_ready, i + 1 + START)
                    for j in range(TJ):
                        dve.tensor_scalar(xn[:, j, :], w.x[:, bass.ds(i * TJ + j, 1), :], mv[:, j, 0:1],
                                          rstd[:, j:j + 1], ALU.subtract, ALU.mult).then_inc(S.xn_ready, 1)
                    dve.wait_ge(S.hT_psum, i + 1 + START)
                    dve.wait_ge(S.w_psum, i * FC + START)
                    dve.tensor_copy(hT[:].rearrange("p k t -> p (k t)"), bk01[:]).then_inc(S.hT_ready, 1)
                    for t in range(TJ):
                        of_tile = slice(t * H, (t + 1) * H)
                        dve.wait_ge(S.sim_ready, i * TJ + t + 1 + START)
                        carry_wait()
                        for q in range(2):
                            for h in range(H):
                                m = dve.max(top[:, q, t * H + h, :], sim[:, t, q, h, :])
                        link(m)
                        settle(carry=True)
                        for q in range(2):
                            for h in range(H):
                                m = dve.max_index(idx[:, q, t * H + h, :], top[:, q, t * H + h, :], sim[:, t, q, h, :])
                        m.then_inc(S.top_ready, 1)
                        if t >= 2:
                            times_up(t - 2)
                        dve.wait_ge(S.top_ready, i * TJ + t + 1 + START)
                        link(dve.tensor_copy(idxb[:, :, of_tile, :], idx[:, :, of_tile, :]))
                        settle()
                        if t >= 2:
                            dve.wait_ge(S.digits_ready, i * 6 + t - 1 + START)
                        dve.tensor_tensor(hot_y[t % 2], spread(w.iota_lo[:], 1, H),
                                          spread(idxb[:, 1, of_tile], 2, NKEYS), ALU.is_equal).then_inc(S.hot_ready, 1)
                        if t >= 1:
                            rank_lo(t - 1)
                    dve.tensor_tensor(below[:], top[:], top[:, :, :, 0:1].to_broadcast([P, 2, G, KPH]),
                                      ALU.subtract).then_inc(S.below_ready, 1)
                    link(dve.tensor_tensor(hot_x, spread(w.iota_lo[:, 0:NHI, :], 1, G), spread(idxb[:, 0], 2, NHI),
                                           ALU.is_equal))
                    rank_lo(TJ - 1)
                    dve.wait_ge(S.digits_ready, i * 6 + TJ + START)
                    link(dve.tensor_tensor(pair[:], spread(top[:, 0], 3, KPH), spread(top[:, 1], 2, KPH), ALU.add))
                    times_up(2)
                    settle(carry=True)
                    flat = pair[:].rearrange("p g i j -> p g (i j)")
                    marked = picked[:].rearrange("p g i j -> p g (i j)")
                    for g in range(G):
                        m = dve.max(best[:, g, :], flat[:, g, :])
                    link(m)
                    times_up(3)
                    settle(carry=True)
                    for g in range(G):
                        m = dve.match_replace(marked[:, g, :], best[:, g, :], flat[:, g, :], -3.0e38)
                    link(m)
                    times_up(4)
                    settle()
                    link(dve.tensor_tensor(picked[:], picked[:], pair[:], ALU.not_equal))
                    settle()
                    dve.wait_ge(S.expo_ready, i + 1 + START)
                    link(dve.tensor_tensor(pair[:], picked[:], spread(expo[:, 1], 2, KPH), ALU.mult))
                    with nc.allow_low_precision(reason="whole numbers up to 8, exact in bf16"):
                        link(dve.tensor_reduce(countb[:], picked[:], AX.X, ALU.add))
                    settle()
                    link(dve.tensor_reduce(row_sum[:], pair[:], AX.X, ALU.add))
                    link(dve.tensor_tensor(hot_x, hot_x, spread(countb[:], 2, NHI), ALU.mult))
                    settle()
                    link(dve.tensor_tensor(row_sum[:], row_sum[:], expo[:, 0], ALU.mult))
                    times_up(5)
                    settle()
                    dve.tensor_reduce(total[:], row_sum[:], AX.X, ALU.add).then_inc(S.total_ready, 1)
                    link(dve.scalar_tensor_tensor(out=beyond[:], in0=idxb[:, 0], scalar=float(NHI), in1=row_sum[:],
                                                  op0=ALU.is_ge, op1=ALU.mult))
                    with nc.allow_low_precision(reason="whole numbers up to 8, exact in bf16"):
                        dve.tensor_reduce(digits[:].rearrange("p t h r -> p (t h) r")[:, :, 0:NHI], hot_x, AX.X,
                                          ALU.add).then_inc(S.digits_ready, 1)
                    dve.wait_ge(S.total_ready, i + 1 + START)
                    link(dve.reciprocal(inv_total[:], total[:]))
                    settle()
                    link(dve.tensor_reduce(over[:], beyond[:], AX.X, ALU.add))
                    times_up(6)
                    settle()
                    link(dve.tensor_tensor(over[:], over[:], inv_total[:], ALU.mult))
                    dve.wait_ge(S.ln_ready, i + 1 + START)
                    link(dve.tensor_tensor(offset[:], top[:, 0, :, 0], ln_total[:], ALU.add))
                    settle()
                    link(dve.tensor_reduce(scores[:, :, 0, R], over[:].rearrange("p (t h) -> p t h", h=H), AX.X, ALU.add))
                    dve.tensor_tensor(scores[:, :, :, 0:NHI], sim[:, :, 0, :, 0:NHI],
                                      spread(offset[:].rearrange("p (t h) -> p t h", h=H), 3, NHI),
                                      ALU.subtract).then_inc(S.digits_ready, 1)
                    times_up(7)
                    for h in range(H):
                        dve.wait_ge(S.turned_ready, i * (2 * H) + 2 * (h + 1) + START)
                        dve.tensor_tensor(scoreT[:, 1, h, :], bk[2 + h % 2][0:ROWS, :],
                                          scoreT[:, 0, h, :].bitcast(F32), ALU.subtract).then_inc(S.rest_ready, 1)
                    assert steps[0] == RANK_STEPS, steps

                    def mix(c):
                        both, last = E[:, c % 2, 0], c == FC - 1
                        dve.wait_ge(S.pool_sum, i * POOL_SUMS + 2 * c + 2 + last + START)
                        dve.tensor_tensor(both, both, E[:, c % 2, 2], ALU.add).then_inc(S.mix_step, 1)
                        if c >= 2:
                            dve.wait_ge(S.mix_used, i * FC + c - 1 + START)
                        dve.wait_ge(S.mix_step, i * FC + c + 1 + START)
                        dve.tensor_tensor(mixed[c % 2], both, reach[:, c, :], ALU.mult).then_inc(S.mix_ready, 1)

                    dve.wait_ge(S.mid_used, i * FC + FC + START)
                    for c in range(FC):
                        for h in range(H):
                            n = c * H + h
                            dve.wait_ge(S.E_ready, i * (FC * H) + n + 1 + START)
                            dve.scalar_tensor_tensor(out=E[:, c % 2, h], in0=rank_bank[n % 3], scalar=float(KPH),
                                                     in1=E[:, c % 2, h], op0=ALU.is_gt, op1=ALU.mult
                                                     ).then_inc(S.masked, 1)
                            if c >= 1 and h == 1:
                                mix(c - 1)
                    mix(FC - 1)
                    dve.wait_ge(S.mix_used, i * FC + FC + START)
                    xs = w.x[:, bass.ds(i * TJ, TJ), :].rearrange("p j c -> p (j c)")
                    dve.tensor_tensor(xs, acc[:], xs, ALU.add).then_inc(S.x_added, 1)

            @block.gpsimd
            def _(pool):
                with pool.Fori(0, ROUNDS) as i:
                    pool.wait_ge(S.xn_ready, i * TJ + START)
                    pool.wait_ge(S.mv_ready, i * TJ + TJ + START)
                    pool.tensor_tensor(rstd[:], mv[:, :, 1], w.eps[:, 0:TJ], ALU.add).then_inc(S.var_eps, 1)
                    pool.wait_ge(S.var_eps, i + 1 + START)
                    pool.tensor_tensor(rstd[:], rstd[:], w.minus_half[:, 0:TJ], ALU.pow).then_inc(S.rstd_ready, 1)
                    for t in range(TJ):
                        pool.wait_ge(S.hot_ready, i * TJ + t + 1 + START)
                        pool.tensor_tensor(hot_y[t % 2], hot_y[t % 2], spread(w.rank_weight[:], 1, H), ALU.mult
                                           ).then_inc(S.hot_weighted, 1)
                    pool.wait_ge(S.turned_psum, i * H + START)
                    pool.tensor_tensor(scores[:, :, :, NHI:R], sim[:, :, 1],
                                       spread(top[:, 1, :, 0].rearrange("p (t h) -> p t h", h=H), 3, NKEYS),
                                       ALU.subtract).then_inc(S.second_ready, 1)
                    for c in range(FC):
                        for a in (0, 2):
                            pool.wait_ge(S.masked, i * (FC * H) + c * H + a + 2 + START)
                            pool.tensor_tensor(E[:, c % 2, a], E[:, c % 2, a], E[:, c % 2, a + 1], ALU.add
                                               ).then_inc(S.pool_sum, 1)
                    pool.wait_ge(S.over_ready, i + 1 + START)
                    pool.wait_ge(S.pool_sum, i * POOL_SUMS + 2 * FC + START)
                    pool.tensor_tensor(E[:, (FC - 1) % 2, 2], E[:, (FC - 1) % 2, 2], over_row, ALU.add
                                       ).then_inc(S.pool_sum, 1)

            @block.tensor
            def _(pe):
                with pe.Fori(0, ROUNDS) as i:
                    pe.wait_ge(S.xn_ready, i * TJ + TJ + START)
                    pe.wait_ge(S.masked, i * (FC * H) + START)
                    for k in range(KC):
                        for j in range(TJ):
                            mm = pe.transpose(bk[k][:, j * P:(j + 1) * P], xn[:, j, k * P:(k + 1) * P], w.ident[:])
                    mm.then_inc(S.hT_psum, 1)
                    pe.wait_ge(S.hT_ready, i + 1 + START)
                    for t in range(TJ):
                        if t >= 2:
                            pe.wait_ge(S.sim_ready, i * TJ + t - 1 + START)
                        for k in range(KC):
                            mm = pe.matmul(bk[2 + t % 2], hT[:, k, t * P:(t + 1) * P], w.wsim[:, k, :],
                                           start=(k == 0), stop=(k == KC - 1))
                        mm.then_inc(S.sim_psum, 1)
                    for c in range(FC):
                        if c >= 4:
                            pe.wait_ge(S.reach_ready, i * FC + c - 3 + START)
                        for k in range(KC):
                            mm = pe.matmul(bk[(4, 5, 0, 1)[c % 4]], w.deT[:, k, c * P:(c + 1) * P], hT[:, k, :],
                                           start=(k == 0), stop=(k == KC - 1))
                        mm.then_inc(S.w_psum, 1)
                    pe.wait_ge(S.x_added, i + START)
                    for n in range(2):
                        pe.matmul(acc[:, n * 512:(n + 1) * 512], w.ones3[:], bias(w, "bd", 2), start=True, stop=True)

                    def mlp_out(f):
                        pe.wait_ge(S.mid_ready, i * FC + f + 1 + START)
                        for j in range(TJ):
                            mm = pe.matmul(acc[:, j * C:(j + 1) * C], mid[:, f % 4, j * P:(j + 1) * P], w.wd[:, f, :],
                                           start=False, stop=True, skip_group_check=True)
                        mm.then_inc(S.mid_used, 1)

                    for f in range(FC):
                        if f < 2:
                            pe.wait_ge(S.reach_ready, i * FC + 6 + 2 * f + START)
                        else:
                            pe.wait_ge(S.mid_ready, i * FC + f - 1 + START)
                        g, u = (bk[4], bk[5]) if f % 2 == 0 else (bk[0], bk[1])
                        for out, weights in ((g, w.wg), (u, w.wu)):
                            for k in range(KC):
                                mm = pe.matmul(out, weights[:, k, f * P:(f + 1) * P], hT[:, k, :],
                                               start=(k == 0), stop=(k == KC - 1))
                        mm.then_inc(S.gu_psum, 1)
                        if f >= 1:
                            mlp_out(f - 1)

                    def turn_digits(h):
                        if h >= 2:
                            pe.wait_ge(S.rest_ready, i * H + h - 1 + START)
                        for t in range(TJ):
                            pe.transpose(bk[2 + h % 2][0:ROWS, t * P:(t + 1) * P], scores[:, t, h, :], w.ident[:])
                            mm = pe.transpose(bk[4 + h % 2].bitcast(BF16)[0:ROWS, t * P:(t + 1) * P],
                                              digits[:, t, h, :], w.identb[:])
                        mm.then_inc(S.turned_psum, 1)

                    pe.wait_ge(S.digits_ready, i * 6 + 6 + START)
                    pe.wait_ge(S.second_ready, i + 1 + START)
                    turn_digits(0)
                    turn_digits(1)
                    mlp_out(FC - 1)
                    turn_digits(2)
                    turn_digits(3)

                    def experts(c):
                        pe.wait_ge(S.mix_ready, i * FC + c + 1 + START)
                        for j in range(TJ):
                            mm = pe.matmul(acc[:, j * C:(j + 1) * C], mixed[c % 2][:, j * P:(j + 1) * P],
                                           w.ue[:, c, :], start=False, stop=True, skip_group_check=True)
                        mm.then_inc(S.mix_used, 1)

                    pe.wait_ge(S.rest_ready, i * H + H + START)
                    for part in range(2):
                        mm = pe.matmul(bk[0], w.selovf[:], scoreT[:, part, 0, :], start=(part == 0), stop=(part == 1))
                    mm.then_inc(S.over_psum, 1)
                    for c in range(FC):
                        for h in range(H):
                            n = c * H + h
                            if n == 2:
                                pe.wait_ge(S.over_ready, i + 1 + START)
                            if n >= 3:
                                pe.wait_ge(S.masked, i * (FC * H) + n - 2 + START)
                            pe.matmul(rank_bank[n % 3], w.selb[:, c].rearrange("r a e -> r (a e)"), digitsT[:, h, :],
                                      start=True, stop=True)
                            for part in range(2):
                                mm = pe.matmul(score_bank[n % 3], w.sel[:, c].rearrange("r a e -> r (a e)"),
                                               scoreT[:, part, h, :], start=(part == 0), stop=(part == 1))
                            mm.then_inc(S.ds_psum, 1)
                            if c >= 2 and h == 1:
                                experts(c - 2)
                    experts(FC - 2)
                    experts(FC - 1)

            @block.scalar
            def _(act):
                with act.Fori(0, ROUNDS) as i:
                    act.activation(idle[:], w.eps[:, 0:1], ACT.Silu)
                    act.wait_ge(S.ds_psum, i * (FC * H) + START)
                    for t in range(TJ):
                        act.wait_ge(S.sim_psum, i * TJ + t + 1 + START)
                        act.activation(sim_row[:, t * 512:(t + 1) * 512], bk[2 + t % 2], ACT.Copy).then_inc(S.sim_ready, 1)
                    act.wait_ge(S.mix_ready, i * FC + START)
                    for c in range(FC):
                        act.wait_ge(S.w_psum, i * FC + c + 1 + START)
                        act.activation(reach[:, c, :], bk[(4, 5, 0, 1)[c % 4]], ACT.Silu).then_inc(S.reach_ready, 1)

                    def gates(f):
                        act.wait_ge(S.gu_psum, i * FC + f + 1 + START)
                        if f >= 2:
                            act.wait_ge(S.mid_ready, i * FC + f - 1 + START)
                        act.activation(gate[:, f % 2, :], bk[4] if f % 2 == 0 else bk[0], ACT.Silu,
                                       bias=w.bg[:, f:f + 1]).then_inc(S.gate_ready, 1)

                    for f in range(3):
                        gates(f)
                    act.wait_ge(S.below_ready, i + 1 + START)
                    act.activation(expo[:], below[:], ACT.Exp).then_inc(S.expo_ready, 1)
                    for f in range(3, 7):
                        gates(f)
                    act.wait_ge(S.total_ready, i + 1 + START)
                    act.activation(ln_total[:], total[:], ACT.Ln).then_inc(S.ln_ready, 1)
                    gates(7)
                    for h in range(H):
                        act.wait_ge(S.turned_psum, i * H + h + 1 + START)
                        act.activation(digitsT[:, h, :], bk[4 + h % 2].bitcast(BF16)[0:ROWS, 0:T], ACT.Copy
                                       ).then_inc(S.turned_ready, 1)
                        act.activation(scoreT[:, 0, h, :], bk[2 + h % 2][0:ROWS, :], ACT.Copy
                                       ).then_inc(S.turned_ready, 1)
                    act.wait_ge(S.over_psum, i + 1 + START)
                    act.wait_ge(S.mid_used, i * FC + FC + START)
                    act.activation(over_row, bk[0], ACT.Copy).then_inc(S.over_ready, 1)
                    for c in range(FC):
                        if c >= 2:
                            act.wait_ge(S.mix_ready, i * FC + c - 1 + START)
                        for h in range(H):
                            n = c * H + h
                            act.wait_ge(S.ds_psum, i * (FC * H) + n + 1 + START)
                            act.activation(E[:, c % 2, h], score_bank[n % 3], ACT.Exp).then_inc(S.E_ready, 1)


def linear_attention(nc, w, sem):
    with ExitStack() as ctx:
        def tmp(name, shape, dt=F32):
            return ctx.enter_context(nc.sbuf_tensor(f"b_{name}", shape, dt))

        def psum(name, n):
            return ctx.enter_context(nc.psum_tensor(f"b_{name}", [P, n], F32))

        COL = [0, 640, 1024, 512]
        NCOL = 1280
        NG = 2 * HEADS
        HP = HEADS // 2
        QH = 4
        V1 = FEAT + 1

        score = [psum("score0", 3 * 512), psum("score1", 3 * 512)]
        yb = [psum("y0", 512), psum("y1", 512)]

        stats, mv, rstd = tmp("stats", [P, TJ, 6]), tmp("mv", [P, TJ, 2]), tmp("rstd", [P, TJ])
        pause = tmp("pause", [P, 1])
        xn = tmp("xn", [P, TJ, C])
        hT = tmp("hT", [P, KC, T])
        qk = tmp("qk", [P, TJ * NG, FEAT])
        sums, rms = tmp("sums", [P, TJ * NG]), tmp("rms", [P, TJ * NG])
        eps16 = tmp("eps16", [P, TJ * NG])
        half = tmp("half", [P, TJ * NG])
        stacked = [tmp("q_parts", [P, TJ, HEADS, 4, FEAT]), tmp("k_parts", [P, TJ, HEADS, 4, FEAT])]
        squares = stacked[0][:].rearrange("p t h s f -> p (t h s f)")[:, 0:TJ * NG * FEAT].rearrange(
            "p (g f) -> p g f", f=FEAT)
        qkT = [tmp("qT", [P, HP, T], F32R), tmp("kT", [P, HP, T], F32R)]
        va = tmp("va", [P, TJ, HEADS, V1])
        U = tmp("U", [P, 2, NCOL])
        den, inv = tmp("den", [P, TJ, QH]), tmp("inv", [P, TJ, QH])

        S = w.attn_signals
        consts = sem("b_consts")
        STEPS = 5

        def slots(tile, q, first, second):
            v = tile[:].rearrange("p t h s f -> p (t h) s f")
            return v[:, :, first:second + 1:second - first, :]

        def bank_of(u):
            return score[(u // 3) % 2][:, (u % 3) * 512:(u % 3 + 1) * 512]

        with nc.Block() as block:
            @block.vector
            def _(dve):
                dve.memset(va[:], 1.0).then_inc(consts, 1)
                dve.memset(eps16[:], LN_EPS * FEAT).then_inc(consts, 1)
                dve.memset(half[:], -0.5).then_inc(consts, 1)
                dve.tensor_scalar(w.gamma[:], w.gamma[:], math.sqrt(FEAT), None, ALU.mult).then_inc(consts, 1)
                dve.wait_ge(consts, 4)
                with dve.Fori(0, B) as i:
                    for j in range(TJ):
                        dve.bn_stats(stats[:, j, :], w.x[:, bass.ds(i * TJ + j, 1), :]).then_inc(S.stats_ready, 1)
                    dve.wait_ge(S.stats_ready, i * TJ + TJ + START)
                    dve.memset(pause[:], 0.0)
                    for j in range(TJ):
                        dve.bn_aggr(mv[:, j, :], stats[:, j, :]).then_inc(S.mv_ready, 1)
                    dve.wait_ge(S.rstd_ready, i + 1 + START)
                    for j in range(TJ):
                        dve.tensor_scalar(xn[:, j, :], w.x[:, bass.ds(i * TJ + j, 1), :], mv[:, j, 0:1],
                                          rstd[:, j:j + 1], ALU.subtract, ALU.mult).then_inc(S.xn_ready, 1)
                    for t in range(TJ):
                        dve.wait_ge(S.qkv_psum, i * TJ + t + 1 + START)
                        dve.wait_ge(S.qk_ready, i * TJ + t + 1 + START)
                        dve.tensor_copy(va[:, t, :, 0:FEAT],
                                        score[t % 2][:, 512:512 + C].rearrange("p (h f) -> p h f", f=FEAT)
                                        ).then_inc(S.v_ready, 1)
                    dve.wait_ge(S.qk_ready, i * TJ + TJ + START)
                    dve.tensor_reduce(sums[:], qk[:], AX.X, ALU.add).then_inc(S.feat_step, 1)
                    dve.wait_ge(S.feat_step, i * STEPS + 1 + START)
                    dve.scalar_tensor_tensor(out=qk[:], in0=spread(sums[:], 2, FEAT), scalar=-1.0 / FEAT, in1=qk[:],
                                             op0=ALU.mult, op1=ALU.add).then_inc(S.feat_step, 1)
                    dve.wait_ge(S.squared, i + 1 + START)
                    dve.tensor_reduce(rms[:], squares, AX.X, ALU.add).then_inc(S.var_ready, 1)
                    dve.wait_ge(S.rms_ready, i + 1 + START)
                    dve.tensor_tensor(qk[:], qk[:], spread(rms[:], 2, FEAT), ALU.mult).then_inc(S.feat_step, 1)
                    dve.wait_ge(S.feat_step, i * STEPS + 3 + START)
                    dve.tensor_tensor(qk[:], qk[:], spread(w.gamma[:], 1, TJ * NG), ALU.mult).then_inc(S.feat_step, 1)
                    dve.wait_ge(S.feat_step, i * STEPS + 4 + START)
                    dve.tensor_tensor(qk[:], qk[:], spread(w.beta[:], 1, TJ * NG), ALU.add).then_inc(S.feat_step, 1)
                    dve.wait_ge(S.hi_ready, i * (2 * TJ) + 2 * TJ + START)
                    heads = qk[:].rearrange("p (t m h) f -> p t m h f", m=2, h=HEADS)
                    for m, (hi, lo) in enumerate((((0, 1), (2, 3)), ((0, 2), (1, 3)))):
                        for t in range(TJ):
                            part = stacked[m][:, t]
                            for s in lo:
                                one = dve.tensor_tensor(part[:, :, s, :], heads[:, t, m], part[:, :, 0, :],
                                                        ALU.subtract)
                            one.then_inc(S.lo_ready, 1)
                    for u in range(1, 2 * HP, 2):
                        dve.wait_ge(S.turned_psum, i * (2 * HP) + u + 1 + START)
                        dve.tensor_copy(qkT[u % 2][:, u // 2, :], bank_of(u)).then_inc(S.turned_ready, 1)
                    for n in range(HEADS // QH):
                        dve.wait_ge(S.y_psum, i * HEADS + QH * (n + 1) + START)
                        y = yb[n % 2][:, 0:TJ * QH * V1].rearrange("p (t h f) -> p t h f", t=TJ, f=V1)
                        dve.tensor_scalar(den[:], y[:, :, :, FEAT], 1e-5, None, ALU.add).then_inc(S.den_step, 1)
                        dve.wait_ge(S.den_step, i * (2 * HEADS // QH) + 2 * n + 1 + START)
                        dve.reciprocal(inv[:], den[:]).then_inc(S.den_step, 1)
                        dve.wait_ge(S.den_step, i * (2 * HEADS // QH) + 2 * n + 2 + START)
                        out = xn[:].rearrange("p t (h f) -> p t h f", f=FEAT)[:, :, QH * n:QH * (n + 1), :]
                        dve.tensor_tensor(out, y[:, :, :, 0:FEAT], spread(inv[:], 3, FEAT), ALU.mult
                                          ).then_inc(S.y_ready, 1)
                    dve.wait_ge(S.proj_psum, i + 1 + START)
                    xs = w.x[:, bass.ds(i * TJ, TJ), :].rearrange("p j c -> p (j c)")
                    dve.tensor_tensor(xs, score[1][:, 0:TJ * C], xs, ALU.add).then_inc(S.x_added, 1)

            @block.gpsimd
            def _(pool):
                pool.wait_ge(consts, 4)
                with pool.Fori(0, B) as i:
                    pool.wait_ge(S.xn_ready, i * TJ + START)
                    pool.wait_ge(S.mv_ready, i * TJ + TJ + START)
                    pool.tensor_tensor(rstd[:], mv[:, :, 1], w.eps[:, 0:TJ], ALU.add).then_inc(S.var_eps, 1)
                    pool.wait_ge(S.var_eps, i + 1 + START)
                    pool.tensor_tensor(rstd[:], rstd[:], w.minus_half[:, 0:TJ], ALU.pow).then_inc(S.rstd_ready, 1)
                    pool.wait_ge(S.var_ready, i + 1 + START)
                    pool.tensor_tensor(rms[:], rms[:], eps16[:], ALU.add).then_inc(S.rms_step, 1)
                    pool.wait_ge(S.rms_step, i + 1 + START)
                    pool.tensor_tensor(rms[:], rms[:], half[:], ALU.pow).then_inc(S.rms_ready, 1)
                    for h in range(HEADS):
                        pool.wait_ge(S.U_ready, i * HEADS + h + 1 + START)
                        for at in COL:
                            diagonal = U[:, h % 2, at:at + P]
                            last = pool.tensor_tensor(diagonal, diagonal, w.tri[:], ALU.mult)
                        last.then_inc(S.U_masked, 1)

            @block.tensor
            def _(pe):
                def turn(src, out):
                    for k in range(KC):
                        for j in range(TJ):
                            mm = pe.transpose(out[:, k * T + j * P:k * T + (j + 1) * P],
                                              src[:, j, k * P:(k + 1) * P], w.ident[:])
                    return mm

                with pe.Fori(0, B) as i:
                    pe.wait_ge(S.xn_ready, i * TJ + TJ + START)
                    turn(xn, score[0]).then_inc(S.hT_psum, 1)
                    pe.wait_ge(S.hT_ready, i * 2 + 1 + START)
                    pe.wait_ge(S.x_added, i + START)
                    for t in range(TJ):
                        if t >= 2:
                            pe.wait_ge(S.v_ready, i * TJ + t - 1 + START)
                        for out, weights in ((score[t % 2][:, 0:512], w.wqk), (score[t % 2][:, 512:512 + C], w.wvb)):
                            for k in range(KC):
                                mm = pe.matmul(out, hT[:, k, t * P:(t + 1) * P], weights[:, k, :],
                                               start=(k == 0), stop=(k == KC - 1))
                        mm.then_inc(S.qkv_psum, 1)
                    pe.wait_ge(S.v_ready, i * TJ + TJ + START)
                    for u in range(2 * HP):
                        m, hp = u % 2, u // 2
                        if u == 0:
                            pe.wait_ge(S.lo_ready, i * (2 * TJ) + 2 * TJ + START)
                        if u >= 6:
                            pe.wait_ge(S.turned_ready if m else S.qk_normal, i * HP + (u - 6) // 2 + 1 + START)
                        for t in range(TJ):
                            mm = pe.transpose(bank_of(u)[:, t * P:(t + 1) * P],
                                              stacked[m][:, t, 2 * hp:2 * hp + 2].rearrange("p h s f -> p (h s f)"),
                                              w.ident[:])
                        mm.then_inc(S.turned_psum, 1)

                    def scores(h):
                        rows = slice(64 * (h % 2), 64 * (h % 2) + 64)
                        if h == 0:
                            pe.wait_ge(S.turned_ready, i * HP + HP + START)
                            pe.wait_ge(S.qk_normal, i * HP + HP + START)
                        if h >= 2:
                            pe.wait_ge(S.U_ready, i * HEADS + h - 1 + START)
                        for n, kb in enumerate((0, 3, 1, 2)):
                            mm = pe.matmul(score[h % 2][:, COL[kb]:COL[kb] + T - kb * P],
                                           qkT[1][rows, h // 2, kb * P:(kb + 1) * P], qkT[0][rows, h // 2, kb * P:T],
                                           start=(kb != 1), stop=True, skip_group_check=(kb == 1))
                        mm.then_inc(S.score_psum, 1)

                    def outputs(h):
                        pe.wait_ge(S.U_masked, i * HEADS + h + 1 + START)
                        if h % QH == 0 and h >= 2 * QH:
                            pe.wait_ge(S.y_ready, i * (HEADS // QH) + h // QH - 1 + START)
                        for qb in range(TJ):
                            at = (qb * QH + h % QH) * V1
                            for kb in range(qb + 1):
                                c = COL[kb] + (qb - kb) * P
                                mm = pe.matmul(yb[(h // QH) % 2][:, at:at + V1], U[:, h % 2, c:c + P], va[:, kb, h, :],
                                               start=(kb == 0), stop=(kb == qb))
                        mm.then_inc(S.y_psum, 1)

                    scores(0)
                    for h in range(HEADS):
                        if h + 1 < HEADS:
                            scores(h + 1)
                        outputs(h)
                    pe.wait_ge(S.y_ready, i * (HEADS // QH) + HEADS // QH + START)
                    turn(xn, score[0]).then_inc(S.yT_psum, 1)
                    pe.wait_ge(S.hT_ready, i * 2 + 2 + START)
                    for j in range(TJ):
                        for k in range(KC):
                            mm = pe.matmul(score[1][:, j * C:(j + 1) * C], hT[:, k, j * P:(j + 1) * P], w.wo[:, k, :],
                                           start=(k == 0), stop=(k == KC - 1))
                    mm.then_inc(S.proj_psum, 1)

            @block.scalar
            def _(act):
                with act.Fori(0, B) as i:
                    act.wait_ge(S.hT_psum, i + 1 + START)
                    act.activation(hT[:].rearrange("p k t -> p (k t)"), score[0][:, 0:KC * T], ACT.Copy
                                   ).then_inc(S.hT_ready, 1)
                    for t in range(TJ):
                        act.wait_ge(S.qkv_psum, i * TJ + t + 1 + START)
                        act.activation(qk[:, t * NG:(t + 1) * NG, :].rearrange("p g f -> p (g f)"),
                                       score[t % 2][:, 0:512], ACT.Copy).then_inc(S.qk_ready, 1)
                    act.wait_ge(S.feat_step, i * STEPS + 2 + START)
                    act.activation(squares, qk[:], ACT.Square).then_inc(S.squared, 1)
                    act.wait_ge(S.feat_step, i * STEPS + 5 + START)
                    act.wait_ge(S.var_ready, i + 1 + START)
                    heads = qk[:].rearrange("p (t m h) f -> p t m h f", m=2, h=HEADS)
                    for m, second in ((0, 1), (1, 2)):
                        for t in range(TJ):
                            part = stacked[m][:, t].bitcast(F32R)
                            act.activation(part[:, :, 0, :], heads[:, t, m], ACT.Copy)
                            act.activation(part[:, :, second, :], heads[:, t, m], ACT.Copy).then_inc(S.hi_ready, 1)
                    for u in range(0, 2 * HP, 2):
                        act.wait_ge(S.turned_psum, i * (2 * HP) + u + 1 + START)
                        act.activation(qkT[0][:, u // 2, :], bank_of(u), ACT.Copy).then_inc(S.qk_normal, 1)
                    for h in range(HEADS):
                        act.wait_ge(S.score_psum, i * HEADS + h + 1 + START)
                        if h >= 2:
                            act.wait_ge(S.y_psum, i * HEADS + h - 1 + START)
                        act.activation(U[:, h % 2, :], score[h % 2][:, 0:NCOL], ACT.Square, scale=0.25
                                       ).then_inc(S.U_ready, 1)
                    act.wait_ge(S.yT_psum, i + 1 + START)
                    act.activation(hT[:].rearrange("p k t -> p (k t)"), score[0][:, 0:KC * T], ACT.Copy
                                   ).then_inc(S.hT_ready, 1)


def program(nc, io, phases=("a", "f1", "b", "f2")):
    with ExitStack() as ctx:
        def sb(name, shape, dt=F32):
            return ctx.enter_context(nc.sbuf_tensor(name, shape, dt))

        def sem(name):
            return ctx.enter_context(nc.semaphore(name))

        w = Named()
        w.x = sb("x", [P, B * TJ, C])
        w.ident, w.identb, w.tri = sb("ident", [P, P]), sb("identb", [P, P], BF16), sb("tri", [P, P])
        w.ones3, w.ones3b = sb("ones3", [3, P], BF16), sb("ones3b", [3, T], BF16)
        w.minus_half, w.eps = sb("minus_half", [P, 32]), sb("eps", [P, 32])
        w.iota_lo, w.rank_weight = sb("iota_lo", [P, NKEYS, KPH], BF16), sb("rank_weight", [P, NKEYS, KPH], BF16)
        w.sel, w.selb = sb("sel", [ROWS, FC, 2, NKEYS], F32R), sb("selb", [ROWS, FC, 2, NKEYS], BF16)
        w.selovf = sb("selovf", [ROWS, P], F32R)
        w.bias3 = sb("bias3", [3, NBIAS], BF16)
        w.wg, w.wu, w.wd = sb("wg", [P, KC, DCD]), sb("wu", [P, KC, DCD]), sb("wd", [P, FC, C])
        w.deT, w.ue, w.wsim = sb("deT", [P, KC, NEXP]), sb("ue", [P, FC, C]), sb("wsim", [P, KC, 2 * H * NKEYS])
        w.bg, w.bu = sb("bg", [P, FC]), sb("bu", [P, FC])
        w.wqk, w.wvb, w.wo = sb("wqk", [P, KC, 2 * C]), sb("wvb", [P, KC, C]), sb("wo", [P, KC, C])
        w.gamma, w.beta = sb("gamma", [P, FEAT]), sb("beta", [P, FEAT])

        w.scan_signals, w.attn_signals = ScanSignals(sem, "a"), AttnSignals(sem, "b")
        w.ffn_signals = {"f1": FfnSignals(sem, "f1"), "f2": FfnSignals(sem, "f2")}
        w.all_signals = (w.scan_signals.all + w.attn_signals.all + w.ffn_signals["f1"].all
                         + w.ffn_signals["f2"].all)
        w.x_loaded = [sem(f"x_loaded{b}") for b in range(B)]
        with ExitStack() as scan_ctx:
            def scan_sb(name, shape):
                return scan_ctx.enter_context(nc.sbuf_tensor(name, shape, F32))

            w.wv, w.gq, w.wproj = scan_sb("wv", [P, KC, C]), scan_sb("gq", [P, KC, P]), scan_sb("wproj", [P, KC, C])
            w.wz, w.gz = scan_sb("wz", [P, C]), scan_sb("gz", [P, P])
            setup(nc, w, io, sem)
            scan_attention(nc, w, sem)
        if "f1" in phases:
            experts_ffn(nc, w, sem, "f1")
        if "b" in phases:
            linear_attention(nc, w, sem)
        if "f2" in phases:
            experts_ffn(nc, w, sem, "f2")
        out_stored = sem("out_stored")
        with nc.Block() as block:
            @block.sync
            def _(sp):
                for b in range(B):
                    sp.dma_start(io.out[b].rearrange("(j p) c -> p j c", p=P),
                                 w.x[:, b * TJ:(b + 1) * TJ, :]).then_inc(out_stored, 16)
                sp.wait_ge(out_stored, 16 * B)


def arguments(args, out):
    io = Named()
    (io.x, io.attn_W, io.attn_b, io.freq_W, io.freq_b, io.out_W, io.out_b, io.proj_W, io.proj_b,
     io.identity, io.b_Wq, io.b_Wk, io.b_Wv, io.b_Wo, io.gamma, io.beta, io.Wg, io.bg, io.Wu, io.bu,
     io.Wd, io.bd, io.ffn_Wq, io.keys, io.down_embed, io.up_embed) = args
    io.out = out
    return io


_INPUTS = (
    "L0_attn_a_x",
    "L0_attn_a_attn_W",
    "L0_attn_a_attn_b",
    "L0_attn_a_freq_W",
    "L0_attn_a_freq_b",
    "L0_attn_a_out_W",
    "L0_attn_a_out_b",
    "L0_attn_a_proj_W",
    "L0_attn_a_proj_b",
    "L0_attn_a_identity",
    "L0_attn_b_Wq",
    "L0_attn_b_Wk",
    "L0_attn_b_Wv",
    "L0_attn_b_Wo",
    "L0_attn_b_gamma",
    "L0_attn_b_beta",
    "L0_ffn_Wg",
    "L0_ffn_bg",
    "L0_ffn_Wu",
    "L0_ffn_bu",
    "L0_ffn_Wd",
    "L0_ffn_bd",
    "L0_ffn_Wq",
    "L0_ffn_keys",
    "L0_ffn_down_embed",
    "L0_ffn_up_embed",
)


def kernel(**inputs):
    import numpy as _np
    import concourse.bacc as _bacc
    from concourse.bass_utils import run_bass_kernel_spmd as _run

    nc = _bacc.Bacc("TRN2", target_bir_lowering=False, num_devices=1)
    args, arrays = [], {}
    for name in _INPUTS:
        a = _np.ascontiguousarray(inputs[name])
        arrays[f"in_{name}"] = a
        args.append(nc.dram_tensor(f"in_{name}", a.shape, mybir.dt.from_np(a.dtype), kind="ExternalInput").ap())
    out = nc.dram_tensor("out_x", (B, T, C), F32, kind="ExternalOutput").ap()
    program(nc, arguments(args, out))
    return _run(nc, [arrays], core_ids=[0]).results[0]["out_x"]
```

```python
from contextlib import ExitStack
import math

import concourse.bass as bass
from concourse import mybir

F32 = mybir.dt.float32
F32R = mybir.dt.float32r
BF16 = mybir.dt.bfloat16
U32 = mybir.dt.uint32
ACT = mybir.ActivationFunctionType
ALU = mybir.AluOpType
AX = mybir.AxisListType

P = 128
B, T, C = 8, 512, 256
KC = C // P
TJ = T // P
NF = 64
SHIFTS = [1 << s for s in range(9)]
TURN = 2.0 * math.pi
SIN_SCALE = 6.2831850
MAGIC = 1.5 * 2.0 ** 23
DCD, NEXP, H, NKEYS, KPH = 1024, 1024, 4, 64, 8
FC = DCD // P
NHI = NEXP // NKEYS
ROWS = 96
HEADS, FEAT = 16, 16
LN_EPS = 1e-5

BIAS = {}
_at = 0
for _name, _n in (("v", C), ("gq", P), ("z", C), ("gz", P), ("proj", C), ("bd", C), ("f", P), ("id", P)):
    BIAS[_name] = (_at, _at + _n)
    _at += _n
NBIAS = _at

START = 1


class Named:
    pass


class ScanSignals:
    def __init__(self, sem, tag):
        self.all = [sem(f"{tag}_{n}") for n in (
            "stats_ready mv_ready var_eps rstd_ready xn_ready xT_psum xT_ready z_psum v_ready gs_ready "
            "f_psum whole_ready turns_ready wave_ready peak_ready peak_eps scale_ready y_ready y_psum "
            "proj_psum x_added "
        ).split()]
        (self.stats_ready, self.mv_ready, self.var_eps, self.rstd_ready, self.xn_ready, self.xT_psum,
         self.xT_ready, self.z_psum, self.v_ready, self.gs_ready, self.f_psum, self.whole_ready,
         self.turns_ready, self.wave_ready, self.peak_ready, self.peak_eps, self.scale_ready, self.y_ready,
         self.y_psum, self.proj_psum, self.x_added) = self.all


class FfnSignals:
    def __init__(self, sem, tag):
        self.all = [sem(f"{tag}_{n}") for n in (
            "stats_ready mv_ready var_eps rstd_ready xn_ready hT_psum hT_ready sim_psum sim_ready "
            "gu_psum gate_ready mid_ready w_psum reach_ready rank_step below_ready expo_ready "
            "total_ready ln_ready digits_ready turned_psum turned_ready ds_psum E_ready masked pool_sum "
            "mix_ready mix_used over_psum x_added mix_step top_ready hot_ready hot_weighted second_ready rest_ready mid_used over_ready "
        ).split()]
        (self.stats_ready, self.mv_ready, self.var_eps, self.rstd_ready, self.xn_ready, self.hT_psum,
         self.hT_ready, self.sim_psum, self.sim_ready, self.gu_psum, self.gate_ready, self.mid_ready,
         self.w_psum, self.reach_ready, self.rank_step, self.below_ready, self.expo_ready, self.total_ready,
         self.ln_ready, self.digits_ready, self.turned_psum, self.turned_ready, self.ds_psum, self.E_ready,
         self.masked, self.pool_sum, self.mix_ready, self.mix_used, self.over_psum, self.x_added,
         self.mix_step, self.top_ready, self.hot_ready, self.hot_weighted,
         self.second_ready, self.rest_ready, self.mid_used, self.over_ready) = self.all


class AttnSignals:
    def __init__(self, sem, tag):
        self.all = [sem(f"{tag}_{n}") for n in (
            "stats_ready mv_ready var_eps rstd_ready xn_ready qk_psum qk_ready squared var_ready "
            "rms_step rms_ready feat_step hi_ready lo_ready filled act_read dve_read masked "
            "y_psum y_copied y_turned den_step y_ready "
        ).split()]
        (self.stats_ready, self.mv_ready, self.var_eps, self.rstd_ready, self.xn_ready, self.qk_psum,
         self.qk_ready, self.squared, self.var_ready, self.rms_step, self.rms_ready, self.feat_step,
         self.hi_ready, self.lo_ready, self.filled, self.act_read, self.dve_read, self.masked,
         self.y_psum, self.y_copied, self.y_turned, self.den_step,
         self.y_ready) = self.all


def spread(ap, axis, n):
    out = ap.unsqueeze(axis)
    shape = list(out.shape)
    shape[axis] = n
    return out.to_broadcast(shape)


def setup(nc, w, io, sem):
    with ExitStack() as ctx:
        def tmp(name, shape, dt=F32):
            return ctx.enter_context(nc.sbuf_tensor(name, shape, dt))

        bank = [ctx.enter_context(nc.psum_tensor(f"setup_bank{i}", [P, 512], F32)) for i in range(4)]
        loaded = sem("loaded")
        ident_ready = sem("ident_ready")
        steps = sem("pool_steps")
        job_done, job_out = sem("job_done"), sem("job_out")
        bias_made, bias_moved = sem("bias_made"), sem("bias_moved")

        sel0, selovf0 = tmp("sel0", [ROWS, FC, 2, NKEYS]), tmp("selovf0", [ROWS, P])
        outw = tmp("outw", [P, C])
        freqw = tmp("freqw", [P, 4, NF])
        attnw = tmp("attnw", [P, KC, 2 * C])
        outwT = tmp("outwT", [P, KC, P])
        attnqT = tmp("attnqT", [P, KC, C])
        bq_col, bo_col, id_col = tmp("bq_col", [P, KC]), tmp("bo_col", [P, KC]), tmp("id_col", [P, KC])
        ffq = tmp("ffq", [P, KC, H, 2, NKEYS])
        ffqT = tmp("ffqT", [P, H, C])
        keys = tmp("keys_rows", [P, 2, P])
        keysT = tmp("keysT", [P, 2, P])
        de = tmp("de_rows", [P, FC, C])
        wrow = tmp("wrow", [P, 4, 2, C])
        brow = tmp("brow", [1, NBIAS])
        rest = tmp("rest", [1, NBIAS])
        parts = tmp("parts", [1, 3, NBIAS], BF16)
        fq_row = tmp("fq_row", [1, NF])

        loads = [
            (outw[:], io.out_W), (freqw[:], io.freq_W.rearrange("(k p) n -> p k n", p=P)),
            (attnw[:], io.attn_W.rearrange("(k p) n -> p k n", p=P)),
            (bq_col[:], io.attn_b[0:C].rearrange("(k p) -> p k", p=P)),
            (bo_col[:], io.out_b.rearrange("(k p) -> p k", p=P)),
            (id_col[:], io.identity.rearrange("(k p) -> p k", p=P)),
            (brow[0:1, BIAS["v"][0]:BIAS["v"][1]], io.attn_b[C:2 * C].unsqueeze(0)),
            (brow[0:1, BIAS["z"][0]:BIAS["z"][1]], io.out_b.unsqueeze(0)),
            (brow[0:1, BIAS["proj"][0]:BIAS["proj"][1]], io.proj_b.unsqueeze(0)),
            (brow[0:1, BIAS["bd"][0]:BIAS["bd"][1]], io.bd.unsqueeze(0)),
            (fq_row[:], io.freq_b.unsqueeze(0)),
            (w.wz[:], io.out_W), (w.wproj[:], io.proj_W.rearrange("(k p) n -> p k n", p=P)),
            (w.wv[:], io.attn_W[:, C:2 * C].rearrange("(k p) n -> p k n", p=P)),
            (keys[:], io.keys.rearrange("(a b) k q n -> (b k) a (q n)", a=2)),
            (de[:], io.down_embed.rearrange("(e p) c -> p e c", p=P)),
            (w.ue[:], io.up_embed.rearrange("(e p) c -> p e c", p=P)),
            (w.wg[:], io.Wg.rearrange("(k p) n -> p k n", p=P)),
            (w.wu[:], io.Wu.rearrange("(k p) n -> p k n", p=P)),
            (w.wd[:], io.Wd.rearrange("(f p) n -> p f n", p=P)),
            (w.bg[:], io.bg.rearrange("(f p) -> p f", p=P)),
            (w.bu[:], io.bu.rearrange("(f p) -> p f", p=P)),
            (w.gamma[:], io.gamma.partition_broadcast(P)),
            (w.beta[:], io.beta.partition_broadcast(P)),
        ]
        for k in range(KC):
            for q in range(2):
                loads.append((ffq[:, k, :, q, :], io.ffn_Wq[k * P:(k + 1) * P, q * C:(q + 1) * C]
                              .rearrange("p (h n) -> p h n", h=H)))
        for m, src in enumerate((io.b_Wq, io.b_Wk, io.b_Wv, io.b_Wo)):
            loads.append((wrow[:, m], src.rearrange("(r p) c -> p r c", p=P)))

        jobs = []

        def turned(src, dst):
            jobs.append(([(src, None)], P, dst, 1.0))

        for k in range(KC):
            turned(outw[:, k * P:(k + 1) * P], outwT[:, k, :])
            for r in range(KC):
                turned(attnw[:, r, k * P:(k + 1) * P], attnqT[:, k, r * P:(r + 1) * P])
            for h in range(H):
                turned(ffq[:, k, h].rearrange("p q n -> p (q n)"), ffqT[:, h, k * P:(k + 1) * P])
            turned(keys[:, k, :], keysT[:, k, :])
            for e in range(FC):
                turned(de[:, e, k * P:(k + 1) * P], w.deT[:, k, e * P:(e + 1) * P])
            for r in range(2):
                turned(wrow[:, 0, r, k * P:(k + 1) * P], w.wqk[:, k, r * P:(r + 1) * P])
                turned(wrow[:, 1, r, k * P:(k + 1) * P], w.wqk[:, k, C + r * P:C + (r + 1) * P])
                turned(wrow[:, 2, r, k * P:(k + 1) * P], w.wvb[:, k, r * P:(r + 1) * P])
                turned(wrow[:, 3, r, k * P:(k + 1) * P], w.wo[:, k, r * P:(r + 1) * P])
        for half in range(2):
            fw = [freqw[:, 2 * half + k, :] for k in range(KC)]
            cols = slice(half * NF, (half + 1) * NF)
            jobs.append(([(outwT[:, k, :], fw[k]) for k in range(KC)], P, w.gz[:, cols], 1.0 / TURN))
            for r in range(KC):
                jobs.append(([(attnqT[:, k, r * P:(r + 1) * P], fw[k]) for k in range(KC)],
                             P, w.gq[:, r, cols], 1.0 / TURN))
            for name, col in (("gz", bo_col), ("gq", bq_col)):
                at = BIAS[name][0] + half * NF
                jobs.append(([(col[:, k:k + 1], fw[k]) for k in range(KC)], 1, brow[0:1, at:at + NF], 1.0 / TURN))
            if half == 0:
                for d in range(2):
                    at = BIAS["id"][0] + d * NF
                    jobs.append(([(id_col[:, k:k + 1], fw[k]) for k in range(KC)], 1,
                                 brow[0:1, at:at + NF], 1.0 / TURN))
        for q in range(2):
            for h in range(H):
                rows = slice(q * NKEYS, (q + 1) * NKEYS)
                for k in range(KC):
                    jobs.append(([(ffqT[rows, h, k * P:(k + 1) * P],
                                   keysT[rows, h // 2, (h % 2) * NKEYS:(h % 2 + 1) * NKEYS])],
                                 P, w.wsim[:, k, (q * H + h) * NKEYS:(q * H + h + 1) * NKEYS], 1.0))

        with nc.Block() as block:
            @block.sync
            def _(sp):
                for dst, src in loads:
                    sp.dma_start(dst, src, allow_slow_non_contiguous=True).then_inc(loaded, 16)
                for b in range(B):
                    sp.dma_start(w.x[:, b * TJ:(b + 1) * TJ, :],
                                 io.x[b].rearrange("(j p) c -> p j c", p=P)).then_inc(w.x_loaded[b], 16)
                for signal in w.all_signals:
                    sp.sem_inc(signal, START)
                sp.wait_ge(bias_made, 1)
                sp.dma_start(w.bias3[:], parts[:]).then_inc(bias_moved, 16)
                sp.wait_ge(bias_moved, 16)

            @block.gpsimd
            def _(pool):
                pool.memset(w.ident[:], 0.0).then_inc(steps, 1)
                pool.memset(w.tri[:], 1.0).then_inc(steps, 1)
                pool.memset(w.ones3[:], 1.0)
                pool.memset(w.ones3b[:], 1.0)
                pool.memset(w.minus_half[:], -0.5)
                pool.memset(w.eps[:], LN_EPS)
                pool.memset(sel0[:], 0.0).then_inc(steps, 1)
                pool.memset(selovf0[:], 0.0).then_inc(steps, 1)
                pool.iota(w.iota_lo[:], pattern=[[1, NKEYS], [0, KPH]], base=0, channel_multiplier=0,
                          allow_small_or_imprecise_dtypes=True)
                pool.iota(w.rank_weight[:], pattern=[[0, NKEYS], [-1, KPH]], base=KPH, channel_multiplier=0,
                          allow_small_or_imprecise_dtypes=True)
                pool.wait_ge(steps, 1)
                pool.affine_select(out=w.ident[:], in_=w.ident[:], compare_op=ALU.not_equal, fill=1.0, base=0,
                                   pattern=[[-1, P]], channel_multiplier=1).then_inc(ident_ready, 1)
                pool.wait_ge(ident_ready, 1)
                pool.tensor_copy(w.identb[:], w.ident[:])
                pool.wait_ge(steps, 2)
                pool.affine_select(out=w.tri[:], in_=w.tri[:], compare_op=ALU.is_ge, fill=0.0, base=0,
                                   pattern=[[1, P]], channel_multiplier=-1)
                pool.wait_ge(steps, 4)
                pool.affine_select(out=sel0[:], in_=sel0[:], compare_op=ALU.not_equal, fill=1.0,
                                   base=0, pattern=[[-2, FC], [-1, 2], [0, NKEYS]],
                                   channel_multiplier=1).then_inc(steps, 1)
                pool.wait_ge(steps, 5)
                pool.affine_select(out=sel0[:], in_=sel0[:], compare_op=ALU.not_equal, fill=1.0,
                                   base=-NHI, pattern=[[0, FC], [0, 2], [-1, NKEYS]],
                                   channel_multiplier=1).then_inc(steps, 1)
                pool.affine_select(out=selovf0[:, P - 1:P], in_=selovf0[:, P - 1:P], compare_op=ALU.not_equal,
                                   fill=1.0, base=-(NHI + NKEYS), pattern=[[0, 1]], channel_multiplier=1
                                   ).then_inc(steps, 1)

            @block.tensor
            def _(pe):
                pe.wait_ge(loaded, 16 * len(loads))
                pe.wait_ge(ident_ready, 1)
                for n, (products, m, dst, scale) in enumerate(jobs):
                    if n >= 4:
                        pe.wait_ge(job_out, n - 3)
                    width = products[0][1].shape[-1] if products[0][1] is not None else P
                    out = bank[n % 4][0:m, 0:width]
                    if products[0][1] is None:
                        pe.transpose(out, products[0][0], w.ident[:]).then_inc(job_done, 1)
                        turned_last = n
                        continue
                    if n == turned_last + 1:
                        pe.wait_ge(job_out, n)
                    for k, (lhsT, rhs) in enumerate(products):
                        mm = pe.matmul(out, lhsT, rhs, start=(k == 0), stop=(k == len(products) - 1))
                    mm.then_inc(job_done, 1)

            @block.vector
            def _(dve):
                for n, (products, m, dst, scale) in enumerate(jobs):
                    width = products[0][1].shape[-1] if products[0][1] is not None else P
                    dve.wait_ge(job_done, n + 1)
                    src = bank[n % 4][0:m, 0:width]
                    if scale == 1.0:
                        dve.tensor_copy(dst, src).then_inc(job_out, 1)
                    else:
                        dve.tensor_scalar(dst, src, scale, None, ALU.mult).then_inc(job_out, 1)
                dve.wait_ge(steps, 7)
                dve.tensor_copy(w.sel[:], sel0[:])
                dve.tensor_copy(w.selb[:], sel0[:])
                dve.tensor_copy(w.selovf[:], selovf0[:])
                chain = sem("bias_chain")
                f0 = BIAS["f"][0]
                dve.wait_ge(loaded, 16 * len(loads))
                dve.wait_ge(job_out, len(jobs))
                dve.tensor_scalar(brow[0:1, f0:f0 + NF], fq_row[:], 1.0 / TURN, None, ALU.mult).then_inc(chain, 1)
                dve.tensor_scalar(brow[0:1, f0 + NF:f0 + 2 * NF], fq_row[:], 1.0 / TURN, 0.25,
                                  ALU.mult, ALU.add).then_inc(chain, 1)
                dve.wait_ge(chain, 2)
                dve.tensor_copy(parts[0:1, 0, :], brow[:]).then_inc(chain, 1)
                dve.wait_ge(chain, 3)
                dve.tensor_tensor(rest[:], brow[:], parts[0:1, 0, :], ALU.subtract).then_inc(chain, 1)
                dve.wait_ge(chain, 4)
                dve.tensor_copy(parts[0:1, 1, :], rest[:]).then_inc(chain, 1)
                dve.wait_ge(chain, 5)
                dve.tensor_tensor(brow[:], rest[:], parts[0:1, 1, :], ALU.subtract).then_inc(chain, 1)
                dve.wait_ge(chain, 6)
                dve.tensor_copy(parts[0:1, 2, :], brow[:]).then_inc(bias_made, 1)


def bias(w, name, times=1):
    a, b = BIAS[name]
    return spread(w.bias3[:, a:b], 1, times) if times > 1 else w.bias3[:, a:b]


def scan_attention(nc, w, sem):
    with ExitStack() as ctx:
        def tmp(name, shape, dt=F32):
            return [ctx.enter_context(nc.sbuf_tensor(f"{name}{lane}", shape, dt)) for lane in range(2)]

        def psum(name, n):
            return [ctx.enter_context(nc.psum_tensor(f"{name}{lane}", [P, n], F32)) for lane in range(2)]

        zb, gb, fb = psum("zb", 4 * C), psum("gb", 4 * P), psum("fb", T)
        stats, mv, rstd = tmp("a_stats", [P, TJ, 6]), tmp("a_mv", [P, TJ, 2]), tmp("a_rstd", [P, TJ])
        xn = tmp("a_xn", [P, TJ, C])
        xT = tmp("a_xT", [P, KC, T])
        v = tmp("a_v", [P, TJ, C])
        gs = tmp("a_gs", [P, 2 * TJ, 2, NF])
        whole, turns, wave = tmp("a_whole", [P, T]), tmp("a_turns", [P, T]), tmp("a_wave", [P, T])
        pause = tmp("a_pause", [P, 1])
        peak, scale = tmp("a_peak", [P, TJ]), tmp("a_scale", [P, TJ])

        S = w.scan_signals
        NS = len(SHIFTS)
        ROUNDS = B // 2

        def twice(g):
            return spread(g[:].rearrange("p (q n) -> p q n", n=NF), 2, 2)

        def nth(i, per_lane, k, lane):
            return i * (2 * per_lane) + 2 * k + lane + 1

        with nc.Block() as block:
            @block.vector
            def _(dve):
                for b in range(B):
                    dve.wait_ge(w.x_loaded[b], 16)
                with dve.Fori(0, ROUNDS) as i:
                    for l in range(2):
                        for j in range(TJ):
                            dve.bn_stats(stats[l][:, j, :], w.x[:, bass.ds(i * 2 * TJ + l * TJ + j, 1), :]
                                         ).then_inc(S.stats_ready, 1)
                        dve.wait_ge(S.stats_ready, i * (2 * TJ) + (l + 1) * TJ + START)
                        dve.memset(pause[l][:], 0.0)
                        for j in range(TJ):
                            dve.bn_aggr(mv[l][:, j, :], stats[l][:, j, :]).then_inc(S.mv_ready, 1)
                    for l in range(2):
                        dve.wait_ge(S.rstd_ready, nth(i, 1, 0, l) + START)
                        for j in range(TJ):
                            dve.tensor_scalar(xn[l][:, j, :], w.x[:, bass.ds(i * 2 * TJ + l * TJ + j, 1), :],
                                              mv[l][:, j, 0:1], rstd[l][:, j:j + 1],
                                              ALU.subtract, ALU.mult).then_inc(S.xn_ready, 1)
                    for l in range(2):
                        dve.wait_ge(S.z_psum, nth(i, NS + 1, 0, l) + START)
                        dve.tensor_copy(gs[l][:], twice(gb[l])).then_inc(S.gs_ready, 1)
                    for s in range(NS):
                        for l in range(2):
                            dve.wait_ge(S.whole_ready, nth(i, NS, s, l) + START)
                            dve.scalar_tensor_tensor(out=turns[l][:], in0=whole[l][:], scalar=MAGIC, in1=fb[l][:],
                                                     op0=ALU.subtract, op1=ALU.subtract).then_inc(S.turns_ready, 1)
                        for l in range(2):
                            dve.wait_ge(S.z_psum, nth(i, NS + 1, s + 1, l) + START)
                            dve.tensor_reduce(peak[l][:], zb[l][:].rearrange("p (j c) -> p j c", c=C), AX.X, ALU.max,
                                              apply_absolute_value=True).then_inc(S.peak_ready, 1)
                            dve.wait_ge(S.peak_ready, nth(i, NS, s, l) + START)
                            dve.tensor_scalar(peak[l][:], peak[l][:], 1e-6, None, ALU.add).then_inc(S.peak_eps, 1)
                            dve.wait_ge(S.peak_eps, nth(i, NS, s, l) + START)
                            dve.reciprocal(scale[l][:], peak[l][:]).then_inc(S.scale_ready, 1)
                            dve.wait_ge(S.scale_ready, nth(i, NS, s, l) + START)
                            if s < NS - 1:
                                for j in range(TJ):
                                    g = dve.tensor_scalar(gs[l][:, 2 * j:2 * j + 2], twice(gb[l])[:, 2 * j:2 * j + 2],
                                                          scale[l][:, j:j + 1], None, ALU.mult)
                                g.then_inc(S.gs_ready, 1)
                            else:
                                dve.wait_ge(S.v_ready, nth(i, 1, 0, l) + START)
                                for j in range(TJ):
                                    dve.scalar_tensor_tensor(out=xn[l][:, j, :], in0=zb[l][:, j * C:(j + 1) * C],
                                                             scalar=scale[l][:, j:j + 1], in1=v[l][:, j, :],
                                                             op0=ALU.mult, op1=ALU.mult).then_inc(S.y_ready, 1)
                    for l in range(2):
                        dve.wait_ge(S.proj_psum, nth(i, 1, 0, l) + START)
                        xs = w.x[:, bass.ds((i * 2 + l) * TJ, TJ), :].rearrange("p j c -> p (j c)")
                        dve.tensor_tensor(xs, zb[l][:], xs, ALU.add).then_inc(S.x_added, 1)

            @block.gpsimd
            def _(pool):
                with pool.Fori(0, ROUNDS) as i:
                    for l in range(2):
                        pool.wait_ge(S.mv_ready, i * (2 * TJ) + (l + 1) * TJ + START)
                        pool.wait_ge(S.xn_ready, i * (2 * TJ) + START)
                        pool.tensor_tensor(rstd[l][:], mv[l][:, :, 1], w.eps[:, 0:TJ], ALU.add).then_inc(S.var_eps, 1)
                        pool.wait_ge(S.var_eps, nth(i, 1, 0, l) + START)
                        pool.tensor_tensor(rstd[l][:], rstd[l][:], w.minus_half[:, 0:TJ], ALU.pow
                                           ).then_inc(S.rstd_ready, 1)

            @block.tensor
            def _(pe):
                def turn_to(l, src, out):
                    for k in range(KC):
                        for j in range(TJ):
                            mm = pe.transpose(out[:, k * T + j * P:k * T + (j + 1) * P],
                                              src[:, j, k * P:(k + 1) * P], w.ident[:])
                    return mm

                def tokens(l, lhsT, rz, rg, bz, bg):
                    for n in range(2):
                        pe.matmul(zb[l][:, n * T:(n + 1) * T], w.ones3[:], bias(w, bz, 2), start=True, stop=True)
                    if rg is not None:
                        pe.matmul(gb[l][:], w.ones3[:], bias(w, bg, TJ), start=True, stop=True)
                    for j in range(TJ):
                        for k, a in enumerate(lhsT):
                            last = k == len(lhsT) - 1
                            mm = pe.matmul(zb[l][:, j * C:(j + 1) * C], a[:, j * P:(j + 1) * P], rz[k],
                                           start=False, stop=last, skip_group_check=True)
                            if rg is not None:
                                mm = pe.matmul(gb[l][:, j * P:(j + 1) * P], a[:, j * P:(j + 1) * P], rg[k],
                                               start=False, stop=last, skip_group_check=True)
                    return mm

                with pe.Fori(0, ROUNDS) as i:
                    for l in range(2):
                        pe.wait_ge(S.xn_ready, i * (2 * TJ) + (l + 1) * TJ + START)
                        pe.wait_ge(S.x_added, i * 2 + START)
                        turn_to(l, xn[l], zb[l]).then_inc(S.xT_psum, 1)
                    for l in range(2):
                        pe.wait_ge(S.xT_ready, nth(i, 2, 0, l) + START)
                        tokens(l, [xT[l][:, k, :] for k in range(KC)], [w.wv[:, k, :] for k in range(KC)],
                               [w.gq[:, k, :] for k in range(KC)], "v", "gq").then_inc(S.z_psum, 1)
                    for s, n in enumerate(SHIFTS):
                        for l in range(2):
                            pe.wait_ge(S.gs_ready, nth(i, NS, s, l) + START)
                            pe.matmul(fb[l][:], bias(w, "f"), w.ones3b[:], start=True, stop=True)
                            pe.matmul(fb[l][:, 0:n], bias(w, "id"), w.ones3b[:, 0:n], start=False, stop=False,
                                      skip_group_check=True)
                            for j in range(TJ):
                                width = min(P, T - j * P - n)
                                if width > 0:
                                    prev = gs[l][:, 2 * j].rearrange("p d n -> p (d n)")
                                    pe.matmul(fb[l][:, j * P + n:j * P + n + width], prev, w.ident[:, 0:width],
                                              start=False, stop=False, skip_group_check=True)
                            for j in range(TJ):
                                own = gs[l][:, 2 * j + 1].rearrange("p d n -> p (d n)")
                                mm = pe.matmul(fb[l][:, j * P:(j + 1) * P], own, w.ident[:],
                                               start=False, stop=True, skip_group_check=True)
                            mm.then_inc(S.f_psum, 1)
                        for l in range(2):
                            pe.wait_ge(S.wave_ready, nth(i, NS, s, l) + START)
                            if s == 0:
                                pe.wait_ge(S.v_ready, nth(i, 1, 0, l) + START)
                            more = s < NS - 1
                            tokens(l, [wave[l]], [w.wz[:]], [w.gz[:]] if more else None,
                                   "z", "gz").then_inc(S.z_psum, 1)
                    for l in range(2):
                        pe.wait_ge(S.y_ready, i * (2 * TJ) + (l + 1) * TJ + START)
                        turn_to(l, xn[l], zb[l]).then_inc(S.y_psum, 1)
                    for l in range(2):
                        pe.wait_ge(S.xT_ready, nth(i, 2, 1, l) + START)
                        tokens(l, [xT[l][:, k, :] for k in range(KC)], [w.wproj[:, k, :] for k in range(KC)],
                               None, "proj", None).then_inc(S.proj_psum, 1)

            @block.scalar
            def _(act):
                with act.Fori(0, ROUNDS) as i:
                    for l in range(2):
                        act.wait_ge(S.xT_psum, nth(i, 1, 0, l) + START)
                        act.activation(xT[l][:].rearrange("p k t -> p (k t)"), zb[l][:], ACT.Copy).then_inc(S.xT_ready, 1)
                    for l in range(2):
                        act.wait_ge(S.z_psum, nth(i, NS + 1, 0, l) + START)
                        act.activation(v[l][:].rearrange("p j c -> p (j c)"), zb[l][:], ACT.Copy).then_inc(S.v_ready, 1)
                    for s in range(NS):
                        for l in range(2):
                            act.wait_ge(S.f_psum, nth(i, NS, s, l) + START)
                            act.activation(whole[l][:], fb[l][:], ACT.Copy, bias=MAGIC).then_inc(S.whole_ready, 1)
                        for l in range(2):
                            act.wait_ge(S.turns_ready, nth(i, NS, s, l) + START)
                            act.activation(wave[l][:], turns[l][:], ACT.Sin, scale=-SIN_SCALE).then_inc(S.wave_ready, 1)
                    for l in range(2):
                        act.wait_ge(S.y_psum, nth(i, 1, 0, l) + START)
                        act.activation(xT[l][:].rearrange("p k t -> p (k t)"), zb[l][:], ACT.Copy).then_inc(S.xT_ready, 1)


def experts_ffn(nc, w, sem, tag):
    with ExitStack() as ctx:
        def tmp(name, shape, dt=F32):
            return ctx.enter_context(nc.sbuf_tensor(f"{tag}_{name}", shape, dt))

        def psum(name, n):
            return ctx.enter_context(nc.psum_tensor(f"{tag}_{name}", [P, n], F32))

        G = TJ * H
        R = NHI + NKEYS

        bk01, bk2, bk3, bk4, bk5, acc = (
            psum("bk01", 1024), psum("bk2", 512), psum("bk3", 512), psum("bk4", 512), psum("bk5", 512),
            psum("acc", TJ * C))
        bk = [bk01[:, 0:512], bk01[:, 512:1024], bk2[:], bk3[:], bk4[:], bk5[:]]
        rank_bank, score_bank = [bk[2], bk[3], bk[0]], [bk[4], bk[5], bk[1]]

        stats, mv, rstd = tmp("stats", [P, TJ, 6]), tmp("mv", [P, TJ, 2]), tmp("rstd", [P, TJ])
        xn = tmp("xn", [P, TJ, C])
        hot_x = xn[:].rearrange("p j c -> p (j c)").bitcast(BF16).rearrange("p (g r i) -> p g r i", g=G, i=KPH)
        hT = tmp("hT", [P, KC, T])
        sim_row = tmp("sim", [P, TJ * 512])
        sim = sim_row[:].rearrange("p (t q h k) -> p t q h k", q=2, h=H, k=NKEYS)
        top, idx, idxb = tmp("top", [P, 2, G, KPH]), tmp("idx", [P, 2, G, KPH], U32), tmp("idxb", [P, 2, G, KPH], BF16)
        pair, best = tmp("pair", [P, G, KPH, KPH]), tmp("best", [P, G, KPH])
        picked = tmp("picked", [P, G, KPH, KPH])
        hot_y = [x[:].rearrange("p g i j -> p (g i j)").bitcast(BF16).rearrange("p (h k j) -> p h k j", h=H, j=KPH)
                 for x in (picked, pair)]
        count, countb = tmp("count", [P, G, KPH]), tmp("countb", [P, G, KPH], BF16)
        below, expo = tmp("below", [P, 2, G, KPH]), tmp("expo", [P, 2, G, KPH])
        row_sum, beyond = tmp("row_sum", [P, G, KPH]), tmp("beyond", [P, G, KPH])
        total, ln_total, inv_total, offset, over = (tmp(n, [P, G]) for n in (
            "total", "ln_total", "inv_total", "offset", "over"))
        idle = tmp("idle", [P, 1])
        pause = tmp("pause", [P, 16])
        digits = tmp("digits", [P, TJ, H, ROWS], BF16)
        scores = tmp("scores", [P, TJ, H, ROWS])
        digitsT = tmp("digitsT", [ROWS, H, T], BF16)
        scoreT = tmp("scoreT", [ROWS, 2, H, T], F32R)
        gate = tmp("gate", [P, 2, T])
        mid = tmp("mid", [P, 4, T])
        mixed, over_row = [mid[:, 0, :], mid[:, 1, :]], mid[:, 3, :]
        reach = tmp("reach", [P, FC, T])
        E = tmp("E", [P, 2, H, T])

        S = w.ffn_signals[tag]
        ROUNDS = B
        RANK_STEPS = 24
        POOL_SUMS = 2 * FC + 1

        with nc.Block() as block:
            @block.vector
            def _(dve):
                dve.memset(digits[:], 0.0)
                dve.memset(scores[:], 0.0)

                def moments(r):
                    for j in range(TJ):
                        dve.bn_stats(stats[:, j, :], w.x[:, bass.ds(r * TJ + j, 1), :]).then_inc(S.stats_ready, 1)
                    dve.wait_ge(S.stats_ready, r * TJ + TJ + START)
                    dve.memset(pause[:, 15:16], 0.0)
                    for j in range(TJ):
                        dve.bn_aggr(mv[:, j, :], stats[:, j, :]).then_inc(S.mv_ready, 1)

                def normalise(r):
                    dve.wait_ge(S.rstd_ready, r + 1 + START)
                    for j in range(TJ):
                        dve.tensor_scalar(xn[:, j, :], w.x[:, bass.ds(r * TJ + j, 1), :], mv[:, j, 0:1],
                                          rstd[:, j:j + 1], ALU.subtract, ALU.mult).then_inc(S.xn_ready, 1)

                def a_round(i, last):
                    steps, pauses = [0], [0]

                    def carry_wait():
                        dve.memset(pause[:, pauses[0]:pauses[0] + 1], 0.0)
                        pauses[0] += 1

                    def link(ins):
                        steps[0] += 1
                        ins.then_inc(S.rank_step, 1)

                    def settle(carry=False):
                        dve.wait_ge(S.rank_step, i * RANK_STEPS + steps[0] + START)
                        if carry:
                            carry_wait()

                    def times_up(f):
                        dve.wait_ge(S.gate_ready, i * FC + f + 1 + START)
                        dve.wait_ge(S.mid_used, i * FC + max(f - 3, 0) + START)
                        up = bk[5] if f % 2 == 0 else bk[1]
                        dve.scalar_tensor_tensor(out=mid[:, f % 4, :], in0=up, scalar=w.bu[:, f:f + 1],
                                                 in1=gate[:, f % 2, :], op0=ALU.add, op1=ALU.mult
                                                 ).then_inc(S.mid_ready, 1)

                    def rank_lo(t):
                        dve.wait_ge(S.hot_weighted, i * TJ + t + 1 + START)
                        with nc.allow_low_precision(reason="whole numbers up to 8, exact in bf16"):
                            dve.tensor_reduce(digits[:, t, :, NHI:R], hot_y[t % 2], AX.X, ALU.add
                                              ).then_inc(S.digits_ready, 1)

                    for t in range(TJ):
                        of_tile = slice(t * H, (t + 1) * H)
                        dve.wait_ge(S.sim_ready, i * TJ + t + 1 + START)
                        carry_wait()
                        for q in range(2):
                            for h in range(H):
                                m = dve.max(top[:, q, t * H + h, :], sim[:, t, q, h, :])
                        link(m)
                        settle(carry=True)
                        for q in range(2):
                            for h in range(H):
                                m = dve.max_index(idx[:, q, t * H + h, :], top[:, q, t * H + h, :], sim[:, t, q, h, :])
                        m.then_inc(S.top_ready, 1)
                        if t >= 2:
                            times_up(t - 2)
                        dve.wait_ge(S.top_ready, i * TJ + t + 1 + START)
                        link(dve.tensor_copy(idxb[:, :, of_tile, :], idx[:, :, of_tile, :]))
                        settle()
                        if t >= 2:
                            dve.wait_ge(S.digits_ready, i * 6 + t - 1 + START)
                        dve.tensor_tensor(hot_y[t % 2], spread(w.iota_lo[:], 1, H),
                                          spread(idxb[:, 1, of_tile], 2, NKEYS), ALU.is_equal).then_inc(S.hot_ready, 1)
                        if t >= 1:
                            rank_lo(t - 1)
                    dve.tensor_tensor(below[:], top[:], top[:, :, :, 0:1].to_broadcast([P, 2, G, KPH]),
                                      ALU.subtract).then_inc(S.below_ready, 1)
                    times_up(2)
                    link(dve.tensor_tensor(hot_x, spread(w.iota_lo[:, 0:NHI, :], 1, G), spread(idxb[:, 0], 2, NHI),
                                           ALU.is_equal))
                    rank_lo(TJ - 1)
                    dve.wait_ge(S.digits_ready, i * 6 + TJ + START)
                    link(dve.tensor_tensor(pair[:], spread(top[:, 0], 3, KPH), spread(top[:, 1], 2, KPH), ALU.add))
                    settle(carry=True)
                    flat = pair[:].rearrange("p g i j -> p g (i j)")
                    marked = picked[:].rearrange("p g i j -> p g (i j)")
                    for g in range(G):
                        m = dve.max(best[:, g, :], flat[:, g, :])
                    link(m)
                    times_up(3)
                    settle(carry=True)
                    for g in range(G):
                        m = dve.match_replace(marked[:, g, :], best[:, g, :], flat[:, g, :], -3.0e38)
                    link(m)
                    times_up(4)
                    settle()
                    link(dve.tensor_tensor(picked[:], picked[:], pair[:], ALU.not_equal))
                    settle()
                    dve.wait_ge(S.expo_ready, i + 1 + START)
                    link(dve.tensor_tensor(pair[:], picked[:], spread(expo[:, 1], 2, KPH), ALU.mult))
                    with nc.allow_low_precision(reason="whole numbers up to 8, exact in bf16"):
                        link(dve.tensor_reduce(countb[:], picked[:], AX.X, ALU.add))
                    settle()
                    link(dve.tensor_reduce(row_sum[:], pair[:], AX.X, ALU.add))
                    link(dve.tensor_tensor(hot_x, hot_x, spread(countb[:], 2, NHI), ALU.mult))
                    settle()
                    link(dve.tensor_tensor(row_sum[:], row_sum[:], expo[:, 0], ALU.mult))
                    times_up(5)
                    settle()
                    dve.tensor_reduce(total[:], row_sum[:], AX.X, ALU.add).then_inc(S.total_ready, 1)
                    link(dve.scalar_tensor_tensor(out=beyond[:], in0=idxb[:, 0], scalar=float(NHI), in1=row_sum[:],
                                                  op0=ALU.is_ge, op1=ALU.mult))
                    with nc.allow_low_precision(reason="whole numbers up to 8, exact in bf16"):
                        dve.tensor_reduce(digits[:].rearrange("p t h r -> p (t h) r")[:, :, 0:NHI], hot_x, AX.X,
                                          ALU.add).then_inc(S.digits_ready, 1)
                    dve.wait_ge(S.total_ready, i + 1 + START)
                    link(dve.reciprocal(inv_total[:], total[:]))
                    settle()
                    link(dve.tensor_reduce(over[:], beyond[:], AX.X, ALU.add))
                    times_up(6)
                    settle()
                    link(dve.tensor_tensor(over[:], over[:], inv_total[:], ALU.mult))
                    dve.wait_ge(S.ln_ready, i + 1 + START)
                    link(dve.tensor_tensor(offset[:], top[:, 0, :, 0], ln_total[:], ALU.add))
                    settle()
                    link(dve.tensor_reduce(scores[:, :, 0, R], over[:].rearrange("p (t h) -> p t h", h=H), AX.X, ALU.add))
                    dve.tensor_tensor(scores[:, :, :, 0:NHI], sim[:, :, 0, :, 0:NHI],
                                      spread(offset[:].rearrange("p (t h) -> p t h", h=H), 3, NHI),
                                      ALU.subtract).then_inc(S.digits_ready, 1)
                    times_up(7)
                    for h in range(H):
                        dve.wait_ge(S.turned_ready, i * (2 * H) + 2 * (h + 1) + START)
                        dve.tensor_tensor(scoreT[:, 1, h, :], bk[2 + h % 2][0:ROWS, :],
                                          scoreT[:, 0, h, :].bitcast(F32), ALU.subtract).then_inc(S.rest_ready, 1)
                    assert steps[0] == RANK_STEPS, steps

                    def mix(c):
                        both, last = E[:, c % 2, 0], c == FC - 1
                        dve.wait_ge(S.pool_sum, i * POOL_SUMS + 2 * c + 2 + last + START)
                        dve.tensor_tensor(both, both, E[:, c % 2, 2], ALU.add).then_inc(S.mix_step, 1)
                        if c >= 2:
                            dve.wait_ge(S.mix_used, i * FC + c - 1 + START)
                        dve.wait_ge(S.mix_step, i * FC + c + 1 + START)
                        dve.tensor_tensor(mixed[c % 2], both, reach[:, c, :], ALU.mult).then_inc(S.mix_ready, 1)

                    dve.wait_ge(S.mid_used, i * FC + FC + START)
                    for c in range(FC):
                        for h in range(H):
                            n = c * H + h
                            dve.wait_ge(S.E_ready, i * (FC * H) + n + 1 + START)
                            dve.scalar_tensor_tensor(out=E[:, c % 2, h], in0=rank_bank[n % 3], scalar=float(KPH),
                                                     in1=E[:, c % 2, h], op0=ALU.is_gt, op1=ALU.mult
                                                     ).then_inc(S.masked, 1)
                            if c >= 1 and h == 1:
                                mix(c - 1)
                        if not last:
                            if c == 3:
                                moments(i + 1)
                            if c == 4:
                                normalise(i + 1)
                    mix(FC - 1)
                    dve.wait_ge(S.mix_used, i * FC + FC + START)
                    xs = w.x[:, bass.ds(i * TJ, TJ), :].rearrange("p j c -> p (j c)")
                    dve.tensor_tensor(xs, acc[:], xs, ALU.add).then_inc(S.x_added, 1)

                moments(0)
                normalise(0)
                with dve.Fori(0, ROUNDS - 1) as i:
                    a_round(i, last=False)
                a_round(ROUNDS - 1, last=True)

            @block.gpsimd
            def _(pool):
                def deviations(r):
                    pool.wait_ge(S.xn_ready, r * TJ + START)
                    pool.wait_ge(S.mv_ready, r * TJ + TJ + START)
                    pool.tensor_tensor(rstd[:], mv[:, :, 1], w.eps[:, 0:TJ], ALU.add).then_inc(S.var_eps, 1)
                    pool.wait_ge(S.var_eps, r + 1 + START)
                    pool.tensor_tensor(rstd[:], rstd[:], w.minus_half[:, 0:TJ], ALU.pow).then_inc(S.rstd_ready, 1)

                def a_round(i, last):
                    for t in range(TJ):
                        pool.wait_ge(S.hot_ready, i * TJ + t + 1 + START)
                        pool.tensor_tensor(hot_y[t % 2], hot_y[t % 2], spread(w.rank_weight[:], 1, H), ALU.mult
                                           ).then_inc(S.hot_weighted, 1)
                    pool.wait_ge(S.turned_psum, i * H + START)
                    pool.tensor_tensor(scores[:, :, :, NHI:R], sim[:, :, 1],
                                       spread(top[:, 1, :, 0].rearrange("p (t h) -> p t h", h=H), 3, NKEYS),
                                       ALU.subtract).then_inc(S.second_ready, 1)
                    for c in range(FC):
                        for a in (0, 2):
                            pool.wait_ge(S.masked, i * (FC * H) + c * H + a + 2 + START)
                            pool.tensor_tensor(E[:, c % 2, a], E[:, c % 2, a], E[:, c % 2, a + 1], ALU.add
                                               ).then_inc(S.pool_sum, 1)
                        if c == 3 and not last:
                            deviations(i + 1)
                    pool.wait_ge(S.over_ready, i + 1 + START)
                    pool.wait_ge(S.pool_sum, i * POOL_SUMS + 2 * FC + START)
                    pool.tensor_tensor(E[:, (FC - 1) % 2, 2], E[:, (FC - 1) % 2, 2], over_row, ALU.add
                                       ).then_inc(S.pool_sum, 1)

                deviations(0)
                with pool.Fori(0, ROUNDS - 1) as i:
                    a_round(i, last=False)
                a_round(ROUNDS - 1, last=True)

            @block.tensor
            def _(pe):
                def turn_x(r):
                    pe.wait_ge(S.xn_ready, r * TJ + TJ + START)
                    pe.wait_ge(S.masked, r * (FC * H) + START)
                    for k in range(KC):
                        for j in range(TJ):
                            mm = pe.transpose(bk[k][:, j * P:(j + 1) * P], xn[:, j, k * P:(k + 1) * P], w.ident[:])
                    mm.then_inc(S.hT_psum, 1)

                def similarities(r, tiles):
                    for t in tiles:
                        if t == 0:
                            pe.wait_ge(S.hT_ready, r + 1 + START)
                        if t >= 2:
                            pe.wait_ge(S.sim_ready, r * TJ + t - 1 + START)
                        for k in range(KC):
                            mm = pe.matmul(bk[2 + t % 2], hT[:, k, t * P:(t + 1) * P], w.wsim[:, k, :],
                                           start=(k == 0), stop=(k == KC - 1))
                        mm.then_inc(S.sim_psum, 1)

                def a_round(i, last):
                    for c in range(FC):
                        if c >= 4:
                            pe.wait_ge(S.reach_ready, i * FC + c - 3 + START)
                        for k in range(KC):
                            mm = pe.matmul(bk[(4, 5, 0, 1)[c % 4]], w.deT[:, k, c * P:(c + 1) * P], hT[:, k, :],
                                           start=(k == 0), stop=(k == KC - 1))
                        mm.then_inc(S.w_psum, 1)
                    pe.wait_ge(S.x_added, i + START)
                    for n in range(2):
                        pe.matmul(acc[:, n * 512:(n + 1) * 512], w.ones3[:], bias(w, "bd", 2), start=True, stop=True)

                    def mlp_out(f):
                        pe.wait_ge(S.mid_ready, i * FC + f + 1 + START)
                        for j in range(TJ):
                            mm = pe.matmul(acc[:, j * C:(j + 1) * C], mid[:, f % 4, j * P:(j + 1) * P], w.wd[:, f, :],
                                           start=False, stop=True, skip_group_check=True)
                        mm.then_inc(S.mid_used, 1)

                    for f in range(FC):
                        if f < 2:
                            pe.wait_ge(S.reach_ready, i * FC + 6 + 2 * f + START)
                        else:
                            pe.wait_ge(S.mid_ready, i * FC + f - 1 + START)
                        g, u = (bk[4], bk[5]) if f % 2 == 0 else (bk[0], bk[1])
                        for out, weights in ((g, w.wg), (u, w.wu)):
                            for k in range(KC):
                                mm = pe.matmul(out, weights[:, k, f * P:(f + 1) * P], hT[:, k, :],
                                               start=(k == 0), stop=(k == KC - 1))
                        mm.then_inc(S.gu_psum, 1)
                        if f >= 1:
                            mlp_out(f - 1)

                    def turn_digits(h):
                        if h >= 2:
                            pe.wait_ge(S.rest_ready, i * H + h - 1 + START)
                        for t in range(TJ):
                            pe.transpose(bk[2 + h % 2][0:ROWS, t * P:(t + 1) * P], scores[:, t, h, :], w.ident[:])
                            mm = pe.transpose(bk[4 + h % 2].bitcast(BF16)[0:ROWS, t * P:(t + 1) * P],
                                              digits[:, t, h, :], w.identb[:])
                        mm.then_inc(S.turned_psum, 1)

                    pe.wait_ge(S.digits_ready, i * 6 + 6 + START)
                    pe.wait_ge(S.second_ready, i + 1 + START)
                    turn_digits(0)
                    turn_digits(1)
                    mlp_out(FC - 1)
                    turn_digits(2)
                    turn_digits(3)

                    def experts(c):
                        pe.wait_ge(S.mix_ready, i * FC + c + 1 + START)
                        for j in range(TJ):
                            mm = pe.matmul(acc[:, j * C:(j + 1) * C], mixed[c % 2][:, j * P:(j + 1) * P],
                                           w.ue[:, c, :], start=False, stop=True, skip_group_check=True)
                        mm.then_inc(S.mix_used, 1)

                    pe.wait_ge(S.rest_ready, i * H + H + START)
                    for part in range(2):
                        mm = pe.matmul(bk[0], w.selovf[:], scoreT[:, part, 0, :], start=(part == 0), stop=(part == 1))
                    mm.then_inc(S.over_psum, 1)
                    for c in range(FC):
                        for h in range(H):
                            n = c * H + h
                            if n == 2:
                                pe.wait_ge(S.over_ready, i + 1 + START)
                            if n >= 3:
                                pe.wait_ge(S.masked, i * (FC * H) + n - 2 + START)
                            pe.matmul(rank_bank[n % 3], w.selb[:, c].rearrange("r a e -> r (a e)"), digitsT[:, h, :],
                                      start=True, stop=True)
                            for part in range(2):
                                mm = pe.matmul(score_bank[n % 3], w.sel[:, c].rearrange("r a e -> r (a e)"),
                                               scoreT[:, part, h, :], start=(part == 0), stop=(part == 1))
                            mm.then_inc(S.ds_psum, 1)
                            if c >= 2 and h == 1:
                                experts(c - 2)
                    if not last:
                        turn_x(i + 1)
                    experts(FC - 2)
                    if not last:
                        similarities(i + 1, (0, 1))
                    experts(FC - 1)
                    if not last:
                        similarities(i + 1, (2, 3))

                turn_x(0)
                similarities(0, range(TJ))
                with pe.Fori(0, ROUNDS - 1) as i:
                    a_round(i, last=False)
                a_round(ROUNDS - 1, last=True)

            @block.scalar
            def _(act):
                def evacuate(r):
                    act.wait_ge(S.hT_psum, r + 1 + START)
                    act.activation(hT[:].rearrange("p k t -> p (k t)"), bk01[:], ACT.Copy).then_inc(S.hT_ready, 1)
                    act.activation(idle[:], w.eps[:, 0:1], ACT.Silu)
                    for t in range(TJ):
                        act.wait_ge(S.sim_psum, r * TJ + t + 1 + START)
                        act.activation(sim_row[:, t * 512:(t + 1) * 512], bk[2 + t % 2], ACT.Copy).then_inc(S.sim_ready, 1)

                def a_round(i, last):
                    act.wait_ge(S.mix_ready, i * FC + START)
                    for c in range(FC):
                        act.wait_ge(S.w_psum, i * FC + c + 1 + START)
                        act.activation(reach[:, c, :], bk[(4, 5, 0, 1)[c % 4]], ACT.Silu).then_inc(S.reach_ready, 1)

                    def gates(f):
                        act.wait_ge(S.gu_psum, i * FC + f + 1 + START)
                        if f >= 2:
                            act.wait_ge(S.mid_ready, i * FC + f - 1 + START)
                        act.activation(gate[:, f % 2, :], bk[4] if f % 2 == 0 else bk[0], ACT.Silu,
                                       bias=w.bg[:, f:f + 1]).then_inc(S.gate_ready, 1)

                    for f in range(3):
                        gates(f)
                    act.wait_ge(S.below_ready, i + 1 + START)
                    act.activation(expo[:], below[:], ACT.Exp).then_inc(S.expo_ready, 1)
                    for f in range(3, 7):
                        gates(f)
                    act.wait_ge(S.total_ready, i + 1 + START)
                    act.activation(ln_total[:], total[:], ACT.Ln).then_inc(S.ln_ready, 1)
                    gates(7)
                    for h in range(H):
                        act.wait_ge(S.turned_psum, i * H + h + 1 + START)
                        act.activation(digitsT[:, h, :], bk[4 + h % 2].bitcast(BF16)[0:ROWS, 0:T], ACT.Copy
                                       ).then_inc(S.turned_ready, 1)
                        act.activation(scoreT[:, 0, h, :], bk[2 + h % 2][0:ROWS, :], ACT.Copy
                                       ).then_inc(S.turned_ready, 1)
                    act.wait_ge(S.over_psum, i + 1 + START)
                    act.wait_ge(S.mid_used, i * FC + FC + START)
                    act.activation(over_row, bk[0], ACT.Copy).then_inc(S.over_ready, 1)
                    for c in range(FC):
                        if c >= 2:
                            act.wait_ge(S.mix_ready, i * FC + c - 1 + START)
                        for h in range(H):
                            n = c * H + h
                            act.wait_ge(S.ds_psum, i * (FC * H) + n + 1 + START)
                            act.activation(E[:, c % 2, h], score_bank[n % 3], ACT.Exp).then_inc(S.E_ready, 1)
                    if not last:
                        evacuate(i + 1)

                evacuate(0)
                with act.Fori(0, ROUNDS - 1) as i:
                    a_round(i, last=False)
                a_round(ROUNDS - 1, last=True)


class Turns:

    def __init__(self, order, readers, before, each, S):
        self.order, self.reader = order, readers
        self.before, self.each = before, each
        self.S = S

    def _count(self, names, engine):
        return len([n for n in names if self.reader[n[0]] == engine])

    def place(self, name):
        return (len(self.before) + self.order.index(name)) % 3

    def filled(self, i, name):
        return self.S.filled, i * len(self.each) + len(self.before) + self.order.index(name) + 1 + START

    def read(self, i, name):
        return self._read_to(i, self.order.index(name))

    def _read_to(self, i, at):
        if at >= 0:
            engine = self.reader[self.order[at][0]]
            extra = self._count(self.order[:at + 1], engine)
        else:
            past = self.each if self.each else self.order
            engine = self.reader[past[at][0]]
            extra = -self._count(past[len(past) + at + 1:], engine)
        signal = self.S.act_read if engine == "act" else self.S.dve_read
        return signal, i * self._count(self.each, engine) + self._count(self.before, engine) + extra + START

    def free(self, i, name):
        at = self.order.index(name) - 3
        if at < 0 and not self.before:
            return None
        return self._read_to(i, at)


def linear_attention(nc, w, sem):
    with ExitStack() as ctx:
        def tmp(name, shape, dt=F32):
            return ctx.enter_context(nc.sbuf_tensor(f"b_{name}", shape, dt))

        def psum(name, n):
            return ctx.enter_context(nc.psum_tensor(f"b_{name}", [P, n], F32))

        QH = 4
        GROUPS = HEADS // QH
        UNITS = 3 * GROUPS
        WIDTH = [512, 384, 384]
        BLOCKS = [[(0, 0)], [(1, 0)], [(2, 0), (3, 256)]]
        NG = 2 * HEADS
        HP = HEADS // 2
        VW = 2 * FEAT

        two = [psum(f"two{n}", 1024) for n in range(3)]
        yT, aux = psum("yT", 512), psum("aux", 512)

        stats, mv, rstd = tmp("stats", [P, TJ, 6]), tmp("mv", [P, TJ, 2]), tmp("rstd", [P, TJ])
        pause = tmp("pause", [P, 1])
        xn = tmp("xn", [P, TJ, C])
        hT = tmp("hT", [P, KC, T])
        qk = tmp("qk", [P, TJ, NG, FEAT])
        squares, rms = tmp("squares", [P, 2, NG, FEAT]), tmp("rms", [P, TJ, NG])
        mean = tmp("mean", [P, KC, NG])
        parts = [tmp("q_parts", [P, 2, HEADS, 4, FEAT]), tmp("k_parts", [P, 2, HEADS, 4, FEAT])]
        qkT = [tmp("qT", [P, HP, T], F32R), tmp("kT", [P, HP, T], F32R)]
        va = tmp("va", [P, TJ, HEADS, VW])
        U = [tmp(f"U{k}", [P, QH, WIDTH[k]]) for k in range(3)]
        y_heads = tmp("y_heads", [P, T])
        den, inv = tmp("den", [P, TJ, QH]), tmp("inv", [P, TJ, QH])

        S = w.attn_signals
        consts = sem("b_consts")

        readers = {"s": "act", "tq": "dve", "tk": "act", "x": "act", "v": "dve", "o": "act", "p": "dve"}
        turned = [(("tq", "tk")[m], t) for t in range(TJ) for m in range(2)]
        prepare = [("x", 0)] + turned + [("v", 0)]
        s = [("s", n) for n in range(2 * UNITS)]
        each = s[0:6] + [("x", 0)] + s[6:] + turned + [("v", 0), ("o", 0), ("p", 0)]
        assert len(each) % 3 == 0
        start = Turns(prepare, readers, [], [], S)
        steady = Turns(each, readers, prepare, each, S)
        final = Turns(s + [("o", 0), ("p", 0)], readers, prepare, each, S)

        def wide(turns, name):
            return two[turns.place(name)]

        with nc.Block() as block:
            @block.vector
            def _(dve):
                def moments(r):
                    for j in range(TJ):
                        dve.bn_stats(stats[:, j, :], w.x[:, bass.ds(r * TJ + j, 1), :]).then_inc(S.stats_ready, 1)
                    dve.wait_ge(S.stats_ready, r * TJ + TJ + START)
                    dve.memset(pause[:], 0.0)
                    for j in range(TJ):
                        dve.bn_aggr(mv[:, j, :], stats[:, j, :]).then_inc(S.mv_ready, 1)

                def normalise(r):
                    dve.wait_ge(S.rstd_ready, r + 1 + START)
                    for j in range(TJ):
                        dve.tensor_scalar(xn[:, j, :], w.x[:, bass.ds(r * TJ + j, 1), :], mv[:, j, 0:1],
                                          rstd[:, j:j + 1], ALU.subtract, ALU.mult).then_inc(S.xn_ready, 1)

                def variance(r, t):
                    dve.wait_ge(S.squared, r * TJ + t + 1 + START)
                    dve.tensor_reduce(rms[:, t, :], squares[:, t % 2], AX.X, ALU.add).then_inc(S.var_ready, 1)

                def features(r, t):
                    dve.wait_ge(S.rms_ready, r * TJ + t + 1 + START)
                    dve.wait_ge(S.qk_ready, r * TJ + t + 1 + START)
                    for n, (by, op) in enumerate(((spread(rms[:, t], 2, FEAT), ALU.mult), (spread(w.gamma[:], 1, NG), ALU.mult),
                                                  (spread(w.beta[:], 1, NG), ALU.add))):
                        if n >= 1:
                            dve.wait_ge(S.feat_step, (r * TJ + t) * 3 + n + START)
                        dve.tensor_tensor(qk[:, t], qk[:, t], by, op).then_inc(S.feat_step, 1)

                def lower_part(r, n):
                    t, m = n // 2, n % 2
                    dve.wait_ge(S.hi_ready, r * (2 * TJ) + n + 1 + START)
                    heads, part = qk[:, t, m * HEADS:(m + 1) * HEADS, :], parts[m][:, t % 2]
                    lo = part[:, :, 1:4:2, :] if m else part[:, :, 2:4, :]
                    dve.tensor_tensor(lo, spread(heads, 2, 2), spread(part[:, :, 0, :], 2, 2), ALU.subtract
                                      ).then_inc(S.lo_ready, 1)

                def turned_q(i, turns, t):
                    dve.wait_ge(*turns.filled(i, ("tq", t)))
                    dve.tensor_copy(qkT[0][:, :, t * P:(t + 1) * P],
                                    wide(turns, ("tq", t))[:].rearrange("p (g c) -> p g c", c=P)).then_inc(S.dve_read, 1)

                def values(i, turns):
                    dve.wait_ge(*turns.filled(i, ("v", 0)))
                    dve.tensor_copy(va[:, :, :, 0:FEAT], wide(turns, ("v", 0))[:].rearrange(
                        "p (t h f) -> p t h f", t=TJ, f=FEAT)).then_inc(S.dve_read, 1)

                def take_outputs(i, g):
                    dve.wait_ge(S.y_psum, i * UNITS + 3 * g + 3 + START)
                    dve.tensor_copy(y_heads[:], yT[:]).then_inc(S.y_copied, 1)

                def divide(i, g):
                    dve.wait_ge(S.y_turned, i * GROUPS + g + 1 + START)
                    y = aux[:].rearrange("p (t h f) -> p t h f", t=TJ, f=VW)
                    dve.tensor_scalar(den[:], y[:, :, :, FEAT], 1e-5, None, ALU.add).then_inc(S.den_step, 1)
                    dve.wait_ge(S.den_step, i * (2 * GROUPS) + 2 * g + 1 + START)
                    dve.reciprocal(inv[:], den[:]).then_inc(S.den_step, 1)
                    dve.wait_ge(S.den_step, i * (2 * GROUPS) + 2 * g + 2 + START)
                    out = xn[:].rearrange("p t (h f) -> p t h f", f=FEAT)[:, :, QH * g:QH * (g + 1), :]
                    dve.tensor_tensor(out, y[:, :, :, 0:FEAT], spread(inv[:], 3, FEAT), ALU.mult
                                      ).then_inc(S.y_ready, 1)

                def a_batch(i, turns, last):
                    for u in range(UNITS):
                        g, k = u // 3, u % 3
                        dve.wait_ge(*turns.read(i, ("s", 2 * u + 1)))
                        for _, at in BLOCKS[k]:
                            diagonal = U[k][:, :, at:at + P]
                            mask = dve.tensor_tensor(diagonal, diagonal, spread(w.tri[:], 1, QH), ALU.mult)
                        mask.then_inc(S.masked, 1)
                        if not last:
                            if u == 0:
                                moments(i + 1)
                            if u == 1:
                                normalise(i + 1)
                            if 4 <= u < 4 + TJ:
                                variance(i + 1, u - 4)
                            if u >= UNITS - 2:
                                features(i + 1, u - UNITS + 2)
                        if k == 0 and g >= 1:
                            take_outputs(i, g - 1)
                        if k == 1 and g >= 1:
                            if g == 1 and not last:
                                dve.wait_ge(*turns.filled(i, ("x", 0)))
                            divide(i, g - 1)
                    if not last:
                        lower_part(i + 1, 0)
                        lower_part(i + 1, 1)
                        take_outputs(i, GROUPS - 1)
                        for t in range(TJ):
                            if t == 1:
                                divide(i, GROUPS - 1)
                            if t + 2 < TJ:
                                features(i + 1, t + 2)
                            if t + 1 < TJ:
                                lower_part(i + 1, 2 * t + 2)
                                lower_part(i + 1, 2 * t + 3)
                            turned_q(i, turns, t)
                        values(i, turns)
                    else:
                        take_outputs(i, GROUPS - 1)
                        divide(i, GROUPS - 1)
                    dve.wait_ge(*turns.filled(i, ("p", 0)))
                    xs = w.x[:, bass.ds(i * TJ, TJ), :].rearrange("p j c -> p (j c)")
                    dve.tensor_tensor(xs, wide(turns, ("p", 0))[:], xs, ALU.add).then_inc(S.dve_read, 1)

                rows = w.wqk[:].rearrange("p k (g f) -> p k g f", f=FEAT)
                dve.tensor_reduce(mean[:], rows, AX.X, ALU.add).then_inc(consts, 1)
                dve.memset(va[:], 1.0).then_inc(consts, 1)
                dve.wait_ge(consts, 2)
                dve.scalar_tensor_tensor(out=rows, in0=spread(mean[:], 3, FEAT), scalar=-1.0 / FEAT, in1=rows,
                                         op0=ALU.mult, op1=ALU.add).then_inc(consts, 1)
                moments(0)
                normalise(0)
                for t in range(TJ):
                    variance(0, t)
                for t in range(TJ):
                    features(0, t)
                lower_part(0, 0)
                lower_part(0, 1)
                for t in range(TJ):
                    if t + 1 < TJ:
                        lower_part(0, 2 * t + 2)
                        lower_part(0, 2 * t + 3)
                    turned_q(0, start, t)
                values(0, start)
                with dve.Fori(0, B - 1) as i:
                    a_batch(i, steady, last=False)
                a_batch(B - 1, final, last=True)

            @block.gpsimd
            def _(pool):
                def deviations(r):
                    pool.wait_ge(S.xn_ready, r * TJ + START)
                    pool.wait_ge(S.mv_ready, r * TJ + TJ + START)
                    pool.tensor_tensor(rstd[:], mv[:, :, 1], w.eps[:, 0:TJ], ALU.add).then_inc(S.var_eps, 1)
                    pool.wait_ge(S.var_eps, r + 1 + START)
                    pool.tensor_tensor(rstd[:], rstd[:], w.minus_half[:, 0:TJ], ALU.pow).then_inc(S.rstd_ready, 1)

                def head_deviations(r, t):
                    pool.wait_ge(S.var_ready, r * TJ + t + 1 + START)
                    pool.tensor_tensor(rms[:, t], rms[:, t], w.eps[:, 0:NG], ALU.add).then_inc(S.rms_step, 1)
                    pool.wait_ge(S.rms_step, r * TJ + t + 1 + START)
                    pool.tensor_tensor(rms[:, t], rms[:, t], w.minus_half[:, 0:NG], ALU.pow).then_inc(S.rms_ready, 1)

                def a_batch(r):
                    deviations(r)
                    for t in range(TJ):
                        head_deviations(r, t)

                with pool.Fori(0, B) as r:
                    a_batch(r)

            @block.tensor
            def _(pe):
                def claim(i, turns, name):
                    free = turns.free(i, name)
                    if free is not None:
                        pe.wait_ge(*free)
                    return wide(turns, name)

                def turn(out):
                    for k in range(KC):
                        for j in range(TJ):
                            mm = pe.transpose(out[:, k * T + j * P:k * T + (j + 1) * P],
                                              xn[:, j, k * P:(k + 1) * P], w.ident[:])
                    mm.then_inc(S.filled, 1)

                def turn_x(i, turns, r):
                    pe.wait_ge(S.xn_ready, r * TJ + TJ + START)
                    turn(claim(i, turns, ("x", 0)))

                def queries_keys(r, t):
                    for k in range(KC):
                        mm = pe.matmul(aux[:], hT[:, k, t * P:(t + 1) * P], w.wqk[:, k, :],
                                       start=(k == 0), stop=(k == KC - 1))
                    mm.then_inc(S.qk_psum, 1)

                def turn_parts(i, turns, r, n):
                    t, m = n // 2, n % 2
                    out = claim(i, turns, turned[n])
                    pe.wait_ge(S.lo_ready, r * (2 * TJ) + n + 1 + START)
                    for hp in range(HP):
                        mm = pe.transpose(out[:, hp * P:(hp + 1) * P],
                                          parts[m][:, t % 2, 2 * hp:2 * hp + 2].rearrange("p h s f -> p (h s f)"), w.ident[:])
                    mm.then_inc(S.filled, 1)

                def values(i, turns):
                    out = claim(i, turns, ("v", 0))
                    for t in range(TJ):
                        for k in range(KC):
                            mm = pe.matmul(out[:, t * C:(t + 1) * C], hT[:, k, t * P:(t + 1) * P], w.wvb[:, k, :],
                                           start=(k == 0), stop=(k == KC - 1))
                    mm.then_inc(S.filled, 1)

                def scores(i, turns, u):
                    g, k = u // 3, u % 3
                    if u == 0:
                        pe.wait_ge(S.act_read, i * ACT_READS + 1 + TJ + START)
                        pe.wait_ge(S.dve_read, i * DVE_READS + TJ + 1 + START)
                    for q in range(2):
                        out = claim(i, turns, ("s", 2 * u + q))
                        for j in range(2):
                            h = QH * g + 2 * q + j
                            rows = slice(64 * (h % 2), 64 * (h % 2) + 64)
                            for b, (kb, at) in enumerate(BLOCKS[k]):
                                mm = pe.matmul(out[:, j * 512 + at:j * 512 + at + T - kb * P],
                                               qkT[1][rows, h // 2, kb * P:(kb + 1) * P],
                                               qkT[0][rows, h // 2, kb * P:T],
                                               start=(b == 0), stop=True, skip_group_check=(b > 0))
                        mm.then_inc(S.filled, 1)

                def outputs(i, u):
                    g, k = u // 3, u % 3
                    pe.wait_ge(S.masked, i * UNITS + u + 1 + START)
                    if k == 0:
                        pe.wait_ge(S.y_copied, i * GROUPS + g + START)
                    for kb, at in BLOCKS[k]:
                        for j in range(QH):
                            mm = pe.matmul(yT[32 * j:32 * j + 32, kb * P:T], va[:, kb, QH * g + j, :],
                                           U[k][:, j, at:at + T - kb * P], start=(kb == 0), stop=True,
                                           skip_group_check=(kb > 0))
                    mm.then_inc(S.y_psum, 1)

                def turn_outputs(i, g):
                    pe.wait_ge(S.y_copied, i * GROUPS + g + 1 + START)
                    for t in range(TJ):
                        mm = pe.transpose(aux[:, t * P:(t + 1) * P], y_heads[:, t * P:(t + 1) * P], w.ident[:])
                    mm.then_inc(S.y_turned, 1)

                def project(i, turns):
                    out = claim(i, turns, ("o", 0))
                    pe.wait_ge(S.y_ready, i * GROUPS + GROUPS + START)
                    turn(out)
                    out = claim(i, turns, ("p", 0))
                    pe.wait_ge(*turns.read(i, ("o", 0)))
                    for j in range(TJ):
                        for k in range(KC):
                            mm = pe.matmul(out[:, j * C:(j + 1) * C], hT[:, k, j * P:(j + 1) * P], w.wo[:, k, :],
                                           start=(k == 0), stop=(k == KC - 1))
                    mm.then_inc(S.filled, 1)

                def a_batch(i, turns, last):
                    scores(i, turns, 0)
                    for u in range(UNITS):
                        if u + 1 < UNITS:
                            scores(i, turns, u + 1)
                        outputs(i, u)
                        if u == 1 and not last:
                            turn_x(i, turns, i + 1)
                        if u % 3 == 0 and u > 0:
                            if not last:
                                pe.wait_ge(S.qk_ready, i * TJ + TJ + (1, TJ, TJ)[u // 3 - 1] + START)
                            pe.wait_ge(S.y_ready, i * GROUPS + u // 3 - 1 + START)
                            turn_outputs(i, u // 3 - 1)
                        if 2 <= u < 2 + TJ and not last:
                            if u == 2:
                                pe.wait_ge(*turns.read(i, ("x", 0)))
                            pe.wait_ge(S.qk_ready, i * TJ + TJ + u - 2 + START)
                            pe.wait_ge(S.y_ready, i * GROUPS + (0 if u == 2 else 1) + START)
                            queries_keys(i + 1, u - 2)
                    for n in range(0 if last else 2 * TJ):
                        turn_parts(i, turns, i + 1, n)
                        if n == 1:
                            pe.wait_ge(S.y_ready, i * GROUPS + GROUPS - 1 + START)
                            turn_outputs(i, GROUPS - 1)
                    if last:
                        pe.wait_ge(S.y_ready, i * GROUPS + GROUPS - 1 + START)
                        turn_outputs(i, GROUPS - 1)
                    else:
                        values(i, turns)
                    project(i, turns)

                ACT_READS = len([n for n in each if readers[n[0]] == "act"])
                DVE_READS = len(each) - ACT_READS
                turn_x(0, start, 0)
                pe.wait_ge(*start.read(0, ("x", 0)))
                pe.wait_ge(consts, 3)
                for t in range(TJ):
                    if t >= 1:
                        pe.wait_ge(S.qk_ready, t + START)
                    queries_keys(0, t)
                for n in range(2 * TJ):
                    turn_parts(0, start, 0, n)
                values(0, start)
                with pe.Fori(0, B - 1) as i:
                    a_batch(i, steady, last=False)
                a_batch(B - 1, final, last=True)

            @block.scalar
            def _(act):
                def to_hT(i, turns, name):
                    act.wait_ge(*turns.filled(i, name))
                    act.activation(hT[:].rearrange("p k t -> p (k t)"), wide(turns, name)[:], ACT.Copy
                                   ).then_inc(S.act_read, 1)

                def take_qk(r, t):
                    act.wait_ge(S.qk_psum, r * TJ + t + 1 + START)
                    act.wait_ge(S.var_ready, r * TJ + max(t - 1, 0) + START)
                    act.activation(squares[:, t % 2].rearrange("p g f -> p (g f)"), aux[:], ACT.Square, scale=0.25
                                   ).then_inc(S.squared, 1)
                    act.activation(qk[:, t].rearrange("p g f -> p (g f)"), aux[:], ACT.Copy).then_inc(S.qk_ready, 1)

                def upper_part(i, turns, r, n):
                    t, m = n // 2, n % 2
                    act.wait_ge(S.feat_step, (r * TJ + t + 1) * 3 + START)
                    if n >= 4:
                        act.wait_ge(*turns.filled(i, turned[n - 4]))
                    part = parts[m][:, t % 2].bitcast(F32R)
                    hi = part[:, :, 0:4:2, :] if m else part[:, :, 0:2, :]
                    heads = qk[:, t, m * HEADS:(m + 1) * HEADS, :]
                    act.activation(hi, spread(heads, 2, 2), ACT.Copy).then_inc(S.hi_ready, 1)

                def turned_k(i, turns, t):
                    act.wait_ge(*turns.filled(i, ("tk", t)))
                    act.activation(qkT[1][:, :, t * P:(t + 1) * P],
                                   wide(turns, ("tk", t))[:].rearrange("p (g c) -> p g c", c=P), ACT.Copy
                                   ).then_inc(S.act_read, 1)

                def all_parts(i, turns, r):
                    for n in range(2 * TJ):
                        upper_part(i, turns, r, n)
                        if n >= 3 and n % 2 == 1:
                            turned_k(i, turns, n // 2 - 1)
                    turned_k(i, turns, TJ - 1)

                def a_batch(i, turns, last):
                    for u in range(UNITS):
                        g, k = u // 3, u % 3
                        if u >= 3:
                            act.wait_ge(S.y_psum, i * UNITS + u - 2 + START)
                        for q in range(2):
                            act.wait_ge(*turns.filled(i, ("s", 2 * u + q)))
                            act.activation(U[k][:, 2 * q:2 * q + 2, :], wide(turns, ("s", 2 * u + q))[:].rearrange(
                                "p (h c) -> p h c", c=512)[:, :, 0:WIDTH[k]], ACT.Square, scale=0.25
                                ).then_inc(S.act_read, 1)
                        if u == 2 and not last:
                            to_hT(i, turns, ("x", 0))
                        if 3 <= u < 3 + TJ and not last:
                            take_qk(i + 1, u - 3)
                    if not last:
                        all_parts(i, turns, i + 1)
                    to_hT(i, turns, ("o", 0))

                to_hT(0, start, ("x", 0))
                for t in range(TJ):
                    take_qk(0, t)
                all_parts(0, start, 0)
                with act.Fori(0, B - 1) as i:
                    a_batch(i, steady, last=False)
                a_batch(B - 1, final, last=True)


def program(nc, io, phases=("a", "f1", "b", "f2")):
    with ExitStack() as ctx:
        def sb(name, shape, dt=F32):
            return ctx.enter_context(nc.sbuf_tensor(name, shape, dt))

        def sem(name):
            return ctx.enter_context(nc.semaphore(name))

        w = Named()
        w.x = sb("x", [P, B * TJ, C])
        w.ident, w.identb, w.tri = sb("ident", [P, P]), sb("identb", [P, P], BF16), sb("tri", [P, P])
        w.ones3, w.ones3b = sb("ones3", [3, P], BF16), sb("ones3b", [3, T], BF16)
        w.minus_half, w.eps = sb("minus_half", [P, 32]), sb("eps", [P, 32])
        w.iota_lo, w.rank_weight = sb("iota_lo", [P, NKEYS, KPH], BF16), sb("rank_weight", [P, NKEYS, KPH], BF16)
        w.sel, w.selb = sb("sel", [ROWS, FC, 2, NKEYS], F32R), sb("selb", [ROWS, FC, 2, NKEYS], BF16)
        w.selovf = sb("selovf", [ROWS, P], F32R)
        w.bias3 = sb("bias3", [3, NBIAS], BF16)
        w.wg, w.wu, w.wd = sb("wg", [P, KC, DCD]), sb("wu", [P, KC, DCD]), sb("wd", [P, FC, C])
        w.deT, w.ue, w.wsim = sb("deT", [P, KC, NEXP]), sb("ue", [P, FC, C]), sb("wsim", [P, KC, 2 * H * NKEYS])
        w.bg, w.bu = sb("bg", [P, FC]), sb("bu", [P, FC])
        w.wqk, w.wvb, w.wo = sb("wqk", [P, KC, 2 * C]), sb("wvb", [P, KC, C]), sb("wo", [P, KC, C])
        w.gamma, w.beta = sb("gamma", [P, FEAT]), sb("beta", [P, FEAT])

        w.scan_signals, w.attn_signals = ScanSignals(sem, "a"), AttnSignals(sem, "b")
        w.ffn_signals = {"f1": FfnSignals(sem, "f1"), "f2": FfnSignals(sem, "f2")}
        w.all_signals = (w.scan_signals.all + w.attn_signals.all + w.ffn_signals["f1"].all
                         + w.ffn_signals["f2"].all)
        w.x_loaded = [sem(f"x_loaded{b}") for b in range(B)]
        with ExitStack() as scan_ctx:
            def scan_sb(name, shape):
                return scan_ctx.enter_context(nc.sbuf_tensor(name, shape, F32))

            w.wv, w.gq, w.wproj = scan_sb("wv", [P, KC, C]), scan_sb("gq", [P, KC, P]), scan_sb("wproj", [P, KC, C])
            w.wz, w.gz = scan_sb("wz", [P, C]), scan_sb("gz", [P, P])
            setup(nc, w, io, sem)
            scan_attention(nc, w, sem)
        if "f1" in phases:
            experts_ffn(nc, w, sem, "f1")
        if "b" in phases:
            linear_attention(nc, w, sem)
        if "f2" in phases:
            experts_ffn(nc, w, sem, "f2")
        out_stored = sem("out_stored")
        with nc.Block() as block:
            @block.sync
            def _(sp):
                for b in range(B):
                    sp.dma_start(io.out[b].rearrange("(j p) c -> p j c", p=P),
                                 w.x[:, b * TJ:(b + 1) * TJ, :]).then_inc(out_stored, 16)
                sp.wait_ge(out_stored, 16 * B)


def arguments(args, out):
    io = Named()
    (io.x, io.attn_W, io.attn_b, io.freq_W, io.freq_b, io.out_W, io.out_b, io.proj_W, io.proj_b,
     io.identity, io.b_Wq, io.b_Wk, io.b_Wv, io.b_Wo, io.gamma, io.beta, io.Wg, io.bg, io.Wu, io.bu,
     io.Wd, io.bd, io.ffn_Wq, io.keys, io.down_embed, io.up_embed) = args
    io.out = out
    return io


_INPUTS = (
    "L0_attn_a_x",
    "L0_attn_a_attn_W",
    "L0_attn_a_attn_b",
    "L0_attn_a_freq_W",
    "L0_attn_a_freq_b",
    "L0_attn_a_out_W",
    "L0_attn_a_out_b",
    "L0_attn_a_proj_W",
    "L0_attn_a_proj_b",
    "L0_attn_a_identity",
    "L0_attn_b_Wq",
    "L0_attn_b_Wk",
    "L0_attn_b_Wv",
    "L0_attn_b_Wo",
    "L0_attn_b_gamma",
    "L0_attn_b_beta",
    "L0_ffn_Wg",
    "L0_ffn_bg",
    "L0_ffn_Wu",
    "L0_ffn_bu",
    "L0_ffn_Wd",
    "L0_ffn_bd",
    "L0_ffn_Wq",
    "L0_ffn_keys",
    "L0_ffn_down_embed",
    "L0_ffn_up_embed",
)


def kernel(**inputs):
    import numpy as _np
    import concourse.bacc as _bacc
    from concourse.bass_utils import run_bass_kernel_spmd as _run

    nc = _bacc.Bacc("TRN2", target_bir_lowering=False, num_devices=1)
    args, arrays = [], {}
    for name in _INPUTS:
        a = _np.ascontiguousarray(inputs[name])
        arrays[f"in_{name}"] = a
        args.append(nc.dram_tensor(f"in_{name}", a.shape, mybir.dt.from_np(a.dtype), kind="ExternalInput").ap())
    out = nc.dram_tensor("out_x", (B, T, C), F32, kind="ExternalOutput").ap()
    program(nc, arguments(args, out))
    return _run(nc, [arrays], core_ids=[0]).results[0]["out_x"]
```

```python
from contextlib import ExitStack
import math

import concourse.bass as bass
from concourse import mybir

F32 = mybir.dt.float32
F32R = mybir.dt.float32r
BF16 = mybir.dt.bfloat16
U32 = mybir.dt.uint32
ACT = mybir.ActivationFunctionType
ALU = mybir.AluOpType
AX = mybir.AxisListType

P = 128
B, T, C = 8, 512, 256
KC = C // P
TJ = T // P
NF = 64
SHIFTS = [1 << s for s in range(9)]
TURN = 2.0 * math.pi
SIN_SCALE = 6.2831850
MAGIC = 1.5 * 2.0 ** 23
DCD, NEXP, H, NKEYS, KPH = 1024, 1024, 4, 64, 8
FC = DCD // P
NHI = NEXP // NKEYS
ROWS = 96
HEADS, FEAT = 16, 16
LN_EPS = 1e-5

BIAS = {}
_at = 0
for _name, _n in (("v", C), ("z", C), ("proj", C), ("bd", C), ("f", P), ("gq", P), ("gz", P), ("id", P)):
    BIAS[_name] = (_at, _at + _n)
    _at += _n
NBIAS = _at
NGIVEN = BIAS["f"][1]

START = 1


class Named:
    pass


class ScanSignals:
    def __init__(self, sem, tag):
        self.all = [sem(f"{tag}_{n}") for n in (
            "stats_ready mv_ready var_eps rstd_ready xn_ready xT_psum xT_ready z_psum v_ready gs_ready "
            "f_psum whole_ready turns_ready wave_ready peak_ready peak_eps scale_ready y_ready y_psum "
            "proj_psum x_added "
        ).split()]
        (self.stats_ready, self.mv_ready, self.var_eps, self.rstd_ready, self.xn_ready, self.xT_psum,
         self.xT_ready, self.z_psum, self.v_ready, self.gs_ready, self.f_psum, self.whole_ready,
         self.turns_ready, self.wave_ready, self.peak_ready, self.peak_eps, self.scale_ready, self.y_ready,
         self.y_psum, self.proj_psum, self.x_added) = self.all


class FfnSignals:
    def __init__(self, sem, tag):
        self.all = [sem(f"{tag}_{n}") for n in (
            "stats_ready mv_ready var_eps rstd_ready xn_ready hT_psum hT_ready sim_psum sim_ready "
            "gu_psum gate_ready mid_ready w_psum reach_ready rank_step below_ready expo_ready "
            "total_ready ln_ready digits_ready turned_psum turned_ready ds_psum E_ready masked pool_sum "
            "mix_ready mix_used over_psum x_added mix_step top_ready hot_ready hot_weighted second_ready rest_ready mid_used over_ready tree_step hT_rest "
        ).split()]
        (self.stats_ready, self.mv_ready, self.var_eps, self.rstd_ready, self.xn_ready, self.hT_psum,
         self.hT_ready, self.sim_psum, self.sim_ready, self.gu_psum, self.gate_ready, self.mid_ready,
         self.w_psum, self.reach_ready, self.rank_step, self.below_ready, self.expo_ready, self.total_ready,
         self.ln_ready, self.digits_ready, self.turned_psum, self.turned_ready, self.ds_psum, self.E_ready,
         self.masked, self.pool_sum, self.mix_ready, self.mix_used, self.over_psum, self.x_added,
         self.mix_step, self.top_ready, self.hot_ready, self.hot_weighted,
         self.second_ready, self.rest_ready, self.mid_used, self.over_ready,
         self.tree_step, self.hT_rest) = self.all


class AttnSignals:
    def __init__(self, sem, tag):
        self.all = [sem(f"{tag}_{n}") for n in (
            "stats_ready mv_ready var_eps rstd_ready xn_ready qk_psum qk_ready squared var_ready "
            "head_dev rms_step scaled gamma_step feat_ready hi_ready lo_q_ready lo_k_ready filled act_read dve_read masked "
            "y_psum y_copied y_turned den_step y_ready "
        ).split()]
        (self.stats_ready, self.mv_ready, self.var_eps, self.rstd_ready, self.xn_ready, self.qk_psum,
         self.qk_ready, self.squared, self.var_ready, self.head_dev, self.rms_step, self.scaled,
         self.gamma_step, self.feat_ready,
         self.hi_ready, self.lo_q_ready, self.lo_k_ready, self.filled, self.act_read, self.dve_read, self.masked,
         self.y_psum, self.y_copied, self.y_turned, self.den_step,
         self.y_ready) = self.all


def spread(ap, axis, n):
    out = ap.unsqueeze(axis)
    shape = list(out.shape)
    shape[axis] = n
    return out.to_broadcast(shape)


def setup(nc, w, io, sem):
    with ExitStack() as ctx:
        def tmp(name, shape, dt=F32):
            return ctx.enter_context(nc.sbuf_tensor(name, shape, dt))

        bank = [ctx.enter_context(nc.psum_tensor(f"setup_bank{i}", [P, 512], F32)) for i in range(4)]
        loaded = sem("loaded")
        ident_ready = sem("ident_ready")
        steps = sem("pool_steps")
        job_done, job_out = sem("job_done"), sem("job_out")
        rows_loaded, upper_made = sem("rows_loaded"), sem("upper_made")
        bias_cleared, bias_moved = sem("bias_cleared"), sem("bias_moved")

        sel0, selovf0 = tmp("sel0", [ROWS, FC, 2, NKEYS]), tmp("selovf0", [ROWS, P])
        outw = tmp("outw", [P, C])
        freqw = tmp("freqw", [P, 4, NF])
        attnw = tmp("attnw", [P, KC, 2 * C])
        outwT = tmp("outwT", [P, KC, P])
        attnqT = tmp("attnqT", [P, KC, C])
        bq_col, bo_col, id_col = tmp("bq_col", [P, KC]), tmp("bo_col", [P, KC]), tmp("id_col", [P, KC])
        ffq = tmp("ffq", [P, KC, H, 2, NKEYS])
        ffqT = tmp("ffqT", [P, H, C])
        keys = tmp("keys_rows", [P, 2, P])
        keysT = tmp("keysT", [P, 2, P])
        de = tmp("de_rows", [P, FC, C])
        wrow = tmp("wrow", [P, 4, 2, C])
        brow = tmp("brow", [1, NBIAS])
        rest = tmp("rest", [1, NBIAS])
        parts = tmp("parts", [1, 3, NBIAS], BF16)
        fq_row = tmp("fq_row", [1, NF])

        bias_rows = [
            (brow[0:1, BIAS["v"][0]:BIAS["v"][1]], io.attn_b[C:2 * C].unsqueeze(0)),
            (brow[0:1, BIAS["z"][0]:BIAS["z"][1]], io.out_b.unsqueeze(0)),
            (brow[0:1, BIAS["proj"][0]:BIAS["proj"][1]], io.proj_b.unsqueeze(0)),
            (brow[0:1, BIAS["bd"][0]:BIAS["bd"][1]], io.bd.unsqueeze(0)),
            (fq_row[:], io.freq_b.unsqueeze(0)),
        ]
        loads = [
            (outw[:], io.out_W), (freqw[:], io.freq_W.rearrange("(k p) n -> p k n", p=P)),
            (attnw[:], io.attn_W.rearrange("(k p) n -> p k n", p=P)),
            (bq_col[:], io.attn_b[0:C].rearrange("(k p) -> p k", p=P)),
            (bo_col[:], io.out_b.rearrange("(k p) -> p k", p=P)),
            (id_col[:], io.identity.rearrange("(k p) -> p k", p=P)),
            (w.wz[:], io.out_W), (w.wproj[:], io.proj_W.rearrange("(k p) n -> p k n", p=P)),
            (w.wv[:], io.attn_W[:, C:2 * C].rearrange("(k p) n -> p k n", p=P)),
            (keys[:], io.keys.rearrange("(a b) k q n -> (b k) a (q n)", a=2)),
            (de[:], io.down_embed.rearrange("(e p) c -> p e c", p=P)),
            (w.ue[:], io.up_embed.rearrange("(e p) c -> p e c", p=P)),
            (w.wd[:], io.Wd.rearrange("(f p) n -> p f n", p=P)),
            (w.bg[:], io.bg.rearrange("(f p) -> p f", p=P)),
            (w.bu[:], io.bu.rearrange("(f p) -> p f", p=P)),
            (w.gamma[:], io.gamma.partition_broadcast(P)),
            (w.beta[:], io.beta.partition_broadcast(P)),
        ]
        for k in range(KC):
            for q in range(2):
                loads.append((ffq[:, k, :, q, :], io.ffn_Wq[k * P:(k + 1) * P, q * C:(q + 1) * C]
                              .rearrange("p (h n) -> p h n", h=H)))
        for m, src in enumerate((io.b_Wq, io.b_Wk, io.b_Wv, io.b_Wo)):
            loads.append((wrow[:, m], src.rearrange("(r p) c -> p r c", p=P)))

        deT, wsim = tmp("deT32", [P, KC, NEXP]), tmp("wsim32", [P, KC, 2 * H * NKEYS])

        jobs = []

        def turned(src, dst):
            jobs.append(([(src, None)], P, dst, 1.0))

        for k in range(KC):
            turned(outw[:, k * P:(k + 1) * P], outwT[:, k, :])
            for r in range(KC):
                turned(attnw[:, r, k * P:(k + 1) * P], attnqT[:, k, r * P:(r + 1) * P])
            for h in range(H):
                turned(ffq[:, k, h].rearrange("p q n -> p (q n)"), ffqT[:, h, k * P:(k + 1) * P])
            turned(keys[:, k, :], keysT[:, k, :])
            for e in range(FC):
                turned(de[:, e, k * P:(k + 1) * P], deT[:, k, e * P:(e + 1) * P])
            for r in range(2):
                turned(wrow[:, 0, r, k * P:(k + 1) * P], w.wqk[:, k, r * P:(r + 1) * P])
                turned(wrow[:, 1, r, k * P:(k + 1) * P], w.wqk[:, k, C + r * P:C + (r + 1) * P])
                turned(wrow[:, 2, r, k * P:(k + 1) * P], w.wvb[:, k, r * P:(r + 1) * P])
                turned(wrow[:, 3, r, k * P:(k + 1) * P], w.wo[:, k, r * P:(r + 1) * P])
        transposes = len(jobs)
        for half in range(2):
            fw = [freqw[:, 2 * half + k, :] for k in range(KC)]
            cols = slice(half * NF, (half + 1) * NF)
            jobs.append(([(outwT[:, k, :], fw[k]) for k in range(KC)], P, w.gz[:, cols], 1.0 / TURN))
            for r in range(KC):
                jobs.append(([(attnqT[:, k, r * P:(r + 1) * P], fw[k]) for k in range(KC)],
                             P, w.gq[:, r, cols], 1.0 / TURN))
            for name, col in (("gz", bo_col), ("gq", bq_col)):
                at = BIAS[name][0] + half * NF
                jobs.append(([(col[:, k:k + 1], fw[k]) for k in range(KC)], 1, brow[0:1, at:at + NF], 1.0 / TURN))
            if half == 0:
                for d in range(2):
                    at = BIAS["id"][0] + d * NF
                    jobs.append(([(id_col[:, k:k + 1], fw[k]) for k in range(KC)], 1,
                                 brow[0:1, at:at + NF], 1.0 / TURN))
        for q in range(2):
            for h in range(H):
                rows = slice(q * NKEYS, (q + 1) * NKEYS)
                for k in range(KC):
                    jobs.append(([(ffqT[rows, h, k * P:(k + 1) * P],
                                   keysT[rows, h // 2, (h % 2) * NKEYS:(h % 2 + 1) * NKEYS])],
                                 P, wsim[:, k, (q * H + h) * NKEYS:(q * H + h + 1) * NKEYS], 1.0))

        chain = sem("bias_chain")

        with nc.Block() as block:
            @block.sync
            def _(sp):
                for dst, src in bias_rows:
                    sp.dma_start(dst, src).then_inc(rows_loaded, 16)
                for dst, src in loads:
                    sp.dma_start(dst, src, allow_slow_non_contiguous=True).then_inc(loaded, 16)
                for b in range(B):
                    sp.dma_start(w.x[:, b * TJ:(b + 1) * TJ, :],
                                 io.x[b].rearrange("(j p) c -> p j c", p=P)).then_inc(w.x_loaded[b], 16)
                for signal in w.all_signals:
                    sp.sem_inc(signal, START)
                sp.wait_ge(chain, 12)
                sp.wait_ge(bias_cleared, 1)
                sp.dma_start(w.bias3[0:3, :], parts[:]).then_inc(bias_moved, 16)
                sp.wait_ge(bias_moved, 16)

            @block.gpsimd
            def _(pool):
                pool.memset(w.ident[:], 0.0).then_inc(steps, 1)
                pool.memset(w.tri[:], 1.0).then_inc(steps, 1)
                pool.memset(w.bias3[:], 0.0).then_inc(bias_cleared, 1)
                pool.memset(w.ones3[:], 1.0)
                pool.memset(w.ones3b[:], 1.0)
                pool.memset(w.minus_half[:], -0.5)
                pool.memset(w.eps[:], LN_EPS)
                pool.memset(sel0[:], 0.0).then_inc(steps, 1)
                pool.memset(selovf0[:], 0.0).then_inc(steps, 1)
                pool.iota(w.iota_lo[:], pattern=[[1, NKEYS], [0, KPH]], base=0, channel_multiplier=0,
                          allow_small_or_imprecise_dtypes=True)
                pool.iota(w.rank_weight[:], pattern=[[0, NKEYS], [-1, KPH]], base=KPH, channel_multiplier=0,
                          allow_small_or_imprecise_dtypes=True)
                pool.wait_ge(steps, 1)
                pool.affine_select(out=w.ident[:], in_=w.ident[:], compare_op=ALU.not_equal, fill=1.0, base=0,
                                   pattern=[[-1, P]], channel_multiplier=1).then_inc(ident_ready, 1)
                pool.wait_ge(ident_ready, 1)
                pool.tensor_copy(w.identb[:], w.ident[:])
                pool.wait_ge(steps, 2)
                pool.affine_select(out=w.tri[:], in_=w.tri[:], compare_op=ALU.is_ge, fill=0.0, base=0,
                                   pattern=[[1, P]], channel_multiplier=-1)
                pool.wait_ge(steps, 4)
                pool.affine_select(out=sel0[:], in_=sel0[:], compare_op=ALU.not_equal, fill=1.0,
                                   base=0, pattern=[[-2, FC], [-1, 2], [0, NKEYS]],
                                   channel_multiplier=1).then_inc(steps, 1)
                pool.wait_ge(steps, 5)
                pool.affine_select(out=sel0[:], in_=sel0[:], compare_op=ALU.not_equal, fill=1.0,
                                   base=-NHI, pattern=[[0, FC], [0, 2], [-1, NKEYS]],
                                   channel_multiplier=1).then_inc(steps, 1)
                pool.affine_select(out=selovf0[:, P - 1:P], in_=selovf0[:, P - 1:P], compare_op=ALU.not_equal,
                                   fill=1.0, base=-(NHI + NKEYS), pattern=[[0, 1]], channel_multiplier=1
                                   ).then_inc(steps, 1)
                for n, (split, whole) in enumerate(((w.deT, deT), (w.wsim, wsim))):
                    pool.wait_ge(upper_made, n + 1)
                    pool.tensor_tensor(split[:, 1], whole[:], split[:, 0].bitcast(F32), ALU.subtract)

            @block.tensor
            def _(pe):
                pe.wait_ge(loaded, 16 * len(loads))
                pe.wait_ge(ident_ready, 1)
                for n, (products, m, dst, scale) in enumerate(jobs):
                    if n >= 4:
                        pe.wait_ge(job_out, n - 3)
                    width = products[0][1].shape[-1] if products[0][1] is not None else P
                    out = bank[n % 4][0:m, 0:width]
                    if products[0][1] is None:
                        pe.transpose(out, products[0][0], w.ident[:]).then_inc(job_done, 1)
                        turned_last = n
                        continue
                    if n == turned_last + 1:
                        pe.wait_ge(job_out, n)
                    for k, (lhsT, rhs) in enumerate(products):
                        mm = pe.matmul(out, lhsT, rhs, start=(k == 0), stop=(k == len(products) - 1))
                    mm.then_inc(job_done, 1)

            @block.scalar
            def _(act):
                act.wait_ge(steps, 7)
                act.activation(w.sel[:], sel0[:], ACT.Copy)
                act.activation(w.selb[:], sel0[:], ACT.Copy)
                act.activation(w.selovf[:], selovf0[:], ACT.Copy)
                for split, whole, made in ((w.deT, deT, transposes), (w.wsim, wsim, len(jobs))):
                    act.wait_ge(job_out, made)
                    act.activation(split[:, 0], whole[:], ACT.Copy).then_inc(upper_made, 1)

            @block.vector
            def _(dve):
                def split_biases(cols, nth):
                    at, b, r = 5 * nth + 2, brow[0:1, cols], rest[0:1, cols]
                    dve.tensor_copy(parts[0:1, 0, cols], b).then_inc(chain, 1)
                    dve.wait_ge(chain, at + 1)
                    dve.tensor_tensor(r, b, parts[0:1, 0, cols], ALU.subtract).then_inc(chain, 1)
                    dve.wait_ge(chain, at + 2)
                    dve.tensor_copy(parts[0:1, 1, cols], r).then_inc(chain, 1)
                    dve.wait_ge(chain, at + 3)
                    dve.tensor_tensor(b, r, parts[0:1, 1, cols], ALU.subtract).then_inc(chain, 1)
                    dve.wait_ge(chain, at + 4)
                    dve.tensor_copy(parts[0:1, 2, cols], b).then_inc(chain, 1)

                f0 = BIAS["f"][0]
                dve.wait_ge(rows_loaded, 16 * len(bias_rows))
                dve.tensor_scalar(brow[0:1, f0:f0 + NF], fq_row[:], 1.0 / TURN, None, ALU.mult).then_inc(chain, 1)
                dve.tensor_scalar(brow[0:1, f0 + NF:f0 + 2 * NF], fq_row[:], 1.0 / TURN, 0.25,
                                  ALU.mult, ALU.add).then_inc(chain, 1)
                dve.wait_ge(chain, 2)
                split_biases(slice(0, NGIVEN), 0)
                for n, (products, m, dst, scale) in enumerate(jobs):
                    width = products[0][1].shape[-1] if products[0][1] is not None else P
                    dve.wait_ge(job_done, n + 1)
                    src = bank[n % 4][0:m, 0:width]
                    if scale == 1.0:
                        dve.tensor_copy(dst, src).then_inc(job_out, 1)
                    else:
                        dve.tensor_scalar(dst, src, scale, None, ALU.mult).then_inc(job_out, 1)
                dve.wait_ge(job_out, len(jobs))
                split_biases(slice(NGIVEN, NBIAS), 1)


def bias(w, name, times=1):
    a, b = BIAS[name]
    return spread(w.bias3[:, a:b], 1, times) if times > 1 else w.bias3[:, a:b]


def scan_attention(nc, w, sem):
    with ExitStack() as ctx:
        def tmp(name, shape, dt=F32):
            return [ctx.enter_context(nc.sbuf_tensor(f"{name}{lane}", shape, dt)) for lane in range(2)]

        def psum(name, n):
            return [ctx.enter_context(nc.psum_tensor(f"{name}{lane}", [P, n], F32)) for lane in range(2)]

        zb, gb, fb = psum("zb", 4 * C), psum("gb", 4 * P), psum("fb", T)
        stats, mv, rstd = tmp("a_stats", [P, TJ, 6]), tmp("a_mv", [P, TJ, 2]), tmp("a_rstd", [P, TJ])
        xn = tmp("a_xn", [P, TJ, C])
        y = tmp("a_y", [P, TJ, C])
        xT = tmp("a_xT", [P, KC, T])
        v = tmp("a_v", [P, TJ, C])
        gs = tmp("a_gs", [P, 2 * TJ, 2, NF])
        whole, turns, wave = tmp("a_whole", [P, T]), tmp("a_turns", [P, T]), tmp("a_wave", [P, T])
        pause, idle = tmp("a_pause", [P, 1]), tmp("a_idle", [P, 1])
        peak, scale = tmp("a_peak", [P, TJ]), tmp("a_scale", [P, TJ, 2])

        S = w.scan_signals
        NS = len(SHIFTS)
        ROUNDS = B // 2

        def twice(g):
            return spread(g[:].rearrange("p (q n) -> p q n", n=NF), 2, 2)

        def nth(i, per_lane, k, lane):
            return i * (2 * per_lane) + 2 * k + lane + 1

        def halves(i, s, lane, half):
            return i * (4 * (NS + 1)) + 4 * s + 2 * lane + half + 1

        with nc.Block() as block:
            @block.vector
            def _(dve):
                for b in range(B):
                    dve.wait_ge(w.x_loaded[b], 16)

                def moments(r):
                    for l in range(2):
                        for j in range(TJ):
                            dve.bn_stats(stats[l][:, j, :], w.x[:, bass.ds(r * 2 * TJ + l * TJ + j, 1), :]
                                         ).then_inc(S.stats_ready, 1)
                        dve.wait_ge(S.stats_ready, r * (2 * TJ) + (l + 1) * TJ + START)
                        dve.memset(pause[l][:], 0.0)
                        for j in range(TJ):
                            dve.bn_aggr(mv[l][:, j, :], stats[l][:, j, :]).then_inc(S.mv_ready, 1)

                def normalise(r):
                    for l in range(2):
                        dve.wait_ge(S.rstd_ready, nth(r, 1, 0, l) + START)
                        for j in range(TJ):
                            dve.tensor_scalar(xn[l][:, j, :], w.x[:, bass.ds(r * 2 * TJ + l * TJ + j, 1), :],
                                              mv[l][:, j, 0:1], rstd[l][:, j:j + 1],
                                              ALU.subtract, ALU.mult).then_inc(S.xn_ready, 1)

                def a_round(i, last):
                    for l in range(2):
                        dve.wait_ge(S.z_psum, halves(i, 0, l, 1) + START)
                        dve.tensor_copy(gs[l][:], twice(gb[l])).then_inc(S.gs_ready, 1)
                    for s in range(NS):
                        for l in range(2):
                            dve.wait_ge(S.whole_ready, nth(i, NS, s, l) + START)
                            dve.scalar_tensor_tensor(out=turns[l][:], in0=whole[l][:], scalar=MAGIC, in1=fb[l][:],
                                                     op0=ALU.subtract, op1=ALU.subtract).then_inc(S.turns_ready, 1)
                        for l in range(2):
                            for half in range(2):
                                tiles = slice(half * TJ // 2, (half + 1) * TJ // 2)
                                dve.wait_ge(S.z_psum, halves(i, s + 1, l, half) + START)
                                dve.tensor_reduce(peak[l][:, tiles], zb[l][:].rearrange("p (j c) -> p j c", c=C)[:, tiles],
                                                  AX.X, ALU.max, apply_absolute_value=True).then_inc(S.peak_ready, 1)
                            dve.wait_ge(S.peak_ready, i * (4 * NS) + 4 * s + 2 * l + 2 + START)
                            dve.tensor_scalar(peak[l][:], peak[l][:], 1e-6, None, ALU.add).then_inc(S.peak_eps, 1)
                            dve.wait_ge(S.peak_eps, nth(i, NS, s, l) + START)
                            dve.reciprocal(scale[l][:], spread(peak[l][:], 2, 2)).then_inc(S.scale_ready, 1)
                            dve.wait_ge(S.scale_ready, nth(i, NS, s, l) + START)
                            if s < NS - 1:
                                by = spread(spread(scale[l][:].rearrange("p j q -> p (j q)"), 2, 2), 3, NF)
                                dve.tensor_tensor(gs[l][:], twice(gb[l]), by, ALU.mult).then_inc(S.gs_ready, 1)
                            else:
                                dve.wait_ge(S.v_ready, nth(i, 1, 0, l) + START)
                                for j in range(TJ):
                                    dve.scalar_tensor_tensor(out=y[l][:, j, :], in0=zb[l][:, j * C:(j + 1) * C],
                                                             scalar=scale[l][:, j, 0:1], in1=v[l][:, j, :],
                                                             op0=ALU.mult, op1=ALU.mult).then_inc(S.y_ready, 1)
                        if not last and s == 2:
                            moments(i + 1)
                        if not last and s == 4:
                            normalise(i + 1)
                    for l in range(2):
                        dve.wait_ge(S.proj_psum, nth(i, 1, 0, l) + START)
                        xs = w.x[:, bass.ds((i * 2 + l) * TJ, TJ), :].rearrange("p j c -> p (j c)")
                        dve.tensor_tensor(xs, zb[l][:], xs, ALU.add).then_inc(S.x_added, 1)

                moments(0)
                normalise(0)
                with dve.Fori(0, ROUNDS - 1) as i:
                    a_round(i, last=False)
                a_round(ROUNDS - 1, last=True)

            @block.gpsimd
            def _(pool):
                with pool.Fori(0, ROUNDS) as i:
                    for l in range(2):
                        pool.wait_ge(S.mv_ready, i * (2 * TJ) + (l + 1) * TJ + START)
                        pool.wait_ge(S.xn_ready, i * (2 * TJ) + START)
                        pool.tensor_tensor(rstd[l][:], mv[l][:, :, 1], w.eps[:, 0:TJ], ALU.add).then_inc(S.var_eps, 1)
                        pool.wait_ge(S.var_eps, nth(i, 1, 0, l) + START)
                        pool.tensor_tensor(rstd[l][:], rstd[l][:], w.minus_half[:, 0:TJ], ALU.pow
                                           ).then_inc(S.rstd_ready, 1)

            @block.tensor
            def _(pe):
                def turn_to(l, src, out):
                    for k in range(KC):
                        for j in range(TJ):
                            mm = pe.transpose(out[:, k * T + j * P:k * T + (j + 1) * P],
                                              src[:, j, k * P:(k + 1) * P], w.ident[:])
                    return mm

                def token_biases(l, bz, bg):
                    for n in range(2):
                        pe.matmul(zb[l][:, n * T:(n + 1) * T], w.ones3[:], bias(w, bz, 2), start=True, stop=True)
                    if bg is not None:
                        pe.matmul(gb[l][:], w.ones3[:], bias(w, bg, TJ), start=True, stop=True)

                def tokens(l, lhsT, rz, rg, done):
                    for j in range(TJ):
                        for out, n, r in ((gb[l], P, rg), (zb[l], C, rz)):
                            for k, a in enumerate(lhsT if r is not None else []):
                                mm = pe.matmul(out[:, j * n:(j + 1) * n], a[:, j * P:(j + 1) * P], r[k],
                                               start=False, stop=k == len(lhsT) - 1, skip_group_check=True)
                        if done is not None and j % (TJ // 2) == TJ // 2 - 1:
                            mm.then_inc(done, 1)
                    return mm

                with pe.Fori(0, ROUNDS) as i:
                    for l in range(2):
                        pe.wait_ge(S.xn_ready, i * (2 * TJ) + (l + 1) * TJ + START)
                        pe.wait_ge(S.x_added, i * 2 + START)
                        turn_to(l, xn[l], zb[l]).then_inc(S.xT_psum, 1)
                    for l in range(2):
                        pe.wait_ge(S.xT_ready, nth(i, 2, 0, l) + START)
                        token_biases(l, "v", "gq")
                        tokens(l, [xT[l][:, k, :] for k in range(KC)], [w.wv[:, k, :] for k in range(KC)],
                               [w.gq[:, k, :] for k in range(KC)], S.z_psum)
                    for s, n in enumerate(SHIFTS):
                        for l in range(2):
                            pe.matmul(fb[l][:], bias(w, "f"), w.ones3b[:], start=True, stop=True)
                            pe.matmul(fb[l][:, 0:n], bias(w, "id"), w.ones3b[:, 0:n], start=False, stop=False,
                                      skip_group_check=True)
                            pe.wait_ge(S.gs_ready, nth(i, NS, s, l) + START)
                            for j in range(TJ):
                                width = min(P, T - j * P - n)
                                if width > 0:
                                    prev = gs[l][:, 2 * j].rearrange("p d n -> p (d n)")
                                    pe.matmul(fb[l][:, j * P + n:j * P + n + width], prev, w.ident[:, 0:width],
                                              start=False, stop=False, skip_group_check=True)
                            for j in range(TJ):
                                own = gs[l][:, 2 * j + 1].rearrange("p d n -> p (d n)")
                                mm = pe.matmul(fb[l][:, j * P:(j + 1) * P], own, w.ident[:],
                                               start=False, stop=True, skip_group_check=True)
                            mm.then_inc(S.f_psum, 1)
                        for l in range(2):
                            if s == 0:
                                pe.wait_ge(S.v_ready, nth(i, 1, 0, l) + START)
                            more = s < NS - 1
                            token_biases(l, "z", "gz" if more else None)
                            pe.wait_ge(S.wave_ready, nth(i, NS, s, l) + START)
                            tokens(l, [wave[l]], [w.wz[:]], [w.gz[:]] if more else None, S.z_psum)
                    for l in range(2):
                        pe.wait_ge(S.y_ready, i * (2 * TJ) + (l + 1) * TJ + START)
                        turn_to(l, y[l], zb[l]).then_inc(S.y_psum, 1)
                    for l in range(2):
                        pe.wait_ge(S.xT_ready, nth(i, 2, 1, l) + START)
                        token_biases(l, "proj", None)
                        tokens(l, [xT[l][:, k, :] for k in range(KC)], [w.wproj[:, k, :] for k in range(KC)],
                               None, None).then_inc(S.proj_psum, 1)

            @block.scalar
            def _(act):
                with act.Fori(0, ROUNDS) as i:
                    act.activation(idle[0][:], w.eps[:, 0:1], ACT.Sin)
                    for l in range(2):
                        act.wait_ge(S.xT_psum, nth(i, 1, 0, l) + START)
                        act.activation(xT[l][:].rearrange("p k t -> p (k t)"), zb[l][:], ACT.Copy).then_inc(S.xT_ready, 1)
                    for l in range(2):
                        act.wait_ge(S.z_psum, halves(i, 0, l, 1) + START)
                        act.activation(v[l][:].rearrange("p j c -> p (j c)"), zb[l][:], ACT.Copy).then_inc(S.v_ready, 1)
                    for s in range(NS):
                        for l in range(2):
                            act.wait_ge(S.f_psum, nth(i, NS, s, l) + START)
                            act.activation(whole[l][:], fb[l][:], ACT.Copy, bias=MAGIC).then_inc(S.whole_ready, 1)
                        for l in range(2):
                            act.wait_ge(S.turns_ready, nth(i, NS, s, l) + START)
                            act.activation(wave[l][:], turns[l][:], ACT.Sin, scale=-SIN_SCALE).then_inc(S.wave_ready, 1)
                    for l in range(2):
                        act.wait_ge(S.y_psum, nth(i, 1, 0, l) + START)
                        act.activation(xT[l][:].rearrange("p k t -> p (k t)"), zb[l][:], ACT.Copy).then_inc(S.xT_ready, 1)


def experts_ffn(nc, w, io, sem, tag):
    with ExitStack() as ctx:
        def tmp(name, shape, dt=F32):
            return ctx.enter_context(nc.sbuf_tensor(f"{tag}_{name}", shape, dt))

        def psum(name, n):
            return ctx.enter_context(nc.psum_tensor(f"{tag}_{name}", [P, n], F32))

        G = TJ * H
        R = NHI + NKEYS

        bk01, bk2, bk3, bk4, bk5, acc = (
            psum("bk01", 1024), psum("bk2", 512), psum("bk3", 512), psum("bk4", 512), psum("bk5", 512),
            psum("acc", TJ * C))
        bk = [bk01[:, 0:512], bk01[:, 512:1024], bk2[:], bk3[:], bk4[:], bk5[:]]
        rank_bank, score_bank = [bk[0], bk[2], bk[3]], [bk[1], bk[4], bk[5]]

        stats, mv, rstd = tmp("stats", [P, TJ, 6]), tmp("mv", [P, TJ, 2]), tmp("rstd", [P, TJ])
        xn = tmp("xn", [P, TJ, C])
        hot_x = xn[:].rearrange("p j c -> p (j c)").bitcast(BF16).rearrange("p (g r i) -> p g r i", g=G, i=KPH)
        wgu = [tmp("wg", [P, 2, KC, DCD], F32R), tmp("wu", [P, 2, KC, DCD], F32R)]
        E = tmp("E", [P, 2, H, T])
        mid = tmp("mid", [P, 4, T])
        scoreT = tmp("scoreT", [P, 2, H * T], F32R)
        whole_gu = [mid[:].rearrange("p f t -> p (f t)"), E[:, 1].rearrange("p h t -> p (h t)")]
        hT = scoreT[:, 1].rearrange("p (a k t) -> p a k t", a=2, k=KC)
        sim_row = E[:, 0].rearrange("p h t -> p (h t)")
        sim = sim_row.rearrange("p (t q h k) -> p t q h k", q=2, h=H, k=NKEYS)
        picked, pair = [x.rearrange("p (g i j) -> p g i j", i=KPH, j=KPH) for x in (
            E[:, 1, 0:2].rearrange("p h t -> p (h t)"), E[:, 1, 2:4].rearrange("p h t -> p (h t)"))]
        digitsT = tmp("digitsT", [P, H * T], BF16)
        ranking = digitsT[:].bitcast(F32).rearrange("p (n g i) -> p n g i", g=G, i=KPH)
        top, below, expo, idx = ranking[:, 0:2], ranking[:, 2:4], ranking[:, 4:6], ranking[:, 6:8].bitcast(U32)
        best, row_sum, beyond = (tmp(n, [P, G, KPH])[:] for n in ("best", "row_sum", "beyond"))
        hot_y = [x.rearrange("p g i j -> p (g i j)").bitcast(BF16).rearrange("p (h k j) -> p h k j", h=H, j=KPH)
                 for x in (picked, pair)]
        idxb, countb = tmp("idxb", [P, 2, G, KPH], BF16), tmp("countb", [P, G, KPH], BF16)
        total, ln_total, inv_total, offset, over = (tmp(n, [P, G]) for n in (
            "total", "ln_total", "inv_total", "offset", "over"))
        idle = tmp("idle", [P, 2])
        pause = tmp("pause", [P, 16])
        digits = tmp("digits", [P, TJ, H, ROWS], BF16)
        scores = tmp("scores", [P, TJ, H, ROWS])
        gate = tmp("gate", [P, 2, T])
        mixed, over_row = [mid[:, 0, :], mid[:, 1, :]], mid[:, 3, :]
        reach = tmp("reach", [P, FC, T])

        S = w.ffn_signals[tag]
        ROUNDS = B
        RANK_STEPS = 24
        POOL_SUMS = 2 * FC + 1
        TREE_STEPS = 2 * (TJ + 1)

        def lower_weights(engine, n):
            engine.wait_ge(upper_made, n + 1)
            upper, lower = (wgu[n][:, part].rearrange("p k n -> p (k n)") for part in range(2))
            engine.tensor_tensor(lower, whole_gu[n], upper.bitcast(F32), ALU.subtract).then_inc(weights_split, 1)

        weights_loaded = [sem(f"{tag}_wg_loaded"), sem(f"{tag}_wu_loaded")]
        upper_made, weights_split = sem(f"{tag}_upper_made"), sem(f"{tag}_weights_split")

        with nc.Block() as block:
            @block.sync
            def _(sp):
                for whole, src, loaded in zip(whole_gu, (io.Wg, io.Wu), weights_loaded):
                    sp.dma_start(whole.rearrange("p (k n) -> p k n", k=KC), src.rearrange("(k p) n -> p k n", p=P)
                                 ).then_inc(loaded, 16)

            @block.vector
            def _(dve):
                dve.memset(digits[:], 0.0)
                dve.memset(scores[:], 0.0)

                def moments(r):
                    for j in range(TJ):
                        dve.bn_stats(stats[:, j, :], w.x[:, bass.ds(r * TJ + j, 1), :]).then_inc(S.stats_ready, 1)
                    dve.wait_ge(S.stats_ready, r * TJ + TJ + START)
                    dve.memset(pause[:, 15:16], 0.0)
                    for j in range(TJ):
                        dve.bn_aggr(mv[:, j, :], stats[:, j, :]).then_inc(S.mv_ready, 1)

                def normalise(r):
                    dve.wait_ge(S.rstd_ready, r + 1 + START)
                    for j in range(TJ):
                        dve.tensor_scalar(xn[:, j, :], w.x[:, bass.ds(r * TJ + j, 1), :], mv[:, j, 0:1],
                                          rstd[:, j:j + 1], ALU.subtract, ALU.mult).then_inc(S.xn_ready, 1)

                def rest_of_hT(r):
                    dve.wait_ge(S.hT_ready, r + 1 + START)
                    dve.tensor_tensor(hT[:, 1].rearrange("p k t -> p (k t)"), bk01[:],
                                      hT[:, 0].rearrange("p k t -> p (k t)").bitcast(F32), ALU.subtract
                                      ).then_inc(S.hT_rest, 1)

                def a_round(i, last):
                    steps, pauses = [0], [0]

                    def carry_wait():
                        dve.memset(pause[:, pauses[0]:pauses[0] + 1], 0.0)
                        pauses[0] += 1

                    def link(ins):
                        steps[0] += 1
                        ins.then_inc(S.rank_step, 1)

                    def settle(carry=False):
                        dve.wait_ge(S.rank_step, i * RANK_STEPS + steps[0] + START)
                        if carry:
                            carry_wait()

                    def add_up(hot, out, n, name):
                        for level, half in enumerate((4, 2, 1)):
                            if level:
                                dve.wait_ge(S.tree_step, i * TREE_STEPS + 2 * n + level + START)
                            dst = hot[:, :, :, 0:half] if half > 1 else out.unsqueeze(3)
                            ins = dve.tensor_tensor(dst, hot[:, :, :, 0:half], hot[:, :, :, half:2 * half], ALU.add)
                            ins.then_inc(S.tree_step if half > 1 else name, 1)

                    def rank_lo(t):
                        dve.wait_ge(S.hot_weighted, i * TJ + t + 1 + START)
                        add_up(hot_y[t % 2], digits[:, t, :, NHI:R], t, S.digits_ready)

                    for t in range(TJ):
                        of_tile = slice(t * H, (t + 1) * H)
                        dve.wait_ge(S.sim_ready, i * TJ + t + 1 + START)
                        carry_wait()
                        for q in range(2):
                            for h in range(H):
                                m = dve.max(top[:, q, t * H + h, :], sim[:, t, q, h, :])
                        link(m)
                        settle(carry=True)
                        for q in range(2):
                            for h in range(H):
                                m = dve.max_index(idx[:, q, t * H + h, :], top[:, q, t * H + h, :], sim[:, t, q, h, :])
                        m.then_inc(S.top_ready, 1)
                        dve.wait_ge(S.top_ready, i * TJ + t + 1 + START)
                        link(dve.tensor_copy(idxb[:, :, of_tile, :], idx[:, :, of_tile, :]))
                        settle()
                        if t >= 2:
                            dve.wait_ge(S.digits_ready, i * 6 + t - 1 + START)
                        dve.tensor_tensor(hot_y[t % 2], spread(w.iota_lo[:], 1, H),
                                          spread(idxb[:, 1, of_tile], 2, NKEYS), ALU.is_equal).then_inc(S.hot_ready, 1)
                        if t >= 1:
                            rank_lo(t - 1)
                    dve.tensor_tensor(below, top, top[:, :, :, 0:1].to_broadcast([P, 2, G, KPH]),
                                      ALU.subtract).then_inc(S.below_ready, 1)
                    link(dve.tensor_tensor(hot_x, spread(w.iota_lo[:, 0:NHI, :], 1, G), spread(idxb[:, 0], 2, NHI),
                                           ALU.is_equal))
                    rank_lo(TJ - 1)
                    dve.wait_ge(S.digits_ready, i * 6 + TJ + START)
                    link(dve.tensor_tensor(pair, spread(top[:, 0], 3, KPH), spread(top[:, 1], 2, KPH), ALU.add))
                    settle(carry=True)
                    flat = pair.rearrange("p g i j -> p g (i j)")
                    marked = picked.rearrange("p g i j -> p g (i j)")
                    for g in range(G):
                        m = dve.max(best[:, g, :], flat[:, g, :])
                    link(m)
                    settle(carry=True)
                    for g in range(G):
                        m = dve.match_replace(marked[:, g, :], best[:, g, :], flat[:, g, :], -3.0e38)
                    link(m)
                    settle()
                    link(dve.tensor_tensor(picked, picked, pair, ALU.not_equal))
                    settle()
                    dve.wait_ge(S.expo_ready, i + 1 + START)
                    link(dve.tensor_tensor(pair, picked, spread(expo[:, 1], 2, KPH), ALU.mult))
                    with nc.allow_low_precision(reason="whole numbers up to 8, exact in bf16"):
                        link(dve.tensor_reduce(countb[:], picked, AX.X, ALU.add))
                    settle()
                    link(dve.tensor_reduce(row_sum, pair, AX.X, ALU.add))
                    link(dve.tensor_tensor(hot_x, hot_x, spread(countb[:], 2, NHI), ALU.mult))
                    settle()
                    link(dve.tensor_tensor(row_sum, row_sum, expo[:, 0], ALU.mult))
                    settle()
                    dve.tensor_reduce(total[:], row_sum, AX.X, ALU.add).then_inc(S.total_ready, 1)
                    link(dve.scalar_tensor_tensor(out=beyond, in0=idxb[:, 0], scalar=float(NHI), in1=row_sum,
                                                  op0=ALU.is_ge, op1=ALU.mult))
                    add_up(hot_x, digits[:].rearrange("p t h r -> p (t h) r")[:, :, 0:NHI], TJ, S.digits_ready)
                    dve.wait_ge(S.total_ready, i + 1 + START)
                    link(dve.reciprocal(inv_total[:], total[:]))
                    settle()
                    link(dve.tensor_reduce(over[:], beyond, AX.X, ALU.add))
                    settle()
                    link(dve.tensor_tensor(over[:], over[:], inv_total[:], ALU.mult))
                    dve.wait_ge(S.ln_ready, i + 1 + START)
                    link(dve.tensor_tensor(offset[:], top[:, 0, :, 0], ln_total[:], ALU.add))
                    settle()
                    link(dve.tensor_reduce(scores[:, :, 0, R], over[:].rearrange("p (t h) -> p t h", h=H), AX.X, ALU.add))
                    dve.tensor_tensor(scores[:, :, :, 0:NHI], sim[:, :, 0, :, 0:NHI],
                                      spread(offset[:].rearrange("p (t h) -> p t h", h=H), 3, NHI),
                                      ALU.subtract).then_inc(S.digits_ready, 1)
                    for h in range(H):
                        dve.wait_ge(S.turned_ready, i * (2 * H) + 2 * (h + 1) + START)
                        dve.tensor_tensor(scoreT[0:ROWS, 1, h * T:(h + 1) * T], bk[2 + h % 2][0:ROWS, :],
                                          scoreT[0:ROWS, 0, h * T:(h + 1) * T].bitcast(F32), ALU.subtract).then_inc(S.rest_ready, 1)
                    assert steps[0] == RANK_STEPS, steps

                    def mix(c):
                        both, last = E[:, c % 2, 0], c == FC - 1
                        dve.wait_ge(S.pool_sum, i * POOL_SUMS + 2 * c + 2 + last + START)
                        dve.tensor_tensor(both, both, E[:, c % 2, 2], ALU.add).then_inc(S.mix_step, 1)
                        if c >= 2:
                            dve.wait_ge(S.mix_used, i * FC + c - 1 + START)
                        dve.wait_ge(S.mix_step, i * FC + c + 1 + START)
                        dve.tensor_tensor(mixed[c % 2], both, reach[:, c, :], ALU.mult).then_inc(S.mix_ready, 1)

                    dve.wait_ge(S.mid_used, i * FC + FC + START)
                    for c in range(FC):
                        for h in range(H):
                            n = c * H + h
                            dve.wait_ge(S.E_ready, i * (FC * H) + n + 1 + START)
                            dve.scalar_tensor_tensor(out=E[:, c % 2, h], in0=rank_bank[n % 3], scalar=float(KPH),
                                                     in1=E[:, c % 2, h], op0=ALU.is_gt, op1=ALU.mult
                                                     ).then_inc(S.masked, 1)
                            if c >= 1 and h == 1:
                                mix(c - 1)
                        if not last:
                            if c == 3:
                                moments(i + 1)
                            if c == 4:
                                normalise(i + 1)
                    if not last:
                        rest_of_hT(i + 1)
                    mix(FC - 1)
                    dve.wait_ge(S.mix_used, i * FC + FC + START)
                    xs = w.x[:, bass.ds(i * TJ, TJ), :].rearrange("p j c -> p (j c)")
                    dve.tensor_tensor(xs, acc[:], xs, ALU.add).then_inc(S.x_added, 1)

                moments(0)
                normalise(0)
                rest_of_hT(0)
                lower_weights(dve, 1)
                with dve.Fori(0, ROUNDS - 1) as i:
                    a_round(i, last=False)
                a_round(ROUNDS - 1, last=True)

            @block.gpsimd
            def _(pool):
                def deviations(r):
                    pool.wait_ge(S.xn_ready, r * TJ + START)
                    pool.wait_ge(S.mv_ready, r * TJ + TJ + START)
                    pool.tensor_tensor(rstd[:], mv[:, :, 1], w.eps[:, 0:TJ], ALU.add).then_inc(S.var_eps, 1)
                    pool.wait_ge(S.var_eps, r + 1 + START)
                    pool.tensor_tensor(rstd[:], rstd[:], w.minus_half[:, 0:TJ], ALU.pow).then_inc(S.rstd_ready, 1)

                def a_round(i, last):
                    def weigh(t):
                        pool.wait_ge(S.hot_ready, i * TJ + t + 1 + START)
                        pool.tensor_tensor(hot_y[t % 2], hot_y[t % 2], spread(w.rank_weight[:], 1, H), ALU.mult
                                           ).then_inc(S.hot_weighted, 1)

                    def second_digit(t):
                        pool.tensor_tensor(scores[:, t, :, NHI:R], sim[:, t, 1],
                                           spread(top[:, 1, t * H:(t + 1) * H, 0], 2, NKEYS),
                                           ALU.subtract).then_inc(S.second_ready, 1)

                    def times_up(f):
                        pool.wait_ge(S.gate_ready, i * FC + f + 1 + START)
                        pool.tensor_tensor(mid[:, f % 4, :], mid[:, f % 4, :], gate[:, f % 2, :], ALU.mult
                                           ).then_inc(S.mid_ready, 1)

                    for t in range(3):
                        weigh(t)
                    times_up(0)
                    weigh(3)
                    for f in range(1, FC):
                        times_up(f)
                        if 2 <= f < 2 + TJ:
                            second_digit(f - 2)
                    for c in range(FC):
                        for a in (0, 2):
                            pool.wait_ge(S.masked, i * (FC * H) + c * H + a + 2 + START)
                            pool.tensor_tensor(E[:, c % 2, a], E[:, c % 2, a], E[:, c % 2, a + 1], ALU.add
                                               ).then_inc(S.pool_sum, 1)
                        if c == 3 and not last:
                            deviations(i + 1)
                    pool.wait_ge(S.over_ready, i + 1 + START)
                    pool.wait_ge(S.pool_sum, i * POOL_SUMS + 2 * FC + START)
                    pool.tensor_tensor(E[:, (FC - 1) % 2, 2], E[:, (FC - 1) % 2, 2], over_row, ALU.add
                                       ).then_inc(S.pool_sum, 1)

                deviations(0)
                lower_weights(pool, 0)
                with pool.Fori(0, ROUNDS - 1) as i:
                    a_round(i, last=False)
                a_round(ROUNDS - 1, last=True)

            @block.tensor
            def _(pe):
                def three_products(out, lhsT, rhs):
                    terms = [(k, a, b) for k in range(KC) for a, b in ((0, 0), (0, 1), (1, 0))]
                    for n, (k, a, b) in enumerate(terms):
                        mm = pe.matmul(out, lhsT(a, k), rhs(b, k), start=(n == 0), stop=(n == len(terms) - 1))
                    return mm

                def turn_x(r):
                    pe.wait_ge(S.xn_ready, r * TJ + TJ + START)
                    pe.wait_ge(S.masked, r * (FC * H) + START)
                    for k in range(KC):
                        for j in range(TJ):
                            mm = pe.transpose(bk[k][:, j * P:(j + 1) * P], xn[:, j, k * P:(k + 1) * P], w.ident[:])
                    mm.then_inc(S.hT_psum, 1)

                def similarities(r, tiles):
                    for t in tiles:
                        if t == 0:
                            pe.wait_ge(S.hT_rest, r + 1 + START)
                        if t >= 2:
                            pe.wait_ge(S.sim_ready, r * TJ + t - 1 + START)
                        three_products(bk[2 + t % 2], lambda a, k: hT[:, a, k, t * P:(t + 1) * P],
                                       lambda a, k: w.wsim[:, a, k, :]).then_inc(S.sim_psum, 1)

                def a_round(i, last):
                    for c in range(FC):
                        if c >= 4:
                            pe.wait_ge(S.reach_ready, i * FC + c - 3 + START)
                        three_products(bk[(4, 5, 0, 1)[c % 4]], lambda a, k: w.deT[:, a, k, c * P:(c + 1) * P],
                                       lambda a, k: hT[:, a, k, :]).then_inc(S.w_psum, 1)
                    pe.wait_ge(S.x_added, i + START)
                    for n in range(2):
                        pe.matmul(acc[:, n * 512:(n + 1) * 512], w.ones3[:], bias(w, "bd", 2), start=True, stop=True)

                    def mlp_out(f):
                        pe.wait_ge(S.mid_ready, i * FC + f + 1 + START)
                        for j in range(TJ):
                            mm = pe.matmul(acc[:, j * C:(j + 1) * C], mid[:, f % 4, j * P:(j + 1) * P], w.wd[:, f, :],
                                           start=False, stop=True, skip_group_check=True)
                        mm.then_inc(S.mid_used, 1)

                    pe.wait_ge(weights_split, 2)
                    for f in range(FC):
                        if f < 2:
                            pe.wait_ge(S.reach_ready, i * FC + 6 + 2 * f + START)
                        else:
                            pe.wait_ge(S.gate_ready, i * FC + f - 1 + START)
                        g, u = (bk[4], bk[5]) if f % 2 == 0 else (bk[0], bk[1])
                        for out, weights in zip((g, u), wgu):
                            mm = three_products(out, lambda a, k: weights[:, a, k, f * P:(f + 1) * P],
                                                lambda a, k: hT[:, a, k, :])
                        mm.then_inc(S.gu_psum, 1)
                        if f >= 2:
                            mlp_out(f - 2)
                    mlp_out(FC - 2)

                    def turn_digits(h):
                        if h >= 2:
                            pe.wait_ge(S.rest_ready, i * H + h - 1 + START)
                        for t in range(TJ):
                            pe.transpose(bk[2 + h % 2][0:ROWS, t * P:(t + 1) * P], scores[:, t, h, :], w.ident[:])
                            mm = pe.transpose(bk[4 + h % 2].bitcast(BF16)[0:ROWS, t * P:(t + 1) * P],
                                              digits[:, t, h, :], w.identb[:])
                        mm.then_inc(S.turned_psum, 1)

                    pe.wait_ge(S.digits_ready, i * 6 + 6 + START)
                    pe.wait_ge(S.second_ready, i * TJ + TJ + START)
                    turn_digits(0)
                    turn_digits(1)
                    mlp_out(FC - 1)
                    turn_digits(2)
                    turn_digits(3)

                    def experts(c):
                        pe.wait_ge(S.mix_ready, i * FC + c + 1 + START)
                        for j in range(TJ):
                            mm = pe.matmul(acc[:, j * C:(j + 1) * C], mixed[c % 2][:, j * P:(j + 1) * P],
                                           w.ue[:, c, :], start=False, stop=True, skip_group_check=True)
                        mm.then_inc(S.mix_used, 1)

                    for c in range(FC):
                        for h in range(H):
                            n = c * H + h
                            if n < H:
                                there = h if n == 0 else min(h + 1, H - 1)
                                pe.wait_ge(S.turned_ready, i * (2 * H) + 2 * (there + 1) + START)
                                pe.wait_ge(S.rest_ready, i * H + there + 1 + START)
                            if n >= 3:
                                pe.wait_ge(S.masked, i * (FC * H) + n - 2 + START)
                            if n == 3:
                                for part in range(2):
                                    mm = pe.matmul(rank_bank[0], w.selovf[:], scoreT[0:ROWS, part, 0:T],
                                                   start=(part == 0), stop=(part == 1))
                                mm.then_inc(S.over_psum, 1)
                                pe.wait_ge(S.over_ready, i + 1 + START)
                            pe.matmul(rank_bank[n % 3], w.selb[:, c].rearrange("r a e -> r (a e)"), digitsT[0:ROWS, h * T:(h + 1) * T],
                                      start=True, stop=True)
                            for part in range(2):
                                mm = pe.matmul(score_bank[n % 3], w.sel[:, c].rearrange("r a e -> r (a e)"),
                                               scoreT[0:ROWS, part, h * T:(h + 1) * T],
                                               start=(part == 0), stop=(part == 1))
                            mm.then_inc(S.ds_psum, 1)
                            if c >= 2 and h == 1:
                                experts(c - 2)
                    if not last:
                        turn_x(i + 1)
                    experts(FC - 2)
                    if not last:
                        similarities(i + 1, (0, 1))
                    experts(FC - 1)
                    if not last:
                        similarities(i + 1, (2, 3))

                turn_x(0)
                similarities(0, range(TJ))
                with pe.Fori(0, ROUNDS - 1) as i:
                    a_round(i, last=False)
                a_round(ROUNDS - 1, last=True)

            @block.scalar
            def _(act):
                def evacuate(r):
                    act.wait_ge(S.hT_psum, r + 1 + START)
                    act.activation(hT[:, 0].rearrange("p k t -> p (k t)"), bk01[:], ACT.Copy).then_inc(S.hT_ready, 1)
                    act.activation(idle[:, 0:1], w.eps[:, 0:1], ACT.Silu)
                    for t in range(TJ):
                        act.wait_ge(S.sim_psum, r * TJ + t + 1 + START)
                        act.activation(sim_row[:, t * 512:(t + 1) * 512], bk[2 + t % 2], ACT.Copy).then_inc(S.sim_ready, 1)

                def a_round(i, last):
                    act.wait_ge(S.mix_ready, i * FC + START)
                    for c in range(FC):
                        act.wait_ge(S.w_psum, i * FC + c + 1 + START)
                        act.activation(reach[:, c, :], bk[(4, 5, 0, 1)[c % 4]], ACT.Silu).then_inc(S.reach_ready, 1)

                    def gates(f):
                        act.wait_ge(S.gu_psum, i * FC + f + 1 + START)
                        if f >= 2:
                            act.wait_ge(S.mid_ready, i * FC + f - 1 + START)
                        if f >= 4:
                            act.wait_ge(S.mid_used, i * FC + f - 3 + START)
                        g, u = (bk[4], bk[5]) if f % 2 == 0 else (bk[0], bk[1])
                        act.activation(gate[:, f % 2, :], g, ACT.Silu, bias=w.bg[:, f:f + 1])
                        act.activation(mid[:, f % 4, :], u, ACT.Identity, bias=w.bu[:, f:f + 1]
                                       ).then_inc(S.gate_ready, 1)

                    for f in range(3):
                        gates(f)
                    act.wait_ge(S.below_ready, i + 1 + START)
                    act.activation(expo, below, ACT.Exp).then_inc(S.expo_ready, 1)
                    for f in range(3, 6):
                        gates(f)
                    act.wait_ge(S.total_ready, i + 1 + START)
                    act.activation(ln_total[:], total[:], ACT.Ln).then_inc(S.ln_ready, 1)
                    gates(6)
                    gates(7)
                    act.activation(idle[:, 1:2], w.eps[:, 0:1], ACT.Exp)
                    for h in range(H):
                        act.wait_ge(S.turned_psum, i * H + h + 1 + START)
                        act.activation(digitsT[0:ROWS, h * T:(h + 1) * T], bk[4 + h % 2].bitcast(BF16)[0:ROWS, 0:T], ACT.Copy
                                       ).then_inc(S.turned_ready, 1)
                        act.activation(scoreT[0:ROWS, 0, h * T:(h + 1) * T], bk[2 + h % 2][0:ROWS, :], ACT.Copy
                                       ).then_inc(S.turned_ready, 1)
                    for c in range(FC):
                        if c >= 2:
                            act.wait_ge(S.mix_ready, i * FC + c - 1 + START)
                        for h in range(H):
                            n = c * H + h
                            if n == 3:
                                act.wait_ge(S.over_psum, i + 1 + START)
                                act.wait_ge(S.mid_used, i * FC + FC + START)
                                act.activation(over_row, rank_bank[0], ACT.Copy).then_inc(S.over_ready, 1)
                            act.wait_ge(S.ds_psum, i * (FC * H) + n + 1 + START)
                            act.activation(E[:, c % 2, h], score_bank[n % 3], ACT.Exp).then_inc(S.E_ready, 1)
                    if not last:
                        act.wait_ge(S.mix_ready, i * FC + FC - 1 + START)
                        evacuate(i + 1)

                evacuate(0)
                for weights, whole, loaded in zip(wgu, whole_gu, weights_loaded):
                    act.wait_ge(loaded, 16)
                    act.activation(weights[:, 0].rearrange("p k n -> p (k n)"), whole, ACT.Copy).then_inc(upper_made, 1)
                with act.Fori(0, ROUNDS - 1) as i:
                    a_round(i, last=False)
                a_round(ROUNDS - 1, last=True)


class Turns:

    def __init__(self, order, readers, before, each, S):
        self.order, self.reader = order, readers
        self.before, self.each = before, each
        self.S = S

    def _count(self, names, engine):
        return len([n for n in names if self.reader[n[0]] in (engine, "both")])

    def place(self, name):
        return (len(self.before) + self.order.index(name)) % 3

    def filled(self, i, name):
        return self.S.filled, i * len(self.each) + len(self.before) + self.order.index(name) + 1 + START

    def read(self, i, name):
        [wait] = self._read_to(i, self.order.index(name))
        return wait

    def _read_to(self, i, at):
        waits = []
        past = self.each if self.each else self.order
        reader = self.reader[(self.order if at >= 0 else past)[at][0]]
        for engine, signal in (("act", self.S.act_read), ("dve", self.S.dve_read)):
            if reader in (engine, "both"):
                extra = (self._count(self.order[:at + 1], engine) if at >= 0
                         else -self._count(past[len(past) + at + 1:], engine))
                waits.append((signal, i * self._count(self.each, engine) + self._count(self.before, engine)
                              + extra + START))
        return waits

    def free(self, i, name):
        at = self.order.index(name) - 3
        return [] if at < 0 and not self.before else self._read_to(i, at)


def linear_attention(nc, w, sem):
    with ExitStack() as ctx:
        def tmp(name, shape, dt=F32):
            return ctx.enter_context(nc.sbuf_tensor(f"b_{name}", shape, dt))

        def psum(name, n):
            return ctx.enter_context(nc.psum_tensor(f"b_{name}", [P, n], F32))

        QH = 4
        GROUPS = HEADS // QH
        UNITS = 3 * GROUPS
        WIDTH = [512, 384, 384]
        BLOCKS = [[(0, 0)], [(1, 0)], [(2, 0), (3, 256)]]
        NG = 2 * HEADS
        HP = HEADS // 2
        VW = 2 * FEAT

        two = [psum(f"two{n}", 1024) for n in range(3)]
        yT, aux = psum("yT", 512), psum("aux", 512)

        stats, mv, rstd = tmp("stats", [P, TJ, 6]), tmp("mv", [P, TJ, 2]), tmp("rstd", [P, TJ])
        pause = tmp("pause", [P, 1])
        xn = tmp("xn", [P, TJ, C])
        hT = tmp("hT", [P, KC, T])
        qk = tmp("qk", [P, TJ, NG, FEAT])
        var, rms, step = tmp("var", [P, TJ * NG]), tmp("rms", [P, TJ * NG]), tmp("step", [P, TJ * NG])
        mean = tmp("mean", [P, KC, NG])
        parts = [tmp("q_parts", [P, 2, HEADS, 4, FEAT]), tmp("k_parts", [P, 2, HEADS, 4, FEAT])]
        squares = parts[0][:, 0].rearrange("p h s f -> p (h s f)").rearrange(
            "p (t g f) -> p t g f", t=2, g=NG)
        qT, kT = tmp("qT", [P, HEADS, T], F32R), tmp("kT", [P, HP, T], F32R)
        va = tmp("va", [P, TJ, HEADS, VW])
        U = [tmp(f"U{k}", [P, QH, WIDTH[k]]) for k in range(3)]
        y_heads = tmp("y_heads", [P, T])
        den, inv = tmp("den", [P, TJ, QH]), tmp("inv", [P, TJ, QH])

        S = w.attn_signals
        consts, centred, zeros_there = sem("b_consts"), sem("b_centred"), sem("b_zeros_there")

        readers = {"s": "act", "tq": "both", "tk": "act", "x": "act", "v": "dve", "o": "act", "p": "dve"}
        turned = [(("tq", "tk")[m], t) for t in range(TJ) for m in range(2)]
        prepare = [("x", 0)] + turned + [("v", 0)]
        s = [("s", n) for n in range(2 * UNITS)]
        each = s[0:5] + [("x", 0)] + s[5:] + turned + [("v", 0), ("o", 0), ("p", 0)]
        assert len(each) % 3 == 0
        start = Turns(prepare, readers, [], [], S)
        steady = Turns(each, readers, prepare, each, S)
        final = Turns(s + [("o", 0), ("p", 0)], readers, prepare, each, S)

        def wide(turns, name):
            return two[turns.place(name)]

        def lower_part(engine, r, t, m):
            engine.wait_ge(S.hi_ready, r * (2 * TJ) + 2 * t + m + 1 + START)
            heads, part = qk[:, t, m * HEADS:(m + 1) * HEADS, :], parts[m][:, t % 2]
            lo = part[:, :, 1:4:2, :] if m else part[:, :, 2:4, :]
            return engine.tensor_tensor(lo, spread(heads, 2, 2), spread(part[:, :, 0, :], 2, 2), ALU.subtract)

        with nc.Block() as block:
            @block.vector
            def _(dve):
                def moments(r):
                    for j in range(TJ):
                        dve.bn_stats(stats[:, j, :], w.x[:, bass.ds(r * TJ + j, 1), :]).then_inc(S.stats_ready, 1)
                    dve.wait_ge(S.stats_ready, r * TJ + TJ + START)
                    dve.memset(pause[:], 0.0)
                    for j in range(TJ):
                        dve.bn_aggr(mv[:, j, :], stats[:, j, :]).then_inc(S.mv_ready, 1)

                def normalise(r):
                    dve.wait_ge(S.rstd_ready, r + 1 + START)
                    for j in range(TJ):
                        dve.tensor_scalar(xn[:, j, :], w.x[:, bass.ds(r * TJ + j, 1), :], mv[:, j, 0:1],
                                          rstd[:, j:j + 1], ALU.subtract, ALU.mult).then_inc(S.xn_ready, 1)

                def variance(r, t):
                    dve.wait_ge(S.squared, r * TJ + t + 1 + START)
                    dve.tensor_reduce(var[:, t * NG:(t + 1) * NG], squares[:, t % 2], AX.X, ALU.add
                                      ).then_inc(S.var_ready, 1)

                def head_deviations(r, p):
                    v, y, z = (x[:, p * 2 * NG:(p + 1) * 2 * NG] for x in (var, rms, step))
                    at = r * 10 + 5 * p + START
                    dve.wait_ge(S.head_dev, r * 2 + p + 1 + START)
                    dve.reciprocal(y, y).then_inc(S.rms_step, 1)
                    dve.tensor_scalar(v, v, LN_EPS, None, ALU.add).then_inc(S.rms_step, 1)
                    dve.wait_ge(S.rms_step, at + 2)
                    dve.tensor_tensor(z, y, y, ALU.mult).then_inc(S.rms_step, 1)
                    dve.wait_ge(S.rms_step, at + 3)
                    dve.scalar_tensor_tensor(out=z, in0=z, scalar=-0.5, in1=v, op0=ALU.mult, op1=ALU.mult
                                             ).then_inc(S.rms_step, 1)
                    dve.wait_ge(S.rms_step, at + 4)
                    dve.scalar_tensor_tensor(out=y, in0=z, scalar=1.5, in1=y, op0=ALU.add, op1=ALU.mult
                                             ).then_inc(S.rms_step, 1)
                    dve.wait_ge(S.rms_step, at + 5)
                    for t in (2 * p, 2 * p + 1):
                        dve.tensor_tensor(qk[:, t], qk[:, t], spread(rms[:, t * NG:(t + 1) * NG], 2, FEAT), ALU.mult
                                          ).then_inc(S.scaled, 1)

                def lower_q(r, t):
                    lower_part(dve, r, t, 0).then_inc(S.lo_q_ready, 1)

                def turned_q(i, turns, t):
                    dve.wait_ge(*turns.filled(i, ("tq", t)))
                    dve.tensor_copy(qT[64:P, 1:HEADS:2, t * P:(t + 1) * P],
                                    wide(turns, ("tq", t))[64:P, :].rearrange("p (g c) -> p g c", c=P)
                                    ).then_inc(S.dve_read, 1)

                def values(i, turns):
                    dve.wait_ge(*turns.filled(i, ("v", 0)))
                    dve.tensor_copy(va[:, :, :, 0:FEAT], wide(turns, ("v", 0))[:].rearrange(
                        "p (t h f) -> p t h f", t=TJ, f=FEAT)).then_inc(S.dve_read, 1)

                def take_outputs(i, g):
                    dve.wait_ge(S.y_psum, i * UNITS + 3 * g + 3 + START)
                    dve.tensor_copy(y_heads[:], yT[:]).then_inc(S.y_copied, 1)

                def divide(i, g):
                    dve.wait_ge(S.y_turned, i * GROUPS + g + 1 + START)
                    y = aux[:].rearrange("p (t h f) -> p t h f", t=TJ, f=VW)
                    dve.tensor_scalar(den[:], y[:, :, :, FEAT], 1e-5, None, ALU.add).then_inc(S.den_step, 1)
                    dve.wait_ge(S.den_step, i * (2 * GROUPS) + 2 * g + 1 + START)
                    dve.reciprocal(inv[:], den[:]).then_inc(S.den_step, 1)
                    dve.wait_ge(S.den_step, i * (2 * GROUPS) + 2 * g + 2 + START)
                    out = xn[:].rearrange("p t (h f) -> p t h f", f=FEAT)[:, :, QH * g:QH * (g + 1), :]
                    dve.tensor_tensor(out, y[:, :, :, 0:FEAT], spread(inv[:], 3, FEAT), ALU.mult
                                      ).then_inc(S.y_ready, 1)

                def a_batch(i, turns, last, moments_ahead):
                    if not last:
                        normalise(i + 1)
                    for u in range(UNITS):
                        g, k = u // 3, u % 3
                        dve.wait_ge(*turns.read(i, ("s", 2 * u + 1)))
                        for _, at in BLOCKS[k]:
                            diagonal = U[k][:, :, at:at + P]
                            mask = dve.tensor_tensor(diagonal, diagonal, spread(w.tri[:], 1, QH), ALU.mult)
                        mask.then_inc(S.masked, 1)
                        if k == 0 and g >= 1:
                            take_outputs(i, g - 1)
                        if k == 1 and g >= 1:
                            if g == 1 and not last:
                                dve.wait_ge(*turns.filled(i, ("x", 0)))
                            divide(i, g - 1)
                        if not last:
                            if 3 <= u < 3 + TJ:
                                variance(i + 1, u - 3)
                            if u in (5, 7):
                                head_deviations(i + 1, (u - 5) // 2)
                            if u in (9, 10):
                                lower_q(i + 1, u - 9)
                            if u == 10:
                                turned_q(i, turns, 0)
                    if not last:
                        for t in range(1, TJ):
                            if t >= 2:
                                lower_q(i + 1, t)
                            if t == 2:
                                take_outputs(i, GROUPS - 1)
                            turned_q(i, turns, t)
                        divide(i, GROUPS - 1)
                        values(i, turns)
                        if moments_ahead:
                            moments(i + 2)
                    else:
                        take_outputs(i, GROUPS - 1)
                        divide(i, GROUPS - 1)
                    dve.wait_ge(*turns.filled(i, ("p", 0)))
                    xs = w.x[:, bass.ds(i * TJ, TJ), :].rearrange("p j c -> p (j c)")
                    dve.tensor_tensor(xs, wide(turns, ("p", 0))[:], xs, ALU.add).then_inc(S.dve_read, 1)

                moments(0)
                rows = w.wqk[:].rearrange("p k (g f) -> p k g f", f=FEAT)
                dve.tensor_reduce(mean[:], rows, AX.X, ALU.add).then_inc(centred, 1)
                dve.wait_ge(centred, 1)
                dve.scalar_tensor_tensor(out=rows, in0=spread(mean[:], 3, FEAT), scalar=-1.0 / FEAT, in1=rows,
                                         op0=ALU.mult, op1=ALU.add).then_inc(centred, 1)
                normalise(0)
                dve.wait_ge(S.xn_ready, TJ + START)
                moments(1)
                for t in range(TJ):
                    variance(0, t)
                head_deviations(0, 0)
                head_deviations(0, 1)
                for t in range(TJ):
                    lower_q(0, t)
                    if t >= 1:
                        turned_q(0, start, t - 1)
                turned_q(0, start, TJ - 1)
                dve.wait_ge(consts, 2)
                values(0, start)
                with dve.Fori(0, B - 2) as i:
                    a_batch(i, steady, last=False, moments_ahead=True)
                a_batch(B - 2, steady, last=False, moments_ahead=False)
                a_batch(B - 1, final, last=True, moments_ahead=False)

            @block.gpsimd
            def _(pool):
                def deviations(r):
                    pool.wait_ge(S.xn_ready, r * TJ + START)
                    pool.wait_ge(S.mv_ready, r * TJ + TJ + START)
                    pool.tensor_tensor(rstd[:], mv[:, :, 1], w.eps[:, 0:TJ], ALU.add).then_inc(S.var_eps, 1)
                    pool.wait_ge(S.var_eps, r + 1 + START)
                    pool.tensor_tensor(rstd[:], rstd[:], w.minus_half[:, 0:TJ], ALU.pow).then_inc(S.rstd_ready, 1)

                def features(r):
                    for t in range(TJ):
                        pool.wait_ge(S.scaled, r * TJ + t + 1 + START)
                        pool.tensor_tensor(qk[:, t], qk[:, t], spread(w.gamma[:], 1, NG), ALU.mult
                                           ).then_inc(S.gamma_step, 1)
                        pool.wait_ge(S.gamma_step, r * TJ + t + 1 + START)
                        pool.tensor_tensor(qk[:, t], qk[:, t], spread(w.beta[:], 1, NG), ALU.add
                                           ).then_inc(S.feat_ready, 1)
                    for t in range(TJ):
                        lower_part(pool, r, t, 1).then_inc(S.lo_k_ready, 1)

                pool.memset(U[0][:], 0.0).then_inc(consts, 1)
                pool.memset(va[:], 1.0).then_inc(consts, 1)
                deviations(0)
                with pool.Fori(0, B - 1) as r:
                    features(r)
                    deviations(r + 1)
                features(B - 1)

            @block.tensor
            def _(pe):
                def claim(i, turns, name):
                    for wait in turns.free(i, name):
                        pe.wait_ge(*wait)
                    return wide(turns, name)

                def turn(out):
                    for k in range(KC):
                        for j in range(TJ):
                            mm = pe.transpose(out[:, k * T + j * P:k * T + (j + 1) * P],
                                              xn[:, j, k * P:(k + 1) * P], w.ident[:])
                    mm.then_inc(S.filled, 1)

                def turn_x(i, turns, r):
                    pe.wait_ge(S.xn_ready, r * TJ + TJ + START)
                    turn(claim(i, turns, ("x", 0)))

                def queries_keys(r, t):
                    for k in range(KC):
                        mm = pe.matmul(aux[:], hT[:, k, t * P:(t + 1) * P], w.wqk[:, k, :],
                                       start=(k == 0), stop=(k == KC - 1))
                    mm.then_inc(S.qk_psum, 1)

                def turn_parts(i, turns, r, n):
                    t, m = n // 2, n % 2
                    out = claim(i, turns, turned[n])
                    pe.wait_ge(S.lo_k_ready if m else S.lo_q_ready, r * TJ + t + 1 + START)
                    for hp in range(HP):
                        mm = pe.transpose(out[:, hp * P:(hp + 1) * P],
                                          parts[m][:, t % 2, 2 * hp:2 * hp + 2].rearrange("p h s f -> p (h s f)"), w.ident[:])
                    mm.then_inc(S.filled, 1)

                def values(i, turns):
                    out = claim(i, turns, ("v", 0))
                    for t in range(TJ):
                        for k in range(KC):
                            mm = pe.matmul(out[:, t * C:(t + 1) * C], hT[:, k, t * P:(t + 1) * P], w.wvb[:, k, :],
                                           start=(k == 0), stop=(k == KC - 1))
                    mm.then_inc(S.filled, 1)

                def scores(i, turns, n):
                    u, q = n // 2, n % 2
                    g, k = u // 3, u % 3
                    if n == 0:
                        pe.wait_ge(S.act_read, i * ACT_READS + 1 + 2 * TJ + START)
                        pe.wait_ge(S.dve_read, i * DVE_READS + TJ + 1 + START)
                    out = claim(i, turns, ("s", n))
                    for j in range(2):
                        h = QH * g + 2 * q + j
                        for b, (kb, at) in enumerate(BLOCKS[k]):
                            mm = pe.matmul(out[:, j * 512 + at:j * 512 + at + T - kb * P],
                                           kT[:, h // 2, kb * P:(kb + 1) * P], qT[:, h, kb * P:T],
                                           start=(b == 0), stop=True, skip_group_check=(b > 0))
                    mm.then_inc(S.filled, 1)

                def outputs(i, u):
                    g, k = u // 3, u % 3
                    pe.wait_ge(S.masked, i * UNITS + u + 1 + START)
                    if k == 0:
                        pe.wait_ge(S.y_copied, i * GROUPS + g + START)
                    for kb, at in BLOCKS[k]:
                        for j in range(QH):
                            mm = pe.matmul(yT[32 * j:32 * j + 32, kb * P:T], va[:, kb, QH * g + j, :],
                                           U[k][:, j, at:at + T - kb * P], start=(kb == 0), stop=True,
                                           skip_group_check=(kb > 0))
                    mm.then_inc(S.y_psum, 1)

                def turn_outputs(i, g):
                    pe.wait_ge(S.y_copied, i * GROUPS + g + 1 + START)
                    for t in range(TJ):
                        mm = pe.transpose(aux[:, t * P:(t + 1) * P], y_heads[:, t * P:(t + 1) * P], w.ident[:])
                    mm.then_inc(S.y_turned, 1)

                def project(i, turns):
                    out = claim(i, turns, ("o", 0))
                    pe.wait_ge(S.y_ready, i * GROUPS + GROUPS + START)
                    turn(out)
                    out = claim(i, turns, ("p", 0))
                    pe.wait_ge(*turns.read(i, ("o", 0)))
                    for j in range(TJ):
                        for k in range(KC):
                            mm = pe.matmul(out[:, j * C:(j + 1) * C], hT[:, k, j * P:(j + 1) * P], w.wo[:, k, :],
                                           start=(k == 0), stop=(k == KC - 1))
                    mm.then_inc(S.filled, 1)

                def a_batch(i, turns, last):
                    for n in range(3):
                        scores(i, turns, n)
                    for u in range(UNITS):
                        for n in (2 * u + 3, 2 * u + 4):
                            if n < 2 * UNITS:
                                scores(i, turns, n)
                        if u >= UNITS - 2 and not last:
                            for n in ((0,), (1, 2))[u - UNITS + 2]:
                                turn_parts(i, turns, i + 1, n)
                        outputs(i, u)
                        if u == 0 and not last:
                            turn_x(i, turns, i + 1)
                        if u % 3 == 0 and u > 0:
                            if not last:
                                pe.wait_ge(S.qk_ready, i * TJ + TJ + (1, TJ, TJ)[u // 3 - 1] + START)
                            pe.wait_ge(S.y_ready, i * GROUPS + u // 3 - 1 + START)
                            turn_outputs(i, u // 3 - 1)
                        if 2 <= u < 2 + TJ and not last:
                            if u == 2:
                                pe.wait_ge(*turns.read(i, ("x", 0)))
                            pe.wait_ge(S.qk_ready, i * TJ + TJ + u - 2 + START)
                            pe.wait_ge(S.y_ready, i * GROUPS + (0 if u == 2 else 1) + START)
                            queries_keys(i + 1, u - 2)
                    for n in range(0 if last else 3, 0 if last else 2 * TJ):
                        turn_parts(i, turns, i + 1, n)
                        if n == 2 * TJ - 2:
                            pe.wait_ge(S.y_ready, i * GROUPS + GROUPS - 1 + START)
                            turn_outputs(i, GROUPS - 1)
                    if last:
                        pe.wait_ge(S.y_ready, i * GROUPS + GROUPS - 1 + START)
                        turn_outputs(i, GROUPS - 1)
                    else:
                        values(i, turns)
                    project(i, turns)

                ACT_READS, DVE_READS = (len([n for n in each if readers[n[0]] in (engine, "both")])
                                        for engine in ("act", "dve"))
                turn_x(0, start, 0)
                pe.wait_ge(*start.read(0, ("x", 0)))
                pe.wait_ge(centred, 2)
                for t in range(TJ):
                    if t >= 1:
                        pe.wait_ge(S.qk_ready, t + START)
                    queries_keys(0, t)
                for n in range(2 * TJ):
                    turn_parts(0, start, 0, n)
                values(0, start)
                pe.wait_ge(zeros_there, 4)
                with pe.Fori(0, B - 1) as i:
                    a_batch(i, steady, last=False)
                a_batch(B - 1, final, last=True)

            @block.scalar
            def _(act):
                def to_hT(i, turns, name):
                    act.wait_ge(*turns.filled(i, name))
                    act.activation(hT[:].rearrange("p k t -> p (k t)"), wide(turns, name)[:], ACT.Copy
                                   ).then_inc(S.act_read, 1)

                def take_qk(r, t):
                    act.wait_ge(S.qk_psum, r * TJ + t + 1 + START)
                    act.wait_ge(S.var_ready, r * TJ + max(t - 1, 0) + START)
                    act.activation(squares[:, t % 2].rearrange("p g f -> p (g f)"), aux[:], ACT.Square, scale=0.25
                                   ).then_inc(S.squared, 1)
                    act.activation(qk[:, t].rearrange("p g f -> p (g f)"), aux[:], ACT.Copy).then_inc(S.qk_ready, 1)

                def upper_part(i, turns, r, n):
                    t, m = n // 2, n % 2
                    act.wait_ge(S.feat_ready, r * TJ + t + 1 + START)
                    if n >= 4:
                        act.wait_ge(*turns.filled(i, turned[n - 4]))
                    part = parts[m][:, t % 2].bitcast(F32R)
                    hi = part[:, :, 0:4:2, :] if m else part[:, :, 0:2, :]
                    heads = qk[:, t, m * HEADS:(m + 1) * HEADS, :]
                    act.activation(hi, spread(heads, 2, 2), ACT.Copy).then_inc(S.hi_ready, 1)

                def turned_qk(i, turns, t):
                    act.wait_ge(*turns.filled(i, ("tq", t)))
                    act.activation(qT[0:64, 0:HEADS:2, t * P:(t + 1) * P],
                                   wide(turns, ("tq", t))[0:64, :].rearrange("p (g c) -> p g c", c=P), ACT.Copy
                                   ).then_inc(S.act_read, 1)
                    act.wait_ge(*turns.filled(i, ("tk", t)))
                    act.activation(kT[:, :, t * P:(t + 1) * P],
                                   wide(turns, ("tk", t))[:].rearrange("p (g c) -> p g c", c=P), ACT.Copy
                                   ).then_inc(S.act_read, 1)

                def head_root(r, p):
                    act.wait_ge(S.var_ready, r * TJ + 2 * p + 2 + START)
                    two_tiles = slice(p * 2 * NG, (p + 1) * 2 * NG)
                    act.activation(rms[:, two_tiles], var[:, two_tiles], ACT.Sqrt, bias=w.eps[:, 0:1]
                                   ).then_inc(S.head_dev, 1)

                def later_parts(i, turns, r):
                    for t in range(TJ):
                        if t >= 2:
                            upper_part(i, turns, r, 2 * t)
                            upper_part(i, turns, r, 2 * t + 1)
                        if t >= 1:
                            turned_qk(i, turns, t - 1)
                    turned_qk(i, turns, TJ - 1)

                def a_batch(i, turns, last):
                    for u in range(UNITS):
                        g, k = u // 3, u % 3
                        if u >= 3:
                            act.wait_ge(S.y_psum, i * UNITS + u - 2 + START)
                        for q in range(2):
                            act.wait_ge(*turns.filled(i, ("s", 2 * u + q)))
                            act.activation(U[k][:, 2 * q:2 * q + 2, :], wide(turns, ("s", 2 * u + q))[:].rearrange(
                                "p (h c) -> p h c", c=512)[:, :, 0:WIDTH[k]], ACT.Square, scale=0.25
                                ).then_inc(S.act_read, 1)
                            if u == 2 and q == 0 and not last:
                                to_hT(i, turns, ("x", 0))
                            if u in (5, 7) and q == 0 and not last:
                                head_root(i + 1, (u - 5) // 2)
                        if 3 <= u < 3 + TJ and not last:
                            take_qk(i + 1, u - 3)
                        if u in (8, 9) and not last:
                            upper_part(i, turns, i + 1, 2 * (u - 8))
                            upper_part(i, turns, i + 1, 2 * (u - 8) + 1)
                    if not last:
                        later_parts(i, turns, i + 1)
                    to_hT(i, turns, ("o", 0))

                def zeros(half):
                    others = slice(64 * half, 64 * half + 64)
                    for h in range(1 - half, HEADS, 8):
                        act.activation(qT[others, h:h + 7:2, :], U[0][others], ACT.Copy).then_inc(zeros_there, 1)

                act.wait_ge(consts, 1)
                zeros(0)
                to_hT(0, start, ("x", 0))
                zeros(1)
                for t in range(TJ):
                    take_qk(0, t)
                head_root(0, 0)
                head_root(0, 1)
                for n in range(4):
                    upper_part(0, start, 0, n)
                later_parts(0, start, 0)
                with act.Fori(0, B - 1) as i:
                    a_batch(i, steady, last=False)
                a_batch(B - 1, final, last=True)


def program(nc, io, phases=("a", "f1", "b", "f2")):
    with ExitStack() as ctx:
        def sb(name, shape, dt=F32):
            return ctx.enter_context(nc.sbuf_tensor(name, shape, dt))

        def sem(name):
            return ctx.enter_context(nc.semaphore(name))

        w = Named()
        w.x = sb("x", [P, B * TJ, C])
        w.ident, w.identb, w.tri = sb("ident", [P, P]), sb("identb", [P, P], BF16), sb("tri", [P, P])
        w.ones3, w.ones3b = sb("ones3", [ROWS, P], BF16), sb("ones3b", [ROWS, T], BF16)
        w.minus_half, w.eps = sb("minus_half", [P, 32]), sb("eps", [P, 32])
        w.iota_lo, w.rank_weight = sb("iota_lo", [P, NKEYS, KPH], BF16), sb("rank_weight", [P, NKEYS, KPH], BF16)
        w.sel, w.selb = sb("sel", [ROWS, FC, 2, NKEYS], F32R), sb("selb", [ROWS, FC, 2, NKEYS], BF16)
        w.selovf = sb("selovf", [ROWS, P], F32R)
        w.bias3 = sb("bias3", [ROWS, NBIAS], BF16)
        w.wd, w.ue = sb("wd", [P, FC, C]), sb("ue", [P, FC, C])
        w.deT, w.wsim = sb("deT", [P, 2, KC, NEXP], F32R), sb("wsim", [P, 2, KC, 2 * H * NKEYS], F32R)
        w.bg, w.bu = sb("bg", [P, FC]), sb("bu", [P, FC])
        w.wqk, w.wvb, w.wo = sb("wqk", [P, KC, 2 * C]), sb("wvb", [P, KC, C]), sb("wo", [P, KC, C])
        w.gamma, w.beta = sb("gamma", [P, FEAT]), sb("beta", [P, FEAT])

        w.scan_signals, w.attn_signals = ScanSignals(sem, "a"), AttnSignals(sem, "b")
        w.ffn_signals = {"f1": FfnSignals(sem, "f1"), "f2": FfnSignals(sem, "f2")}
        w.all_signals = (w.scan_signals.all + w.attn_signals.all + w.ffn_signals["f1"].all
                         + w.ffn_signals["f2"].all)
        w.x_loaded = [sem(f"x_loaded{b}") for b in range(B)]
        with ExitStack() as scan_ctx:
            def scan_sb(name, shape):
                return scan_ctx.enter_context(nc.sbuf_tensor(name, shape, F32))

            w.wv, w.gq, w.wproj = scan_sb("wv", [P, KC, C]), scan_sb("gq", [P, KC, P]), scan_sb("wproj", [P, KC, C])
            w.wz, w.gz = scan_sb("wz", [P, C]), scan_sb("gz", [P, P])
            setup(nc, w, io, sem)
            scan_attention(nc, w, sem)
        if "f1" in phases:
            experts_ffn(nc, w, io, sem, "f1")
        if "b" in phases:
            linear_attention(nc, w, sem)
        if "f2" in phases:
            experts_ffn(nc, w, io, sem, "f2")
        out_stored = sem("out_stored")
        with nc.Block() as block:
            @block.sync
            def _(sp):
                for b in range(B):
                    sp.dma_start(io.out[b].rearrange("(j p) c -> p j c", p=P),
                                 w.x[:, b * TJ:(b + 1) * TJ, :]).then_inc(out_stored, 16)
                sp.wait_ge(out_stored, 16 * B)


def arguments(args, out):
    io = Named()
    (io.x, io.attn_W, io.attn_b, io.freq_W, io.freq_b, io.out_W, io.out_b, io.proj_W, io.proj_b,
     io.identity, io.b_Wq, io.b_Wk, io.b_Wv, io.b_Wo, io.gamma, io.beta, io.Wg, io.bg, io.Wu, io.bu,
     io.Wd, io.bd, io.ffn_Wq, io.keys, io.down_embed, io.up_embed) = args
    io.out = out
    return io


_INPUTS = (
    "L0_attn_a_x",
    "L0_attn_a_attn_W",
    "L0_attn_a_attn_b",
    "L0_attn_a_freq_W",
    "L0_attn_a_freq_b",
    "L0_attn_a_out_W",
    "L0_attn_a_out_b",
    "L0_attn_a_proj_W",
    "L0_attn_a_proj_b",
    "L0_attn_a_identity",
    "L0_attn_b_Wq",
    "L0_attn_b_Wk",
    "L0_attn_b_Wv",
    "L0_attn_b_Wo",
    "L0_attn_b_gamma",
    "L0_attn_b_beta",
    "L0_ffn_Wg",
    "L0_ffn_bg",
    "L0_ffn_Wu",
    "L0_ffn_bu",
    "L0_ffn_Wd",
    "L0_ffn_bd",
    "L0_ffn_Wq",
    "L0_ffn_keys",
    "L0_ffn_down_embed",
    "L0_ffn_up_embed",
)


def kernel(**inputs):
    import numpy as _np
    import concourse.bacc as _bacc
    from concourse.bass_utils import run_bass_kernel_spmd as _run

    nc = _bacc.Bacc("TRN2", target_bir_lowering=False, num_devices=1)
    args, arrays = [], {}
    for name in _INPUTS:
        a = _np.ascontiguousarray(inputs[name])
        arrays[f"in_{name}"] = a
        args.append(nc.dram_tensor(f"in_{name}", a.shape, mybir.dt.from_np(a.dtype), kind="ExternalInput").ap())
    out = nc.dram_tensor("out_x", (B, T, C), F32, kind="ExternalOutput").ap()
    program(nc, arguments(args, out))
    return _run(nc, [arrays], core_ids=[0]).results[0]["out_x"]
```
